# Optimizing a Trainium2 kernel written in Bass

```python
import numpy as np
import jax
import jax.numpy as jnp

def _softmax(x, axis=-1):
    return jax.nn.softmax(x, axis=axis)

def _gelu(x):
    return jax.nn.gelu(x, approximate=True)

def _silu(x):
    return jax.nn.silu(x)

def _sigmoid(x):
    return jax.nn.sigmoid(x)

def _layernorm(x, axis=-1, eps=1e-05):
    m = jnp.mean(x, axis=axis, keepdims=True)
    v = jnp.var(x, axis=axis, keepdims=True)
    return (x - m) / jnp.sqrt(v + eps)

def _scatter_add(tgt, idx, src, axis=0):
    return tgt.at[idx].add(src)

def _segment_sum(src, seg, n):
    return jax.ops.segment_sum(src, seg, n)
kernel_name = 'mk_decoder_postln_d1_seqx_r4_542f23'

def setup_inputs(seed: int=0):
    np.random.seed(seed)
    _w = jnp.asarray

    def _rec_inputs():
        import jax
        import jax.numpy as jnp
        _rk = jax.random.key(seed)
        x = 7.22e-05 + 1 * jax.random.normal(jax.random.fold_in(_rk, 1), (8, 512, 256), jnp.float32)
        _lenS = 512 - jax.random.randint(jax.random.fold_in(_rk, 7), (8,), 0, max(1, 512 // 4) + 1, jnp.int32)
        _lenS2 = 512 - jax.random.randint(jax.random.fold_in(_rk, 8), (8,), 0, max(1, 512 // 4) + 1, jnp.int32)
        _ctx_1024P = jax.random.normal(jax.random.fold_in(_rk, 11), (8, 16, 256), jnp.float32)
        _ctx_1024c = jax.random.dirichlet(jax.random.fold_in(_rk, 511), 0.3 * jnp.ones((16,), jnp.float32), (8, 512))
        _ctx_1024t = jnp.einsum('bsk,bkd->bsd', _ctx_1024c, _ctx_1024P)
        _ctx_1024t = _ctx_1024t * jax.lax.rsqrt(jnp.mean(jnp.square(_ctx_1024t)) + 1e-12) * 0.953939
        ctx_1024 = 4.13588e-05 + 0.999923 * (_ctx_1024t + 0.3 * jax.random.normal(jax.random.fold_in(_rk, 611), (8, 512, 256), jnp.float32))
        return (x, ctx_1024)
    x, ctx_1024 = _rec_inputs()

    def _L0_attn_setup():
        import jax, jax.numpy as jnp
        import numpy as np
        EMBED_DIM = 256
        NUM_HEADS = 16
        HEAD_DIM = EMBED_DIM // NUM_HEADS
        ROPE_BASE = 10000.0

        def rotate_half(x):
            x1 = x[..., ::2]
            x2 = x[..., 1::2]
            return jnp.stack((-x2, x1), axis=-1).reshape(x.shape)

        def rope_tables(T, dim, dtype):
            inv_freq = 1.0 / ROPE_BASE ** (jnp.arange(0, dim, 2, dtype=jnp.float32) / dim)
            t = jnp.arange(T, dtype=jnp.float32)
            freqs = t[:, None] * inv_freq[None, :]
            emb = jnp.concatenate((freqs, freqs), axis=-1)
            return (jnp.cos(emb).astype(dtype), jnp.sin(emb).astype(dtype))
        key = jax.random.key(seed)
        kx, kq, ko = jax.random.split(key, 3)
        B, T, D = (2, 512, EMBED_DIM)
        x = jax.random.normal(kx, (B, T, D), dtype=jnp.float32)
        s = 1.0 / np.sqrt(D)
        Wqkv = jax.random.normal(kq, (D, 3 * D), dtype=jnp.float32) * s
        Wout = jax.random.normal(ko, (D, D), dtype=jnp.float32) * s
        return {'x': x, 'Wqkv': Wqkv, 'Wout': Wout}
    _L0_attn_all = _L0_attn_setup()
    _L0_attn_in = {k: v for k, v in _L0_attn_all.items() if k in ('Wqkv', 'Wout')}
    del _L0_attn_all

    def _L0_xattn_setup():
        import jax, jax.numpy as jnp
        import numpy as np
        from math import sqrt
        D_MODEL = 256
        N_HEAD = 16
        D_HEAD = D_MODEL // N_HEAD

        def _split_heads(x):
            B, L, D = x.shape
            return x.reshape(B, L, N_HEAD, D_HEAD).transpose(0, 2, 1, 3)
        key = jax.random.key(seed)
        ks = jax.random.split(key, 11)
        B, L = (4, 512)
        s = 1.0 / sqrt(D_MODEL)
        inp = {'q': jax.random.normal(ks[0], (B, L, D_MODEL), jnp.float32), 'k': jax.random.normal(ks[1], (B, L, D_MODEL), jnp.float32), 'v': jax.random.normal(ks[2], (B, L, D_MODEL), jnp.float32), 'w_q': jax.random.normal(ks[3], (D_MODEL, D_MODEL), jnp.float32) * s, 'b_q': jax.random.normal(ks[4], (D_MODEL,), jnp.float32) * s, 'w_k': jax.random.normal(ks[5], (D_MODEL, D_MODEL), jnp.float32) * s, 'b_k': jax.random.normal(ks[6], (D_MODEL,), jnp.float32) * s, 'w_v': jax.random.normal(ks[7], (D_MODEL, D_MODEL), jnp.float32) * s, 'b_v': jax.random.normal(ks[8], (D_MODEL,), jnp.float32) * s, 'w_o': jax.random.normal(ks[9], (D_MODEL, D_MODEL), jnp.float32) * s, 'b_o': jax.random.normal(ks[10], (D_MODEL,), jnp.float32) * s}
        return inp
    _L0_xattn_all = _L0_xattn_setup()
    _L0_xattn_in = {k: v for k, v in _L0_xattn_all.items() if k in ('w_q', 'b_q', 'w_k', 'b_k', 'w_v', 'b_v', 'w_o', 'b_o')}
    del _L0_xattn_all

    def _L0_ffn_setup():
        import math
        import jax, jax.numpy as jnp
        import numpy as np
        B, S, H = (4, 512, 256)
        E, K, I = (8, 2, 256)
        NSH = 2
        CF, RSF = (1.25, 1.0)
        key = jax.random.key(seed)
        ks = jax.random.split(key, 8)
        w = lambda k, sh: jax.random.normal(k, sh, dtype=jnp.float32) * 0.02
        return {'hidden_states': jax.random.normal(ks[0], (B, S, H), dtype=jnp.float32), 'gate_w': w(ks[1], (E, H)), 'we_gate': w(ks[2], (E, I, H)), 'we_up': w(ks[3], (E, I, H)), 'we_down': w(ks[4], (E, H, I)), 'ws_gate': w(ks[5], (NSH * I, H)), 'ws_up': w(ks[6], (NSH * I, H)), 'ws_down': w(ks[7], (H, NSH * I))}
    _L0_ffn_all = _L0_ffn_setup()
    _L0_ffn_in = {k: v for k, v in _L0_ffn_all.items() if k in ('gate_w', 'we_gate', 'we_up', 'we_down', 'ws_gate', 'ws_up', 'ws_down')}
    del _L0_ffn_all
    return {'x': x, 'ctx_1024': ctx_1024, 'L0_attn_Wqkv': _L0_attn_in['Wqkv'], 'L0_attn_Wout': _L0_attn_in['Wout'], 'L0_xattn_w_q': _L0_xattn_in['w_q'], 'L0_xattn_b_q': _L0_xattn_in['b_q'], 'L0_xattn_w_k': _L0_xattn_in['w_k'], 'L0_xattn_b_k': _L0_xattn_in['b_k'], 'L0_xattn_w_v': _L0_xattn_in['w_v'], 'L0_xattn_b_v': _L0_xattn_in['b_v'], 'L0_xattn_w_o': _L0_xattn_in['w_o'], 'L0_xattn_b_o': _L0_xattn_in['b_o'], 'L0_ffn_gate_w': _L0_ffn_in['gate_w'], 'L0_ffn_we_gate': _L0_ffn_in['we_gate'], 'L0_ffn_we_up': _L0_ffn_in['we_up'], 'L0_ffn_we_down': _L0_ffn_in['we_down'], 'L0_ffn_ws_gate': _L0_ffn_in['ws_gate'], 'L0_ffn_ws_up': _L0_ffn_in['ws_up'], 'L0_ffn_ws_down': _L0_ffn_in['ws_down']}

def reference(x, ctx_1024, L0_attn_Wqkv, L0_attn_Wout, L0_xattn_w_q, L0_xattn_b_q, L0_xattn_w_k, L0_xattn_b_k, L0_xattn_w_v, L0_xattn_b_v, L0_xattn_w_o, L0_xattn_b_o, L0_ffn_gate_w, L0_ffn_we_gate, L0_ffn_we_up, L0_ffn_we_down, L0_ffn_ws_gate, L0_ffn_ws_up, L0_ffn_ws_down):
    import jax
    import jax.numpy as jnp

    def _L0_attn_ref(x, Wqkv, Wout):
        import jax, jax.numpy as jnp
        import numpy as np
        EMBED_DIM = 256
        NUM_HEADS = 16
        HEAD_DIM = EMBED_DIM // NUM_HEADS
        ROPE_BASE = 10000.0

        def rotate_half(x):
            x1 = x[..., ::2]
            x2 = x[..., 1::2]
            return jnp.stack((-x2, x1), axis=-1).reshape(x.shape)

        def rope_tables(T, dim, dtype):
            inv_freq = 1.0 / ROPE_BASE ** (jnp.arange(0, dim, 2, dtype=jnp.float32) / dim)
            t = jnp.arange(T, dtype=jnp.float32)
            freqs = t[:, None] * inv_freq[None, :]
            emb = jnp.concatenate((freqs, freqs), axis=-1)
            return (jnp.cos(emb).astype(dtype), jnp.sin(emb).astype(dtype))
        B, T, D = x.shape
        H, hd = (NUM_HEADS, HEAD_DIM)
        qkv = x @ Wqkv
        q, k, v = jnp.split(qkv, 3, axis=-1)
        q = q.reshape(B, T, H, hd).transpose(0, 2, 1, 3)
        k = k.reshape(B, T, H, hd).transpose(0, 2, 1, 3)
        v = v.reshape(B, T, H, hd).transpose(0, 2, 1, 3)
        cos, sin = rope_tables(T, hd, x.dtype)
        cos = cos[None, None, :, :]
        sin = sin[None, None, :, :]
        q = q * cos + rotate_half(q) * sin
        k = k * cos + rotate_half(k) * sin
        scale = 1.0 / np.sqrt(hd).astype(np.float32)
        attn = jnp.einsum('bhtd,bhsd->bhts', q, k) * scale
        attn = jax.nn.softmax(attn, axis=-1)
        out = jnp.einsum('bhts,bhsd->bhtd', attn, v)
        out = out.transpose(0, 2, 1, 3).reshape(B, T, D)
        return out @ Wout

    def _L0_xattn_ref(q, k, v, w_q, b_q, w_k, b_k, w_v, b_v, w_o, b_o):
        import jax, jax.numpy as jnp
        import numpy as np
        from math import sqrt
        D_MODEL = 256
        N_HEAD = 16
        D_HEAD = D_MODEL // N_HEAD

        def _split_heads(x):
            B, L, D = x.shape
            return x.reshape(B, L, N_HEAD, D_HEAD).transpose(0, 2, 1, 3)
        qh = _split_heads(q @ w_q.T + b_q)
        kh = _split_heads(k @ w_k.T + b_k)
        vh = _split_heads(v @ w_v.T + b_v)
        scale = 1.0 / sqrt(D_HEAD)
        score = jnp.einsum('bhqd,bhkd->bhqk', qh, kh) * scale
        attn = jax.nn.softmax(score, axis=-1)
        out = jnp.einsum('bhqk,bhkd->bhqd', attn, vh)
        B, H, L, Dh = out.shape
        out = out.transpose(0, 2, 1, 3).reshape(B, L, D_MODEL)
        return out @ w_o.T + b_o

    def _L0_ffn_ref(hidden_states, gate_w, we_gate, we_up, we_down, ws_gate, ws_up, ws_down):
        import math
        import jax, jax.numpy as jnp
        import numpy as np
        B, S, H = (4, 512, 256)
        E, K, I = (8, 2, 256)
        NSH = 2
        CF, RSF = (1.25, 1.0)
        orig_shape = hidden_states.shape
        x = hidden_states.reshape(-1, H)
        N = x.shape[0]
        logits = x.astype(jnp.float32) @ gate_w.astype(jnp.float32).T
        scores = jax.nn.softmax(logits, axis=-1)
        topk_w, topk_idx = jax.lax.top_k(scores, K)
        topk_w = topk_w / (topk_w.sum(-1, keepdims=True) + 1e-20) * RSF
        capacity = math.ceil(CF * N * K / E)
        flat = topk_idx.reshape(-1)
        one_hot = jax.nn.one_hot(flat, E, dtype=jnp.int32)
        pos = jnp.cumsum(one_hot, axis=0) - 1
        pos_tok = jnp.take_along_axis(pos, flat[:, None], axis=1)[:, 0]
        keep = (pos_tok < capacity).reshape(N, K)
        topk_w = topk_w * keep.astype(topk_w.dtype)
        comb = jnp.zeros((N, E), jnp.float32).at[jnp.arange(N)[:, None], topk_idx].add(topk_w)
        g = jnp.einsum('nh,eih->nei', x, we_gate)
        u = jnp.einsum('nh,eih->nei', x, we_up)
        eo = jnp.einsum('nei,ehi->neh', jax.nn.silu(g) * u, we_down)
        y = jnp.einsum('neh,ne->nh', eo, comb)
        sh = jax.nn.silu(x @ ws_gate.T) * (x @ ws_up.T) @ ws_down.T
        return (y + sh).reshape(orig_shape)
    x = _layernorm(x + _L0_attn_ref(x, L0_attn_Wqkv, L0_attn_Wout), axis=-1)
    x = _layernorm(x + _L0_xattn_ref(x, ctx_1024, ctx_1024, L0_xattn_w_q, L0_xattn_b_q, L0_xattn_w_k, L0_xattn_b_k, L0_xattn_w_v, L0_xattn_b_v, L0_xattn_w_o, L0_xattn_b_o), axis=-1)
    x = _layernorm(x + _L0_ffn_ref(x, L0_ffn_gate_w, L0_ffn_we_gate, L0_ffn_we_up, L0_ffn_we_down, L0_ffn_ws_gate, L0_ffn_ws_up, L0_ffn_ws_down), axis=-1)
    return x

_drawn_inputs = setup_inputs


def setup_inputs(seed=0):
    import zlib

    import numpy as np

    out = dict(_drawn_inputs(seed))
    spreads = {}
    factors = {'L0_xattn_b_q': 4.585,
     'L0_xattn_b_k': 64.0,
     'L0_ffn_gate_w': 5.483,
     'L0_ffn_we_gate': 4.774,
     'L0_ffn_we_up': 4.721,
     'L0_ffn_we_down': 4.714,
     'L0_ffn_ws_gate': 4.644,
     'L0_ffn_ws_up': 4.579,
     'L0_ffn_ws_down': 4.582}
    for name, (base, spread) in spreads.items():
        noise = np.random.default_rng([zlib.crc32(name.encode()), seed]).standard_normal(out[name].shape)
        drawn = base * np.exp(spread * noise) if base else spread * noise
        out[name] = jnp.asarray(drawn.astype(out[name].dtype))
    for name, factor in factors.items():
        out[name] = (out[name] * factor).astype(out[name].dtype)
    return out
```

```python
import concourse.bass as bass
from concourse import mybir
from contextlib import ExitStack

import numpy as np

F32 = mybir.dt.float32
F32R = mybir.dt.float32r
ALU = mybir.AluOpType
ACT = mybir.ActivationFunctionType
AX = mybir.AxisListType

P = 128
B, T, D = 8, 512, 256
H, HD = 16, 16
TT = T // P
FC = D // P
HG = 4
NG = H // HG
HM = H // FC
LEAD = 6
STEPS = NG * TT
NMAX = H * TT
EPS = 1e-5
HI, LO = 0, 1
SLOTS = 4

JOBS = ([("q", 0), ("k", 0), ("v", 0), ("v", 1), ("q", 1), ("k", 1), ("ck", 0), ("ck", 1), ("cv", 0), ("cv", 1)]
        + [("ot0", t) for t in range(TT)] + [("nt0", f) for f in range(FC)] + [("w0", 0), ("w0", 1)]
        + [("xt", f) for f in range(FC)] + [("cq", m) for m in range(FC)]
        + [("ot1", t) for t in range(TT)] + [("nt1", f) for f in range(FC)] + [("w1", 0), ("w1", 1)])
READ_BY_ACT = ("v", "cv")
NJ = len(JOBS)
J = {job: n for n, job in enumerate(JOBS)}
ACT_JOBS = [job for job in JOBS if job[0] in READ_BY_ACT]
ROPE_JOBS = [job for job in JOBS if job[0] in ("q", "k")]
SPLIT_JOBS = [job for job in JOBS if job[0] in ("q", "k", "ck", "nt0", "nt1", "xt", "cq")]
SPLITS = [("x", 0), ("c", 0)] + SPLIT_JOBS
NS = len(SPLITS)
NA = len(ACT_JOBS)

WCOL = {n: i * D for i, n in enumerate(("q", "k", "v", "w0", "cq", "ck", "cv", "w1"))}
NW = len(WCOL) * D


def wait_alone(eng, s, value, met, least):
    value = eng.snap(eng.to_reg(value))
    eng.wait_ge(met, least)
    eng.wait_ge(s, value)


def attention_phase(nc, x, xT, cT, w_att, tables, b_cols, bo_rows, x2, hbm_self, hbm_ck, hbm_cq):
    with ExitStack() as ctx:
        def sb(name, shape, dt=F32):
            return ctx.enter_context(nc.sbuf_tensor(name, shape, dt))

        def sem(name):
            return ctx.enter_context(nc.semaphore(name))

        w = sb("w", [P, 2, FC, NW], F32R)
        ident = sb("ident", [P, P])
        trig = sb("trig", [P, 2, T])
        bcol = sb("bcol", [P, 3, FC])
        bo = sb("bo", [P, D])
        xin = sb("xin", [P, TT, D])
        xraw = sb("xraw", [P, 2, FC, T])
        xf = sb("xf", [P, 2, FC, T], F32R)
        cf = sb("cf", [P, 2, FC, T], F32R)
        nf = cf
        ot = sb("ot", [P, NG, T])
        rot, cosq = ot[:, 0:2, :], ot[:, 2:4, :]
        stage = sb("stage", [P, FC, SLOTS, T], F32R)
        stage_ck = sb("stage_ck", [P, FC, 2, T], F32R)
        qk = sb("qk", [P, 2, H, T], F32R)
        va = sb("va", [P, 2, TT, H, 2 * HD])
        prob = sb("prob", [P, 2, HG, T])
        rows = prob[:, :, :, :].rearrange("p a (u h) t -> p (a u) (h t)", u=2)
        on = rows[:, 0, :].rearrange("p (t n) -> p t n", t=TT)
        res = rows[:, 1, :].rearrange("p (t n) -> p t n", t=TT)
        x2s = rows[:, 2, :].rearrange("p (t n) -> p t n", t=TT)
        nm = sb("nm", [P, 2, HG * TT])
        mst = sb("mst", [HG * TT, 2, 2, P], F32R)
        rden = sb("rden", [P, TT, H])
        x1 = sb("x1", [P, TT, D])
        x1b = xin
        st6 = sb("st6", [P, TT, 6])
        mv = sb("mv", [P, TT, 2])
        rstd = sb("rstd", [P, TT, 1])
        mhalf = sb("mhalf", [P, TT, 1])
        eps = sb("eps", [P, TT, 1])

        ring = ctx.enter_context(nc.psum_tensor("ring", [P, HG, T], F32))
        ps_max = ctx.enter_context(nc.psum_tensor("ps_max", [P, 2, T], F32))
        ps_out = ctx.enter_context(nc.psum_tensor("ps_out", [P, T], F32))
        ps_m = ctx.enter_context(nc.psum_tensor("ps_m", [P, T], F32))

        raw_w, w_hi, w_ready, consts, zeroed = sem("raw_w"), sem("w_hi"), sem("w_ready"), sem("consts"), sem("zeroed")
        consts_dma = sem("consts_dma")
        x_in, xt_in, ct_in = sem("x_in"), sem("xt_in"), sem("ct_in")
        job_done = sem("job_done")
        read_act = sem("read_act")
        hi_done, lo_done = sem("hi_done"), sem("lo_done")
        rotated, cos_done = sem("rotated"), sem("cos_done")
        sin_done, roped = sem("sin_done"), sem("roped")
        self_out = [sem(f"self_out{m}") for m in range(FC)]
        self_in = [sem(f"self_in{m}") for m in range(FC)]
        ck_out, ck_in = sem("ck_out"), sem("ck_in")
        cq_out = [sem(f"cq_out{m}") for m in range(FC)]
        cq_in = [sem(f"cq_in{m}") for m in range(FC)]
        smax_done, max_done = sem("smax_done"), sem("max_done")
        nmt_done, mhi_done, mlo_done = sem("nmt_done"), sem("mhi_done"), sem("mlo_done")
        mrow_in = [sem("mrow_in0"), sem("mrow_in1")]
        st_done, exp_done, pv_done, oev_done = sem("st_done"), sem("exp_done"), sem("pv_done"), sem("oev_done")
        rden_done, on_done = sem("rden_done"), sem("on_done")
        res_done, stat_done, mv_done = sem("res_done"), sem("stat_done"), sem("mv_done")
        var_done, rstd_done = sem("var_done"), sem("rstd_done")
        x1_done, x1b_done, x2_done, x2_out = sem("x1_done"), sem("x1b_done"), sem("x2_done"), sem("x2_out")

        block = ctx.enter_context(nc.Block())

        def split_at(i, job):
            return i * NS + SPLITS.index(job) + 1

        def last_read(job):
            kind, k = job
            if job in ACT_JOBS:
                return read_act, NA, ACT_JOBS.index(job) + 1
            if kind in ("q", "k"):
                return rotated, 4, ROPE_JOBS.index(job) + 1
            if job in SPLITS:
                return lo_done, NS, SPLITS.index(job) + 1
            layer = int(kind[-1])
            if kind[:2] == "ot":
                return on_done, 2 * TT, TT * layer + k + 1
            return res_done, 4, 2 * layer + k + 1

        def read_before(eng, i, n):
            if n >= HG:
                s, total, count = last_read(JOBS[n - HG])
                eng.wait_ge(s, i * total + count)
            else:
                s, total, _ = last_read(JOBS[max(m for m in range(NJ) if m % HG == n)])
                eng.wait_ge(s, i * total)

        @block.sync
        def _(sp):
            sp.dma_start(prob[:, :, :, :].rearrange("p a h t -> p (a h t)"),
                         w_att[:, :, :].rearrange("p f n -> p (f n)")).then_inc(raw_w, 16)
            sp.dma_start(trig[:, :, :], tables).then_inc(consts_dma, 16)
            sp.dma_start(bcol[:, :, :], b_cols).then_inc(consts_dma, 16)
            sp.dma_start(bo[:, :], bo_rows).then_inc(consts_dma, 16)

            def load(i, at):
                wait_alone(sp, lo_done, at * NS, consts_dma, 48)
                sp.dma_start(xraw[:, 0, :, :], xT[i, :, :, :]).then_inc(xt_in, 16)
                sp.dma_start(xraw[:, 1, :, :], cT[i, :, :, :]).then_inc(ct_in, 16)
                wait_alone(sp, res_done, at * 4, consts_dma, 48)
                sp.dma_start(xin[:, :, :], x[i, :, :, :]).then_inc(x_in, 16)

            def mrows(i, layer, g):
                n = layer * NG + g
                sp.wait_ge(mlo_done, i * 2 * NG + n + 1)
                for part in (HI, LO):
                    row = 96 + part
                    sp.dma_start(
                        qk[row:row + 1, 0, HG * g:HG * g + HG, :].rearrange("o h (c q) -> o (h c) q", q=P).bitcast(F32),
                        mst[:, g % 2, part, :].bitcast(F32)).then_inc(mrow_in[g % 2], 16)

            with sp.Fori(0, B) as i:
                load(i, i)
                for m in range(FC):
                    sp.wait_ge(lo_done, split_at(i, ("k", m)))
                    sp.dma_start(hbm_self[m], stage[:, m, :, :].bitcast(F32)).then_inc(self_out[m], 16)
                    stacks_free = sp.snap(sp.to_reg(i * 4 * STEPS)) if m == 0 else None
                    sp.wait_ge(self_out[m], i * 16 + 16)
                    if m == 0:
                        sp.wait_ge(st_done, stacks_free)
                    for r, (a, step) in enumerate(((0, 2), (0, 3), (1, 1))):
                        for s in range(2):
                            slot = a + s * step
                            sp.dma_start(qk[HD * r:HD * r + HD, s, HM * m:HM * m + HM, :].bitcast(F32),
                                         hbm_self[m, :, slot, :].rearrange("(h d) t -> d h t", d=HD)) \
                              .then_inc(self_in[m], 16)
                mrows(i, 0, 0)
                sp.wait_ge(lo_done, split_at(i, ("ck", 1)))
                sp.dma_start(hbm_ck, stage_ck[:, :, :, :].bitcast(F32)).then_inc(ck_out, 16)
                for g in range(1, NG):
                    mrows(i, 0, g)
                stacks_free = sp.snap(sp.to_reg(i * 4 * STEPS + 2 * STEPS))
                sp.wait_ge(ck_out, i * 16 + 16)
                sp.wait_ge(st_done, stacks_free)
                for r, part in enumerate((HI, LO, HI)):
                    for m in range(FC):
                        sp.dma_start(qk[HD * r:HD * r + HD, 1, HM * m:HM * m + HM, :].bitcast(F32),
                                     hbm_ck[:, m, part, :].rearrange("(h d) t -> d h t", d=HD)) \
                          .then_inc(ck_in, 16)
                for m in range(FC):
                    sp.wait_ge(lo_done, split_at(i, ("cq", m)))
                    sp.dma_start(hbm_cq[m], stage[:, m, 0:2, :].bitcast(F32)).then_inc(cq_out[m], 16)
                    sp.wait_ge(cq_out[m], i * 16 + 16)
                    for r, part in enumerate((HI, HI, LO)):
                        sp.dma_start(qk[HD * r:HD * r + HD, 0, HM * m:HM * m + HM, :].bitcast(F32),
                                     hbm_cq[m, :, part, :].rearrange("(h d) t -> d h t", d=HD)) \
                          .then_inc(cq_in[m], 16)
                for g in range(NG):
                    mrows(i, 1, g)
                wait_alone(sp, x2_done, i * TT + TT, consts_dma, 48)
                sp.dma_start(x2[i, :, :, :], x2s[:, :, :]).then_inc(x2_out, 16)
            sp.wait_ge(x2_out, B * 16)

        @block.gpsimd
        def _(pool):
            nc.gpsimd.memset(ident[:, :], 0.0).then_inc(consts, 1)
            pool.wait_ge(consts, 1)
            nc.gpsimd.affine_select(out=ident[:, :], in_=ident[:, :], compare_op=ALU.not_equal, fill=1.0,
                                    base=0, pattern=[[-1, P]], channel_multiplier=1).then_inc(consts, 1)
            nc.gpsimd.memset(mhalf[:, :, :], -0.5).then_inc(consts, 1)
            nc.gpsimd.memset(eps[:, :, :], EPS).then_inc(consts, 1)
            nc.gpsimd.memset(va[:, :, :, :, HD:2 * HD], 1.0).then_inc(consts, 1)
            nc.gpsimd.memset(qk[:, 1, :, :].bitcast(F32), 0.0).then_inc(consts, 1)
            pool.wait_ge(consts, 6)
            nc.gpsimd.memset(qk[96:P, 1, :, :].bitcast(F32), 1.0).then_inc(consts, 1)
            pool.wait_ge(consts_dma, 48)

            def norm(i, n, layer, pair):
                at = slice(2 * pair, 2 * pair + 2)
                pool.wait_ge(mv_done, i * 8 + n * 2 + 2)
                nc.gpsimd.tensor_tensor(rstd[:, at, :], mv[:, at, 1:2], eps[:, at, :], ALU.add).then_inc(var_done, 1)
                pool.wait_ge(var_done, i * 4 + n + 1)
                nc.gpsimd.tensor_tensor(rstd[:, at, :], rstd[:, at, :], mhalf[:, at, :], ALU.pow) \
                    .then_inc(rstd_done, 1)

            with pool.Fori(0, B) as i:
                for n, job in enumerate((("q", 0), ("k", 0), ("q", 1), ("k", 1))):
                    pool.wait_ge(rotated, i * 4 + n + 1)
                    nc.gpsimd.tensor_tensor(rot[:, n % 2, :], rot[:, n % 2, :], trig[:, 1, :], ALU.mult) \
                        .then_inc(sin_done, 1)
                    pool.wait_ge(sin_done, i * 4 + n + 1)
                    pool.wait_ge(cos_done, i * 4 + n + 1)
                    nc.gpsimd.tensor_tensor(cosq[:, n % 2, :], cosq[:, n % 2, :], rot[:, n % 2, :], ALU.add) \
                        .then_inc(roped, 1)
                norm(i, 0, 0, 0)
                norm(i, 1, 0, 1)
                for t in range(TT):
                    pool.wait_ge(x1_done, i * TT + t + 1)
                    nc.gpsimd.tensor_tensor(x1b[:, t, :], x1[:, t, :], bo[:, :], ALU.add).then_inc(x1b_done, 1)
                norm(i, 2, 1, 0)
                norm(i, 3, 1, 1)

        @block.scalar
        def _(act):
            act.wait_ge(raw_w, 16)
            raw = prob[:, :, :, :].rearrange("p a h t -> p (a h t)")
            nc.scalar.activation(w[:, HI, :, :].rearrange("p f n -> p (f n)"), raw, ACT.Copy).then_inc(w_hi, 1)

            def hi(i, job, out, in_, bias=None):
                if bias is None:
                    ins = nc.scalar.activation(out, in_, ACT.Copy)
                else:
                    ins = nc.scalar.activation(out, in_, ACT.Identity, bias=bias)
                ins.then_inc(hi_done, 1)

            def evac_v(i, job, which):
                act.wait_ge(job_done, i * NJ + J[job] + 1)
                if job == (("v", 0) if which == 0 else ("cv", 0)):
                    act.wait_ge(pv_done, i * 2 * STEPS)
                t = 2 * job[1]
                nc.scalar.activation(va[:, which, t:t + 2, :, 0:HD],
                                     ring[:, J[job] % HG, :].rearrange("p (t h d) -> p t h d", t=2, h=H),
                                     ACT.Copy).then_inc(read_act, 1)

            def attention(i, layer):
                def m_hi(g):
                    n = layer * NG + g
                    act.wait_ge(nmt_done, i * 2 * NG + n + 1)
                    act.wait_ge(mrow_in[g % 2], i * 4 * 32 + (n // 2) * 32)
                    nc.scalar.activation(mst[:, g % 2, HI, :], ps_m[0:HG * TT, 0:P], ACT.Copy).then_inc(mhi_done, 1)

                def o_evac(g):
                    act.wait_ge(pv_done, i * 2 * STEPS + layer * STEPS + TT * g + TT)
                    nc.scalar.activation(ot[:, g, :], ps_out[:, :], ACT.Copy).then_inc(oev_done, 1)

                m_hi(0)
                if layer == 0:
                    act.wait_ge(x2_out, i * 16)
                for s in range(STEPS):
                    n = layer * STEPS + s
                    for pair in range(2):
                        act.wait_ge(st_done, i * 4 * STEPS + 2 * n + pair + 1)
                        if pair == 0:
                            act.wait_ge(pv_done, i * 2 * STEPS + max(n - 1, 0))
                        nc.scalar.activation(prob[:, n % 2, 2 * pair:2 * pair + 2, :], ring[:, 2 * pair:2 * pair + 2, :],
                                             ACT.Exp, scale=HD ** -0.5).then_inc(exp_done, 1)
                    if s % TT == TT - 2 and s // TT + 1 < NG:
                        m_hi(s // TT + 1)
                    if s % TT == 0 and s:
                        o_evac(s // TT - 1)
                o_evac(NG - 1)

            def outputs(i, layer):
                for f in range(FC):
                    job = (f"nt{layer}", f)
                    act.wait_ge(job_done, i * NJ + J[job] + 1)
                    hi(i, job, nf[:, HI, f, :], ring[:, J[job] % HG, :], bcol[:, 2, f:f + 1] if layer else None)

            with act.Fori(0, B) as i:
                act.wait_ge(xt_in, i * 16 + 16)
                act.wait_ge(job_done, i * NJ)
                hi(i, ("x", 0), xf[:, HI, :, :], xraw[:, 0, :, :])
                act.wait_ge(ct_in, i * 16 + 16)
                hi(i, ("c", 0), cf[:, HI, :, :], xraw[:, 1, :, :])

                def rope_hi(n, job):
                    act.wait_ge(roped, i * 4 + n + 1)
                    hi(i, job, stage[:, job[1], 0 if job[0] == "q" else 2, :], cosq[:, n % 2, :])

                rope_hi(0, ("q", 0))
                rope_hi(1, ("k", 0))
                evac_v(i, ("v", 0), 0)
                evac_v(i, ("v", 1), 0)
                rope_hi(2, ("q", 1))
                rope_hi(3, ("k", 1))
                for m in range(FC):
                    job = ("ck", m)
                    act.wait_ge(job_done, i * NJ + J[job] + 1)
                    hi(i, job, stage_ck[:, m, HI, :], ring[:, J[job] % HG, :], bcol[:, 1, m:m + 1])
                evac_v(i, ("cv", 0), 1)
                evac_v(i, ("cv", 1), 1)
                attention(i, 0)
                outputs(i, 0)
                for f in range(FC):
                    job = ("xt", f)
                    act.wait_ge(job_done, i * NJ + J[job] + 1)
                    hi(i, job, xf[:, HI, f, :], ring[:, J[job] % HG, :])
                for m in range(FC):
                    job = ("cq", m)
                    act.wait_ge(job_done, i * NJ + J[job] + 1)
                    hi(i, job, stage[:, m, 0, :], ring[:, J[job] % HG, :], bcol[:, 0, m:m + 1])
                attention(i, 1)
                outputs(i, 1)

        @block.vector
        def _(dve):
            nc.vector.memset(qk[:, 0, :, :].bitcast(F32), 0.0).then_inc(zeroed, 1)
            dve.wait_ge(w_hi, 1)
            raw = prob[:, :, :, :].rearrange("p a h t -> p (a h t)")
            nc.vector.tensor_tensor(w[:, LO, :, :].rearrange("p f n -> p (f n)"), raw,
                                    w[:, HI, :, :].rearrange("p f n -> p (f n)").bitcast(F32), ALU.subtract) \
                .then_inc(w_ready, 1)
            dve.wait_ge(consts_dma, 48)

            def lo(i, job, out, in_, high, bias=None):
                dve.wait_ge(hi_done, split_at(i, job))
                if bias is None:
                    ins = nc.vector.tensor_tensor(out, in_, high.bitcast(F32), ALU.subtract)
                else:
                    ins = nc.vector.scalar_tensor_tensor(out=out, in0=in_, scalar=bias, in1=high.bitcast(F32),
                                                         op0=ALU.add, op1=ALU.subtract)
                ins.then_inc(lo_done, 1)
                return ins

            def lo_bank(i, job, out, high, bias=None):
                lo(i, job, out, ring[:, J[job] % HG, :], high, bias)

            def maxima(i, layer, n):
                g, r = n // (HG * TT), n % (HG * TT)
                dve.wait_ge(smax_done, i * 2 * NMAX + layer * NMAX + n + 1)
                if r == 0:
                    k = layer * NG + g
                    dve.wait_ge(nmt_done, i * 2 * NG + max(k - 1, 0))
                nc.vector.tensor_reduce(nm[:, g % 2, r:r + 1], ps_max[:, n % 2, :], axis=AX.X, op=ALU.max,
                                        negate=True).then_inc(max_done, 1)

            def m_lo(i, layer, g):
                dve.wait_ge(mhi_done, i * 2 * NG + layer * NG + g + 1)
                nc.vector.tensor_tensor(mst[:, g % 2, LO, :], ps_m[0:HG * TT, 0:P],
                                        mst[:, g % 2, HI, :].bitcast(F32), ALU.subtract).then_inc(mlo_done, 1)

            def attention(i, layer):
                for n in range(TT * LEAD):
                    maxima(i, layer, n)
                    if n == HG * TT + 1:
                        m_lo(i, layer, 0)
                for s in range(STEPS):
                    for n in range(TT * (s + LEAD), min(TT * (s + LEAD + 1), NMAX)):
                        maxima(i, layer, n)
                    if s % TT == TT - 2 and s // TT + 1 < NG:
                        m_lo(i, layer, s // TT + 1)

            def outputs(i, layer):
                for t in range(TT):
                    job = (f"ot{layer}", t)
                    bank = ring[:, J[job] % HG, :].rearrange("p (h e) -> p h e", h=H)
                    dve.wait_ge(job_done, i * NJ + J[job] + 1)
                    nc.vector.reciprocal(rden[:, t, :], bank[:, :, HD]).then_inc(rden_done, 1)
                    dve.wait_ge(rden_done, i * 2 * TT + layer * TT + t + 1)
                    nc.vector.tensor_tensor(on[:, t, :].rearrange("p (h d) -> p h d", h=H), bank[:, :, 0:HD],
                                            rden[:, t, :].unsqueeze(2).to_broadcast([P, H, HD]), ALU.mult) \
                        .then_inc(on_done, 1)
                for f in range(FC):
                    job = (f"nt{layer}", f)
                    lo_bank(i, job, nf[:, LO, f, :], nf[:, HI, f, :], bcol[:, 2, f:f + 1] if layer else None)
                for pair in range(2):
                    job = (f"w{layer}", pair)
                    n = 2 * layer + pair
                    at = slice(2 * pair, 2 * pair + 2)
                    if layer == 0:
                        dve.wait_ge(x_in, i * 16 + 16)
                    else:
                        dve.wait_ge(x1b_done, i * TT + 2 * pair + 2)
                    dve.wait_ge(job_done, i * NJ + J[job] + 1)
                    nc.vector.tensor_tensor(res[:, at, :], ring[:, J[job] % HG, :].rearrange("p (t n) -> p t n", t=2),
                                            (x1b if layer else xin)[:, at, :], ALU.add) \
                        .then_inc(res_done, 1)
                    dve.wait_ge(res_done, i * 4 + n + 1)
                    for t in (2 * pair, 2 * pair + 1):
                        nc.vector.bn_stats(st6[:, t, :], res[:, t, :]).then_inc(stat_done, 1)
                    for t in (2 * pair, 2 * pair + 1):
                        wait_alone(dve, stat_done, i * 8 + layer * TT + t + 1, w_hi, 1)
                        nc.vector.bn_aggr(mv[:, t, :], st6[:, t, :]).then_inc(mv_done, 1)
                for pair in range(2):
                    dve.wait_ge(rstd_done, i * 4 + 2 * layer + pair + 1)
                    if layer and pair == 0:
                        dve.wait_ge(x2_out, i * 16)
                    for t in (2 * pair, 2 * pair + 1):
                        nc.vector.tensor_scalar((x2s if layer else x1)[:, t, :], res[:, t, :], mv[:, t, 0:1],
                                                rstd[:, t, :], ALU.subtract, ALU.mult) \
                            .then_inc(x2_done if layer else x1_done, 1)

            with dve.Fori(0, B) as i:
                lo(i, ("x", 0), xf[:, LO, :, :], xraw[:, 0, :, :], xf[:, HI, :, :])
                lo(i, ("c", 0), cf[:, LO, :, :], xraw[:, 1, :, :], cf[:, HI, :, :])

                def rope(n, job):
                    bank = ring[:, J[job] % HG, :]
                    if n >= 2:
                        dve.wait_ge(lo_done, split_at(i, ROPE_JOBS[n - 2]))
                    dve.wait_ge(job_done, i * NJ + J[job] + 1)
                    nc.vector.tensor_tensor(cosq[:, n % 2, :], bank, trig[:, 0, :], ALU.mult) \
                        .then_inc(cos_done, 1)
                    nc.vector.stream_shuffle(rot[:, n % 2, :], bank, [k ^ 1 for k in range(32)]).then_inc(rotated, 1)

                def rope_lo(n, job):
                    slot = 0 if job[0] == "q" else 2
                    lo(i, job, stage[:, job[1], slot + 1, :], cosq[:, n % 2, :], stage[:, job[1], slot, :])

                rope(0, ("q", 0))
                rope(1, ("k", 0))
                rope_lo(0, ("q", 0))
                rope(2, ("q", 1))
                rope_lo(1, ("k", 0))
                rope(3, ("k", 1))
                rope_lo(2, ("q", 1))
                rope_lo(3, ("k", 1))
                for m in range(FC):
                    lo_bank(i, ("ck", m), stage_ck[:, m, LO, :], stage_ck[:, m, HI, :], bcol[:, 1, m:m + 1])
                attention(i, 0)
                outputs(i, 0)
                for f in range(FC):
                    lo_bank(i, ("xt", f), xf[:, LO, f, :], xf[:, HI, f, :])
                for m in range(FC):
                    lo_bank(i, ("cq", m), stage[:, m, 1, :], stage[:, m, HI, :], bcol[:, 0, m:m + 1])
                attention(i, 1)
                outputs(i, 1)

        @block.tensor
        def _(pe):
            pe.wait_ge(w_ready, 1)
            pe.wait_ge(consts, 7)
            pe.wait_ge(zeroed, 1)

            def products(out, pairs):
                parts = [(a, b) for a, b in ((HI, HI), (HI, LO), (LO, HI))]
                for n, (l, r) in enumerate(pairs):
                    for k, (a, b) in enumerate(parts):
                        ins = nc.tensor.matmul(out, l(a), r(b), start=(n == 0 and k == 0),
                                               stop=(n == len(pairs) - 1 and k == len(parts) - 1))
                return ins

            def by_feature(i, job, src):
                n, c = J[job], WCOL[job[0]] + P * job[1]
                read_before(pe, i, n)
                products(ring[:, n % HG, :],
                         [(lambda a, f=f: w[:, a, f, c:c + P], lambda b, f=f: src[:, b, f, :]) for f in range(FC)]) \
                    .then_inc(job_done, 1)

            def by_token(i, job, src):
                n, c = J[job], WCOL[job[0]]
                read_before(pe, i, n)
                for half in range(2):
                    t = P * (2 * job[1] + half)
                    ins = products(ring[:, n % HG, D * half:D * half + D],
                                   [(lambda a, f=f: src[:, a, f, t:t + P], lambda b, f=f: w[:, b, f, c:c + D])
                                    for f in range(FC)])
                ins.then_inc(job_done, 1)

            def attention(i, layer):
                def scores_max(n):
                    h, c = n // TT, n % TT
                    if n == 0:
                        if layer == 0:
                            pe.wait_ge(self_in[0], i * 96 + 96)
                        else:
                            pe.wait_ge(ck_in, i * 96 + 96)
                            pe.wait_ge(cq_in[0], i * 48 + 48)
                    if n == NMAX // 2:
                        if layer == 0:
                            pe.wait_ge(self_in[1], i * 96 + 96)
                        else:
                            pe.wait_ge(cq_in[1], i * 48 + 48)
                    pe.wait_ge(max_done, i * 2 * NMAX + max(layer * NMAX + n - 1, 0))
                    nc.tensor.matmul(ps_max[:, n % 2, :], qk[0:96, 0, h, P * c:P * c + P], qk[0:96, 1, h, :],
                                     start=True, stop=True).then_inc(smax_done, 1)

                def turn_maxima(g):
                    k = layer * NG + g
                    pe.wait_ge(max_done, i * 2 * NMAX + (k + 1) * HG * TT)
                    pe.wait_ge(mlo_done, i * 2 * NG + k)
                    nc.tensor.transpose(ps_m[0:HG * TT, 0:P], nm[:, g % 2, :], ident[:, :]).then_inc(nmt_done, 1)

                def scores(s, pair):
                    g, c, n = s // TT, s % TT, layer * STEPS + s
                    if n:
                        if s:
                            pe.wait_ge(exp_done, i * 4 * STEPS + 2 * (n - 1) + pair + 1)
                    if c == 0 and pair == 0:
                        pe.wait_ge(mrow_in[g % 2], i * 4 * 32 + ((layer * NG + g) // 2) * 32 + 32)
                    for h in (HG * g + 2 * pair, HG * g + 2 * pair + 1):
                        ins = nc.tensor.matmul(ring[:, h % HG, :], qk[:, 1, h, P * c:P * c + P], qk[:, 0, h, :],
                                               start=True, stop=True)
                    ins.then_inc(st_done, 1)

                def outs(s):
                    g, c, n = s // TT, s % TT, layer * STEPS + s
                    pe.wait_ge(exp_done, i * 4 * STEPS + 2 * n + 2)
                    if c == 0:
                        pe.wait_ge(oev_done, i * 2 * NG + layer * NG + g)
                    for j in range(HG):
                        ins = nc.tensor.matmul(ps_out[32 * j:32 * j + 32, :], va[:, layer, c, HG * g + j, :],
                                               prob[:, n % 2, j, :], start=(c == 0), stop=(c == TT - 1),
                                               tile_position=(0, 32 * j))
                    ins.then_inc(pv_done, 1)

                for n in range(TT * LEAD):
                    scores_max(n)
                    if n == HG * TT + 1:
                        turn_maxima(0)
                if layer == 0:
                    pe.wait_ge(read_act, i * NA + NA)
                pe.wait_ge(lo_done, split_at(i, ("cq", 1) if layer else ("ck", 1)))
                for s in range(STEPS):
                    ahead = list(range(TT * (s + LEAD), min(TT * (s + LEAD + 1), NMAX)))
                    if ahead:
                        scores_max(ahead[0])
                    scores(s, 0)
                    if ahead:
                        scores_max(ahead[1])
                    scores(s, 1)
                    if s % TT == TT - 2 and s // TT + 1 < NG:
                        turn_maxima(s // TT + 1)
                    if ahead:
                        scores_max(ahead[2])
                    if s:
                        outs(s - 1)
                    if ahead:
                        scores_max(ahead[3])
                outs(STEPS - 1)

            def outputs(i, layer):
                pe.wait_ge(oev_done, i * 2 * NG + layer * NG + NG)
                for t in range(TT):
                    job = (f"ot{layer}", t)
                    read_before(pe, i, J[job])
                    for g in range(NG):
                        ins = nc.tensor.transpose(ring[:, J[job] % HG, P * g:P * g + P], ot[:, g, P * t:P * t + P],
                                                  ident[:, :])
                    ins.then_inc(job_done, 1)
                pe.wait_ge(on_done, i * 2 * TT + layer * TT + TT)
                turn(i, f"nt{layer}", on)
                pe.wait_ge(lo_done, split_at(i, (f"nt{layer}", 1)))
                for pair in range(2):
                    by_token(i, (f"w{layer}", pair), nf)

            def turn(i, name, src):
                for f in range(FC):
                    job = (name, f)
                    read_before(pe, i, J[job])
                    for t in range(TT):
                        ins = nc.tensor.transpose(ring[:, J[job] % HG, P * t:P * t + P],
                                                  src[:, t, P * f:P * f + P], ident[:, :])
                    ins.then_inc(job_done, 1)

            with pe.Fori(0, B) as i:
                pe.wait_ge(lo_done, split_at(i, ("x", 0)))
                by_feature(i, ("q", 0), xf)
                by_feature(i, ("k", 0), xf)
                by_token(i, ("v", 0), xf)
                by_token(i, ("v", 1), xf)
                by_feature(i, ("q", 1), xf)
                by_feature(i, ("k", 1), xf)
                pe.wait_ge(lo_done, split_at(i, ("c", 0)))
                by_feature(i, ("ck", 0), cf)
                by_feature(i, ("ck", 1), cf)
                by_token(i, ("cv", 0), cf)
                by_token(i, ("cv", 1), cf)
                attention(i, 0)
                outputs(i, 0)
                pe.wait_ge(x1_done, i * TT + TT)
                turn(i, "xt", x1)
                pe.wait_ge(lo_done, split_at(i, ("xt", 1)))
                by_feature(i, ("cq", 0), xf)
                by_feature(i, ("cq", 1), xf)
                attention(i, 1)
                outputs(i, 1)


NE = 8
NSHARED = 2
EXPERTS = list(range(NE, NE + NSHARED)) + list(range(NE))
NX = len(EXPERTS)
I = 256
IC = I // P
CAP = 1280
BF16 = mybir.dt.bfloat16
ROUTE_STEPS = 22


def moe_phase(nc, x2, w_moe, w_gate, index, out):
    with ExitStack() as ctx:
        def sb(name, shape, dt=F32):
            return ctx.enter_context(nc.sbuf_tensor(name, shape, dt))

        def sem(name):
            return ctx.enter_context(nc.semaphore(name))

        w = sb("we", [P, NX, 2, 3, FC, I], F32R)
        wraw = sb("weraw", [P, 2, 3, FC, I])
        wg = sb("wg", [P, 2, FC, NE], F32R)
        wgraw = sb("wgraw", [P, FC, NE])
        ident = sb("ident2", [P, P])
        before = sb("before", [P, P], BF16)
        ones = sb("ones", [P, P], BF16)
        idx = sb("idx", [P, TT, NE])
        mhalf = sb("mhalf2", [P, TT, 1])
        eps = sb("eps2", [P, TT, 1])
        xin = sb("x2in", [P, 2, TT, D])
        xf = sb("x2f", [P, 2, FC, T], F32R)
        sg = sb("sg", [P, IC, T])
        h = sb("h", [P, IC, T])
        hf = sb("hf", [P, 2, 2, IC, T], F32R)
        y = sb("y", [P, TT, D])
        yo = sb("yo", [P, TT, D])
        st6 = sb("st62", [P, TT, 6])
        mv = sb("mv2", [P, TT, 2])
        rstd = sb("rstd2", [P, TT, 1])
        r4 = sb("r4", [P, 8, TT, 1])
        r32 = sb("r32", [P, 10, TT, NE])
        sel = sb("sel", [P, TT, NE], BF16)
        comb = sb("comb", [P, TT, NE])
        carry = sb("carry", [P, 1, NE])

        ps_gu = ctx.enter_context(nc.psum_tensor("ps_gu", [P, 2 * IC, T], F32))
        ps_dn = ctx.enter_context(nc.psum_tensor("ps_dn", [P, 2, T], F32))
        ps_x = ctx.enter_context(nc.psum_tensor("ps_x", [P, T], F32))
        ps_r = ctx.enter_context(nc.psum_tensor("ps_r", [P, T], F32))
        logits = ps_r[:, 0:TT * NE].rearrange("p (t e) -> p t e", t=TT)
        counts = ps_r[:, P:P + (TT + 1) * NE].rearrange("p (t e) -> p t e", e=NE)

        w_in = [sem("w_in0"), sem("w_in1")]
        wg_in, idx_in = sem("wg_in"), sem("idx_in")
        w_hi, w_lo, consts, ready = sem("we_hi"), sem("we_lo"), sem("consts2"), sem("ready")
        x_in = [sem("x2_in0"), sem("x2_in1")]
        xt_done, xhi_done, xlo_done = sem("xt2_done"), sem("xhi_done"), sem("xlo_done")
        logits_done, shift_done, exp_done, step_done, cnt_done = (
            sem("logits_done"), sem("shift_done"), sem("rexp_done"), sem("step_done"), sem("cnt_done"))
        gu_done, silu_done, h_done, hhi_done, hlo_done = (
            sem("gu_done"), sem("silu_done"), sem("h_done"), sem("hhi_done"), sem("hlo_done"))
        dn_done, acc_done = sem("dn_done"), sem("acc_done")
        stat_done, mv_done, var_done, rstd_done = sem("stat2"), sem("mv_done2"), sem("var2"), sem("rstd2d")
        y_done, out_done = sem("y_done"), sem("out_done")
        GU, HN, DN, ACC = 4 * NX, IC * NX, 2 * NX, TT * NX

        block = ctx.enter_context(nc.Block())

        @block.sync
        def _(sp):
            sp.dma_start(wgraw[:, :, :], w_gate).then_inc(wg_in, 16)
            sp.dma_start(idx[:, :, :], index).then_inc(idx_in, 16)
            for n, e in enumerate(EXPERTS):
                if n >= 2:
                    sp.wait_ge(w_lo, n - 1)
                sp.dma_start(wraw[:, n % 2, :, :, :], w_moe[e]).then_inc(w_in[n % 2], 16)

            def load(i, par):
                sp.dma_start(xin[:, par, :, :], x2[i, :, :, :]).then_inc(x_in[par], 16)

            def store(i):
                wait_alone(sp, y_done, i * TT + TT, idx_in, 16)
                sp.dma_start(out[i, :, :, :], yo[:, :, :]).then_inc(out_done, 16)

            load(0, 0)
            load(1, 1)
            with sp.Fori(0, B // 2 - 1) as k:
                for par in range(2):
                    store(2 * k + par)
                    load(2 * k + par + 2, par)
            store(B - 2)
            store(B - 1)
            sp.wait_ge(out_done, B * 16)

        @block.gpsimd
        def _(pool):
            nc.gpsimd.memset(ident[:, :], 0.0).then_inc(consts, 1)
            nc.gpsimd.memset(before[:, :], 1.0).then_inc(consts, 1)
            nc.gpsimd.memset(ones[:, :], 1.0).then_inc(consts, 1)
            nc.gpsimd.memset(mhalf[:, :, :], -0.5).then_inc(consts, 1)
            nc.gpsimd.memset(eps[:, :, :], EPS).then_inc(consts, 1)
            pool.wait_ge(consts, 5)
            nc.gpsimd.affine_select(out=ident[:, :], in_=ident[:, :], compare_op=ALU.not_equal, fill=1.0,
                                    base=0, pattern=[[-1, P]], channel_multiplier=1).then_inc(consts, 1)
            nc.gpsimd.affine_select(out=before[:, :], in_=before[:, :], compare_op=ALU.is_gt, fill=0.0,
                                    base=0, pattern=[[1, P]], channel_multiplier=-1).then_inc(consts, 1)
            with pool.Fori(0, B) as i:
                for pair in range(2):
                    at = slice(2 * pair, 2 * pair + 2)
                    pool.wait_ge(mv_done, i * TT + 2 * pair + 2)
                    nc.gpsimd.tensor_tensor(rstd[:, at, :], mv[:, at, 1:2], eps[:, at, :], ALU.add).then_inc(var_done, 1)
                    pool.wait_ge(var_done, i * 2 + pair + 1)
                    nc.gpsimd.tensor_tensor(rstd[:, at, :], rstd[:, at, :], mhalf[:, at, :], ALU.pow) \
                        .then_inc(rstd_done, 1)

        @block.scalar
        def _(act):
            act.wait_ge(wg_in, 16)
            nc.scalar.activation(wg[:, HI, :, :], wgraw[:, :, :], ACT.Copy).then_inc(w_hi, 1)
            for n in range(NX):
                act.wait_ge(w_in[n % 2], 16 * (n // 2) + 16)
                nc.scalar.activation(w[:, n, HI, :, :, :].rearrange("p a f i -> p (a f i)"),
                                     wraw[:, n % 2, :, :, :].rearrange("p a f i -> p (a f i)"),
                                     ACT.Copy).then_inc(w_hi, 1)
            with act.Fori(0, B) as i:
                for f in range(FC):
                    act.wait_ge(xt_done, i * FC + f + 1)
                    if f == 0:
                        act.wait_ge(gu_done, i * GU)
                    nc.scalar.activation(xf[:, HI, f, :], ps_x[:, :], ACT.Copy).then_inc(xhi_done, 1)
                act.wait_ge(shift_done, i + 1)
                nc.scalar.activation(r32[:, 1, :, :], r32[:, 0, :, :], ACT.Exp).then_inc(exp_done, 1)
                for n in range(NX):
                    for c in range(IC):
                        act.wait_ge(gu_done, i * GU + 4 * n + 2 * c + 1)
                        act.wait_ge(h_done, i * HN + max(IC * (n - 1) + c + 1, 0))
                        nc.scalar.activation(sg[:, c, :], ps_gu[:, 2 * c, :], ACT.Silu).then_inc(silu_done, 1)
                    for c in range(IC):
                        act.wait_ge(h_done, i * HN + IC * n + c + 1)
                        if c == 0:
                            act.wait_ge(dn_done, i * DN + max(2 * (n - 1), 0))
                        nc.scalar.activation(hf[:, n % 2, HI, c, :], h[:, c, :], ACT.Copy).then_inc(hhi_done, 1)

        @block.vector
        def _(dve):
            nc.vector.memset(carry[:, :, :], 0.0).then_inc(ready, 1)
            dve.wait_ge(w_hi, 1)
            nc.vector.tensor_tensor(wg[:, LO, :, :], wgraw[:, :, :], wg[:, HI, :, :].bitcast(F32), ALU.subtract) \
                .then_inc(ready, 1)
            for n in range(NX):
                dve.wait_ge(w_hi, n + 2)
                nc.vector.tensor_tensor(w[:, n, LO, :, :, :].rearrange("p a f i -> p (a f i)"),
                                        wraw[:, n % 2, :, :, :].rearrange("p a f i -> p (a f i)"),
                                        w[:, n, HI, :, :, :].rearrange("p a f i -> p (a f i)").bitcast(F32),
                                        ALU.subtract).then_inc(w_lo, 1)
            dve.wait_ge(ready, 2)
            dve.wait_ge(idx_in, 16)

            def route(i):
                done = [0]

                def step(ins):
                    done[0] += 1
                    ins.then_inc(step_done, 1)
                    dve.wait_ge(step_done, i * ROUTE_STEPS + done[0])

                def wide(a):
                    return a.to_broadcast([P, TT, NE])

                v = nc.vector
                mx, total, inv, top1, j1, top2, j2, den = (r4[:, k, :, :] for k in range(8))
                shifted, e, s, eq, cand, one, rest, two, pos, keep = (r32[:, k, :, :] for k in range(10))
                dve.wait_ge(logits_done, i + 1)
                dve.wait_ge(acc_done, i * ACC)
                step(v.tensor_reduce(mx, logits, axis=AX.X, op=ALU.max))
                v.tensor_tensor(shifted, logits, wide(mx), ALU.subtract).then_inc(shift_done, 1)
                dve.wait_ge(exp_done, i + 1)
                step(v.tensor_reduce(total, e, axis=AX.X, op=ALU.add))
                step(v.reciprocal(inv, total))
                step(v.tensor_tensor(s, e, wide(inv), ALU.mult))
                step(v.tensor_reduce(top1, s, axis=AX.X, op=ALU.max))
                step(v.tensor_tensor(eq, s, wide(top1), ALU.is_equal))
                step(v.tensor_tensor(cand, eq, idx[:, :, :], ALU.mult))
                step(v.tensor_reduce(j1, cand, axis=AX.X, op=ALU.min))
                step(v.tensor_tensor(one, idx[:, :, :], wide(j1), ALU.is_equal))
                step(v.scalar_tensor_tensor(out=rest, in0=one, scalar=-2.0, in1=s, op0=ALU.mult, op1=ALU.add))
                step(v.tensor_reduce(top2, rest, axis=AX.X, op=ALU.max))
                step(v.tensor_tensor(eq, rest, wide(top2), ALU.is_equal))
                step(v.tensor_tensor(cand, eq, idx[:, :, :], ALU.mult))
                step(v.tensor_reduce(j2, cand, axis=AX.X, op=ALU.min))
                step(v.tensor_tensor(two, idx[:, :, :], wide(j2), ALU.is_equal))
                step(v.tensor_tensor(sel[:, :, :], one, two, ALU.add))
                step(v.scalar_tensor_tensor(out=den, in0=top1, scalar=1e-20, in1=top2, op0=ALU.add, op1=ALU.add))
                step(v.reciprocal(inv, den))
                step(v.tensor_tensor(cand, s, wide(inv), ALU.mult))
                dve.wait_ge(cnt_done, i + 1)
                step(v.tensor_tensor(pos, counts[:, 0:TT, :], carry[:, :, :].to_broadcast([P, TT, NE]), ALU.add))
                v.scalar_tensor_tensor(out=keep, in0=pos, scalar=float(CAP), in1=sel[:, :, :],
                                       op0=ALU.is_lt, op1=ALU.mult).then_inc(step_done, 1)
                v.tensor_tensor(carry[:, :, :], carry[:, :, :], counts[:, TT:TT + 1, :], ALU.add).then_inc(ready, 1)
                done[0] += 1
                dve.wait_ge(step_done, i * ROUTE_STEPS + done[0])
                dve.wait_ge(ready, i + 3)
                step(v.tensor_tensor(comb[:, :, :], cand, keep, ALU.mult))
                assert done[0] == ROUTE_STEPS, done

            def accumulate(i, par, n):
                for t in range(TT):
                    dve.wait_ge(dn_done, i * DN + 2 * n + t // 2 + 1)
                    if n:
                        dve.wait_ge(acc_done, i * ACC + TT * (n - 1) + t + 1)
                    part = ps_dn[:, t // 2, D * (t % 2):D * (t % 2) + D]
                    base = y[:, t, :] if n else xin[:, par, t, :]
                    if n < NSHARED:
                        ins = nc.vector.tensor_tensor(y[:, t, :], part, base, ALU.add)
                    else:
                        e = EXPERTS[n]
                        ins = nc.vector.scalar_tensor_tensor(out=y[:, t, :], in0=part, scalar=comb[:, t, e:e + 1],
                                                             in1=base, op0=ALU.mult, op1=ALU.add)
                    ins.then_inc(acc_done, 1)

            with dve.Fori(0, B // 2) as k:
                for par in range(2):
                    i = 2 * k + par
                    for f in range(FC):
                        dve.wait_ge(xhi_done, i * FC + f + 1)
                        nc.vector.tensor_tensor(xf[:, LO, f, :], ps_x[:, :], xf[:, HI, f, :].bitcast(F32),
                                                ALU.subtract).then_inc(xlo_done, 1)
                    route(i)
                    for n in range(NX):
                        for c in range(IC):
                            dve.wait_ge(silu_done, i * HN + IC * n + c + 1)
                            dve.wait_ge(gu_done, i * GU + 4 * n + 2 * c + 2)
                            dve.wait_ge(hlo_done, i * HN + max(IC * (n - 1) + c + 1, 0))
                            nc.vector.tensor_tensor(h[:, c, :], ps_gu[:, 2 * c + 1, :], sg[:, c, :], ALU.mult) \
                                .then_inc(h_done, 1)
                        for c in range(IC):
                            dve.wait_ge(hhi_done, i * HN + IC * n + c + 1)
                            nc.vector.tensor_tensor(hf[:, n % 2, LO, c, :], h[:, c, :],
                                                    hf[:, n % 2, HI, c, :].bitcast(F32), ALU.subtract) \
                                .then_inc(hlo_done, 1)
                        if n:
                            accumulate(i, par, n - 1)
                    accumulate(i, par, NX - 1)
                    dve.wait_ge(acc_done, i * ACC + ACC)
                    for t in range(TT):
                        nc.vector.bn_stats(st6[:, t, :], y[:, t, :]).then_inc(stat_done, 1)
                    for t in range(TT):
                        wait_alone(dve, stat_done, i * TT + t + 1, idx_in, 16)
                        nc.vector.bn_aggr(mv[:, t, :], st6[:, t, :]).then_inc(mv_done, 1)
                    dve.wait_ge(out_done, i * 16)
                    for t in range(TT):
                        dve.wait_ge(rstd_done, i * 2 + t // 2 + 1)
                        nc.vector.tensor_scalar(yo[:, t, :], y[:, t, :], mv[:, t, 0:1], rstd[:, t, :],
                                                ALU.subtract, ALU.mult).then_inc(y_done, 1)

        @block.tensor
        def _(pe):
            pe.wait_ge(consts, 7)
            pe.wait_ge(ready, 2)

            def products(o, pairs):
                parts = ((HI, HI), (HI, LO), (LO, HI))
                for n, (l, r) in enumerate(pairs):
                    for k, (a, b) in enumerate(parts):
                        ins = nc.tensor.matmul(o, l(a), r(b), start=(n == 0 and k == 0),
                                               stop=(n == len(pairs) - 1 and k == len(parts) - 1))
                return ins

            def gate_up(i, n):
                for c in range(IC):
                    for kind in range(2):
                        pe.wait_ge(h_done if kind else silu_done, i * HN + max(IC * (n - 1) + c + 1, 0))
                        products(ps_gu[:, 2 * c + kind, :],
                                 [(lambda a, f=f: w[:, n, a, kind, f, P * c:P * c + P], lambda b, f=f: xf[:, b, f, :])
                                  for f in range(FC)]).then_inc(gu_done, 1)

            def down(i, n):
                pe.wait_ge(hlo_done, i * HN + IC * n + IC)
                for pair in range(2):
                    pe.wait_ge(acc_done, i * ACC + max(TT * (n - 1) + 2 * pair + 2, 0))
                    for half in range(2):
                        t = P * (2 * pair + half)
                        ins = products(ps_dn[:, pair, D * half:D * half + D],
                                       [(lambda a, c=c: hf[:, n % 2, a, c, t:t + P], lambda b, c=c: w[:, n, b, 2, c, :])
                                        for c in range(IC)])
                    ins.then_inc(dn_done, 1)

            def count(i):
                pe.wait_ge(step_done, i * ROUTE_STEPS + 16)
                for t in range(TT + 1):
                    terms = ([(before, t)] if t < TT else []) + [(ones, u) for u in range(t)]
                    for k, (m, u) in enumerate(terms):
                        ins = nc.tensor.matmul(counts[:, t, :], m[:, :], sel[:, u, :], start=(k == 0),
                                               stop=(k == len(terms) - 1))
                ins.then_inc(cnt_done, 1)

            with pe.Fori(0, B // 2) as kk:
                for par in range(2):
                    i = 2 * kk + par
                    pe.wait_ge(x_in[par], kk * 16 + 16)
                    for f in range(FC):
                        pe.wait_ge(xlo_done, i * FC + f)
                        for t in range(TT):
                            ins = nc.tensor.transpose(ps_x[:, P * t:P * t + P], xin[:, par, t, P * f:P * f + P],
                                                      ident[:, :])
                        ins.then_inc(xt_done, 1)
                    pe.wait_ge(xlo_done, i * FC + FC)
                    for t in range(TT):
                        ins = products(logits[:, t, :],
                                       [(lambda a, f=f, t=t: xf[:, a, f, P * t:P * t + P], lambda b, f=f: wg[:, b, f, :])
                                        for f in range(FC)])
                    ins.then_inc(logits_done, 1)
                    for n in range(NX):
                        pe.wait_ge(w_lo, n + 1)
                        gate_up(i, n)
                        if n == 0:
                            count(i)
                        if n:
                            down(i, n - 1)
                    down(i, NX - 1)


SCRATCH = {"x2": [B, P, TT, D], "hbm_self": [FC, P, SLOTS, T], "hbm_ck": [P, FC, 2, T], "hbm_cq": [FC, P, 2, T]}


def program(nc, ap, scratch, out):
    attention_phase(nc, ap["x"], ap["xT"], ap["cT"], ap["w_att"], ap["tables"], ap["b_cols"], ap["bo_rows"],
                    scratch["x2"], scratch["hbm_self"], scratch["hbm_ck"], scratch["hbm_cq"])
    moe_phase(nc, scratch["x2"], ap["w_moe"], ap["w_gate"], ap["index"], out)


def layout(inp):
    f = {k: np.asarray(v) for k, v in inp.items()}

    def by_token(a):
        return np.ascontiguousarray(a.reshape(a.shape[0], TT, P, D).transpose(0, 2, 1, 3))

    def by_feature(a):
        return np.ascontiguousarray(a.transpose(0, 2, 1).reshape(a.shape[0], FC, P, T).transpose(0, 2, 1, 3))

    def col(b):
        return b.reshape(FC, P).transpose(1, 0)

    w_all = np.concatenate([f["L0_attn_Wqkv"], f["L0_attn_Wout"]]
                           + [f[f"L0_xattn_w_{n}"].T for n in ("q", "k", "v", "o")], axis=1)
    inv_freq = (1.0 / np.float32(10000.0) ** (np.arange(0, HD, 2, dtype=np.float32) / np.float32(HD))).astype(np.float32)
    angle = np.arange(T, dtype=np.float32)[None, :] * inv_freq[np.arange(P) % (HD // 2)][:, None]
    sign = np.where(np.arange(P) % 2 == 0, -1.0, 1.0).astype(np.float32)[:, None]
    def shared(a):
        return a.reshape(NSHARED, I, D)

    gate = np.concatenate([f["L0_ffn_we_gate"], shared(f["L0_ffn_ws_gate"])]).transpose(0, 2, 1)
    up = np.concatenate([f["L0_ffn_we_up"], shared(f["L0_ffn_ws_up"])]).transpose(0, 2, 1)
    down = np.concatenate([f["L0_ffn_we_down"].transpose(0, 2, 1), shared(f["L0_ffn_ws_down"].T)])
    w_moe = np.ascontiguousarray(np.stack([gate, up, down], axis=1).reshape(NX, 3, FC, P, I).transpose(0, 3, 1, 2, 4))
    return {
        "x": by_token(f["x"]), "xT": by_feature(f["x"]), "cT": by_feature(f["ctx_1024"]),
        "w_att": np.ascontiguousarray(w_all.reshape(FC, P, NW).transpose(1, 0, 2)),
        "tables": np.stack([np.cos(angle), np.sin(angle) * sign], axis=1).astype(np.float32),
        "b_cols": np.ascontiguousarray(np.stack([col(f[f"L0_xattn_b_{n}"]) for n in ("q", "k", "v")], axis=1)),
        "w_moe": w_moe, "w_gate": np.ascontiguousarray(f["L0_ffn_gate_w"].T.reshape(FC, P, NE).transpose(1, 0, 2)),
        "index": np.ascontiguousarray(np.broadcast_to(np.arange(NE, dtype=np.float32) - NE, (P, TT, NE))),
        "bo_rows": np.ascontiguousarray(np.broadcast_to(f["L0_xattn_b_o"], (P, D))),
    }

def kernel(**inputs):
    import concourse.bacc as bacc
    from concourse.bass_utils import run_bass_kernel_spmd as run

    nc = bacc.Bacc("TRN2", target_bir_lowering=False, num_devices=1)
    arrays = layout(inputs)
    ap = {n: nc.dram_tensor(n, a.shape, F32, kind="ExternalInput").ap() for n, a in arrays.items()}
    out = nc.dram_tensor("out", [B, P, TT, D], F32, kind="ExternalOutput").ap()
    scratch = {n: nc.dram_tensor(n, s, F32, kind="Internal").ap() for n, s in SCRATCH.items()}
    program(nc, ap, scratch, out)
    r = run(nc, [arrays], core_ids=[0])
    got = np.asarray(r.results[0]["out"])
    return np.ascontiguousarray(got.transpose(0, 2, 1, 3).reshape(B, T, D))
```

```python
import concourse.bass as bass
from concourse import mybir
from contextlib import ExitStack

import numpy as np

F32 = mybir.dt.float32
F32R = mybir.dt.float32r
ALU = mybir.AluOpType
ACT = mybir.ActivationFunctionType
AX = mybir.AxisListType

P = 128
B, T, D = 8, 512, 256
H, HD = 16, 16
TT = T // P
FC = D // P
HG = 4
NG = H // HG
HM = H // FC
LEAD = 6
PV_AT = 2
JOB_AT = 3
DVE_AT = 0
ACT_AT = 0
STEPS = NG * TT
NMAX = H * TT
EPS = 1e-5
HI, LO = 0, 1
SLOTS = 4

WCOL = {n: i * D for i, n in enumerate(("q", "k", "v", "w0", "cq", "ck", "cv", "w1"))}
NW = len(WCOL) * D

FIRST, SECOND = 0, 1
SELF, CROSS = 0, 1
TASKS = {
    FIRST: {
        0: [("cq", 0, -1), ("ck", 0, -1)], 1: [("ot1", 0, -2), ("cq", 1, -1)], 2: [("ot1", 1, -2), ("nm0", 1, 0)],
        3: [("ot1", 2, -2), ("ck", 1, -1)], 4: [("ot1", 3, -2), ("cv", 0, -1)], 5: [("cv", 1, -1)],
        6: [("nm0", 2, 0)], 7: [("nt1", 0, -2)], 8: [("nt1", 1, -2)], 9: [("w1", 0, -2)],
        10: [("w1", 1, -2), ("nm0", 3, 0)], 11: [("x", 0, 1)], 12: [("ln1", 0, -2)], 13: [("x1b", 0, -1)],
        14: [("nm1", 0, -1)],
    },
    SECOND: {
        0: [("q", 0, 1)], 1: [("k", 0, 1), ("qf", 0, 1), ("ot0", 0, 0)], 2: [("ot0", 1, 0), ("nm1", 1, -1)],
        3: [("kf", 0, 1), ("q", 1, 1), ("ot0", 2, 0)], 4: [("k", 1, 1), ("qf", 1, 1), ("ot0", 3, 0)],
        5: [("kf", 1, 1), ("v", 0, 1)], 6: [("nt0", 0, 0), ("nm1", 2, -1)], 7: [("nt0", 1, 0), ("v", 1, 1)],
        8: [("w0", 0, 0)], 9: [("w0", 1, 0)], 10: [("nm1", 3, -1)], 11: [("ln0", 0, 0)], 12: [("c", 0, 0)],
        13: [("xt", 0, 0), ("xt", 1, 0)], 14: [("nm0", 0, 1)],
    },
}
PER = {"q": 2, "k": 2, "v": 2, "ck": 2, "cv": 2, "xt": 2, "cq": 2, "nt0": 2, "nt1": 2, "w0": 2, "w1": 2,
       "ot0": TT, "ot1": TT, "nm0": NG, "nm1": NG, "x": 1, "c": 1}
ORDER = [task for half in (FIRST, SECOND) for s in sorted(TASKS[half]) for task in TASKS[half][s]
         if task[0] in PER and task[0] not in ("x", "c")]
assert len(ORDER) % 2 == 0
SPLIT = ("q", "k", "ck", "cq", "xt", "nt0", "nt1", "nm0", "nm1", "x", "c")


def exists(b):
    return not isinstance(b, int) or 0 <= b < B


def upto(kind, b, n):
    return b * PER[kind] + n + 1


def wait_alone(eng, s, value, met, least):
    value = value if isinstance(value, int) else eng.snap(eng.to_reg(value))
    eng.wait_ge(met, least)
    eng.wait_ge(s, value)


def attention_phase(nc, x, xT, cT, w_att, tables, b_cols, bo_rows, x2, hbm_self, hbm_ck, hbm_cq, slots_x):
    with ExitStack() as ctx:
        def sb(name, shape, dt=F32):
            return ctx.enter_context(nc.sbuf_tensor(name, shape, dt))

        def sem(name):
            return ctx.enter_context(nc.semaphore(name))

        w = sb("w", [P, 2, FC, NW], F32R)
        ident = sb("ident", [P, P])
        trig = sb("trig", [P, 2, T])
        bcol = sb("bcol", [P, 3, FC])
        bo = sb("bo", [P, D])
        xin = sb("xin", [P, TT, D])
        raw = sb("raw", [P, FC, T])
        xf = sb("xf", [P, 2, FC, T], F32R)
        cf = sb("cf", [P, 2, FC, T], F32R)
        nf = cf
        ot = sb("ot", [P, NG, T])
        on = sb("on", [P, TT, D])
        res = sb("res", [P, TT, D])
        rot = res[:, :, :].rearrange("p (a u) d -> p a (u d)", a=2)
        cosq = sb("cosq", [P, 2, T])
        stage = sb("stage", [P, FC, SLOTS, T], F32R)
        qk = sb("qk", [P, 2, H, T], F32R)
        va = sb("va", [P, 2, TT, H, 2 * HD])
        prob = sb("prob", [P, 2, HG, T])
        nm = sb("nm", [P, 2, HG * TT])
        mst = sb("mst", [HG * TT, 2, 2, P], F32R)
        rden = sb("rden", [P, TT, H])
        x1 = sb("x1", [P, TT, D])
        x1b = sb("x1b", [P, TT, D])
        st6 = sb("st6", [P, TT, 6])
        mv = sb("mv", [P, TT, 2])
        rstd = sb("rstd", [P, TT, 1])
        mhalf = sb("mhalf", [P, TT, 1])
        eps = sb("eps", [P, TT, 1])
        zeros = sb("zeros", [P, D])

        ps_sc = ctx.enter_context(nc.psum_tensor("ps_sc", [P, 3, T], F32))
        ps_max = ctx.enter_context(nc.psum_tensor("ps_max", [P, 2, T], F32))
        ps_out = ctx.enter_context(nc.psum_tensor("ps_out", [P, T], F32))
        ps_job = ctx.enter_context(nc.psum_tensor("ps_job", [P, 2, T], F32))

        raw_w, w_hi, w_ready, consts = sem("raw_w"), sem("w_hi"), sem("w_ready"), sem("consts")
        consts_dma = sem("consts_dma")
        in_sem = {n: sem(f"{n}_in") for n in ("x", "c", "xin")}
        job_done = {k: sem(f"{k}_done") for k in PER if k not in ("x", "c")}
        read = {k: sem(f"{k}_read") for k in job_done}
        hi_done = {k: sem(f"{k}_hi") for k in SPLIT}
        lo_done = {k: sem(f"{k}_lo") if k in ("q", "k", "x", "c") else read[k] for k in SPLIT}
        sin_done = {k: sem(f"{k}_sin") for k in ("q", "k")}
        roped = {k: sem(f"{k}_roped") for k in ("q", "k")}
        self_out = [sem(f"self_out{m}") for m in range(FC)]
        ck_out, cq_out = sem("ck_out"), sem("cq_out")
        stack_in = [[sem(f"stack_in{a}{g}") for g in range(NG)] for a in range(2)]
        smax_done, max_done, st_done, exp_done, pv_done, oev_done = (
            [sem(f"{n}{a}") for a in range(2)] for n in ("smax", "max", "st", "exp", "pv", "oev"))
        mrow_in = [[sem(f"mrow_in{a}{g}") for g in range(2)] for a in range(2)]
        rden_done, stat_done, mv_done, var_done, rstd_done, ln_done = (
            [sem(f"{n}{a}") for a in range(2)] for n in ("rden", "stat", "mv", "var", "rstd", "ln"))
        x1b_done, x2_out, cleared = sem("x1b_done"), sem("x2_out"), sem("cleared")

        block = ctx.enter_context(nc.Block())

        def tasks(half, s, k):
            return [(kind, n, k + off) for kind, n, off in TASKS[half].get(s, []) if exists(k + off)]

        def instances(half, k):
            def one(half, k):
                a = (SELF, k) if half == FIRST else (CROSS, k - 1)
                return a if exists(a[1]) else None

            cur = one(half, k)
            nxt = one(SECOND, k) if half == FIRST else one(FIRST, k + 1)
            h, p, prv = half, k, None
            while prv is None and not (isinstance(p, int) and p < -1):
                h, p = (SECOND, p - 1) if h == FIRST else (FIRST, p)
                prv = one(h, p)
            return cur, nxt, prv

        def unfinished(h, k):
            return exists(k if h == SECOND else k - 2)

        def every_period(eng, half):
            for k in (-1, 0, 1):
                half(FIRST, k)
                half(SECOND, k)
            with eng.Fori(2, B - 1) as k:
                half(FIRST, k)
                half(SECOND, k)
            for k in (B - 1, B, B + 1):
                half(FIRST, k)
                half(SECOND, k)

        def bank(kind, n):
            return ps_job[:, [t[:2] for t in ORDER].index((kind, n)) % 2, :]

        def maxima_of(s, cur, nxt):
            inst, first = (cur, TT * (s + LEAD)) if s + LEAD < STEPS else (nxt, TT * (s + LEAD - STEPS))
            return [(inst, n) for n in range(first, first + TT)] if inst else []

        def wait_done(eng, s, kind, b, n):
            if exists(b):
                eng.wait_ge(s, upto(kind, b, n))

        @block.sync
        def _(sp):
            sp.dma_start(prob[:, :, :, :].rearrange("p a h t -> p (a h t)"),
                         w_att[:, :, :].rearrange("p f n -> p (f n)")).then_inc(raw_w, 16)
            sp.dma_start(trig[:, :, :], tables).then_inc(consts_dma, 16)
            sp.dma_start(bcol[:, :, :], b_cols).then_inc(consts_dma, 16)
            sp.dma_start(bo[:, :], bo_rows).then_inc(consts_dma, 16)

            def mrows(a, b, g):
                sp.wait_ge(read[f"nm{a}"], upto(f"nm{a}", b, g))
                for part in (HI, LO):
                    row = 96 + part
                    sp.dma_start(
                        qk[row:row + 1, 0, HG * g:HG * g + HG, :].rearrange("o h (c q) -> o (h c) q", q=P).bitcast(F32),
                        mst[:, g % 2, part, :].bitcast(F32)).then_inc(mrow_in[a][g % 2], 16)

            def stack(inst, before, g):
                a, b = inst
                m, rows = g // 2, slice(64 * (g % 2), 64 * (g % 2) + 64)
                if before:
                    free = before[1] * NMAX + 4 * TT * (g + 1)
                    free = free if isinstance(free, int) else sp.snap(sp.to_reg(free))
                if a == SELF:
                    sp.wait_ge(self_out[m], b * 16 + 16)
                else:
                    out_c = b * 16 + 16
                    out_c = out_c if isinstance(out_c, int) else sp.snap(sp.to_reg(out_c))
                    sp.wait_ge(ck_out, out_c)
                    sp.wait_ge(cq_out, out_c)
                if before:
                    sp.wait_ge(st_done[before[0]], free)
                for r, (qp, kp) in enumerate(((HI, HI), (HI, LO), (LO, HI))):
                    for s, part in ((0, qp), (1, kp)):
                        if a == SELF:
                            src = hbm_self[m, rows, 2 * s + part, :]
                        else:
                            src = (hbm_ck if s else hbm_cq)[rows, m, part, :]
                        sp.dma_start(qk[HD * r:HD * r + HD, s, HG * g:HG * g + HG, :].bitcast(F32),
                                     src.rearrange("(h d) t -> d h t", d=HD)).then_inc(stack_in[a][g], 16)

            shares = slots_x.rearrange("g p t d -> (g p t) d").rearrange("(k p a) d -> k p a d", k=B, p=P)
            sp.wait_ge(consts, 8)

            def load(name, dst, src, b, ready):
                if ready is not None:
                    wait_alone(sp, *ready, consts_dma, 48)
                sp.dma_start(dst, src[b, :, :, :]).then_inc(in_sem[name], 16)

            def half(h, k):
                cur, nxt, prv = instances(h, k)
                last = cur or prv
                if cur:
                    stack(cur, prv, NG - 1)
                if h == FIRST:
                    if exists(k + 1):
                        load("x", raw[:, :, :], xT, k + 1, (lo_done["c"], upto("c", k - 1, 0)) if exists(k - 1) else None)
                    if exists(k):
                        load("xin", xin[:, :, :], x, k, (read["w0"], upto("w0", k - 1, 1)) if exists(k - 1) else None)
                elif exists(k):
                    load("c", raw[:, :, :], cT, k, (lo_done["x"], upto("x", k + 1 if exists(k + 1) else k, 0)))
                for s in range(STEPS):
                    for kind, n, b in tasks(h, s, k):
                        if kind in ("nm0", "nm1"):
                            mrows(int(kind[2]), b, n)
                    if h == FIRST and s == 3 and exists(k - 1):
                        sp.wait_ge(lo_done["ck"], upto("ck", k - 1, 1))
                        sp.dma_start(hbm_ck, stage[:, :, 2:4, :].bitcast(F32)).then_inc(ck_out, 16)
                        sp.wait_ge(lo_done["cq"], upto("cq", k - 1, 1))
                        sp.dma_start(hbm_cq, stage[:, :, 0:2, :].bitcast(F32)).then_inc(cq_out, 16)
                    if h == SECOND and s in (3, 5) and exists(k + 1):
                        m = (s - 3) // 2
                        sp.wait_ge(lo_done["k"], upto("k", k + 1, m))
                        sp.dma_start(hbm_self[m], stage[:, m, :, :].bitcast(F32)).then_inc(self_out[m], 16)
                    if h == FIRST and s == 10 and exists(k):
                        sp.dma_start(shares[k, :, :, :], zeros[:, :].unsqueeze(1).to_broadcast([P, CLEAR, D])) \
                            .then_inc(cleared, 16)
                    if h == FIRST and s == 13 and exists(k - 2):
                        wait_alone(sp, ln_done[CROSS], (k - 2) * TT + TT, consts_dma, 48)
                        sp.dma_start(x2[k - 2, :, :, :], res[:, :, :]).then_inc(x2_out, 16)
                    if nxt and s % TT == 0 and s:
                        stack(nxt, last, s // TT - 1)

            every_period(sp, half)
            sp.wait_ge(x2_out, B * 16)
            sp.wait_ge(cleared, B * 16)

        @block.gpsimd
        def _(pool):
            nc.gpsimd.memset(ident[:, :], 0.0).then_inc(consts, 1)
            pool.wait_ge(consts, 1)
            nc.gpsimd.affine_select(out=ident[:, :], in_=ident[:, :], compare_op=ALU.not_equal, fill=1.0,
                                    base=0, pattern=[[-1, P]], channel_multiplier=1).then_inc(consts, 1)
            nc.gpsimd.memset(mhalf[:, :, :], -0.5).then_inc(consts, 1)
            nc.gpsimd.memset(eps[:, :, :], EPS).then_inc(consts, 1)
            nc.gpsimd.memset(va[:, :, :, :, HD:2 * HD], 1.0).then_inc(consts, 1)
            nc.gpsimd.memset(zeros[:, :], 0.0).then_inc(consts, 1)
            nc.gpsimd.memset(qk[:, 1, :, :].bitcast(F32), 0.0).then_inc(consts, 1)
            pool.wait_ge(consts, 7)
            nc.gpsimd.memset(qk[96:P, 1, :, :].bitcast(F32), 1.0).then_inc(consts, 1)
            pool.wait_ge(consts, 8)
            pool.wait_ge(consts_dma, 48)

            def split_lo(kind, b, n, out, value, high):
                pool.wait_ge(hi_done[kind], upto(kind, b, n))
                nc.gpsimd.tensor_tensor(out, value, high.bitcast(F32), ALU.subtract).then_inc(lo_done[kind], 1)

            def half(h, k):
                for s in range(STEPS):
                    for kind, n, b in tasks(h, s, k):
                        if kind in ("q", "k"):
                            c = 0 if kind == "q" else 1
                            pool.wait_ge(read[kind], upto(kind, b, n))
                            nc.gpsimd.tensor_tensor(rot[:, c, :], rot[:, c, :], trig[:, 1, :], ALU.mult) \
                                .then_inc(sin_done[kind], 1)
                            pool.wait_ge(sin_done[kind], upto(kind, b, n))
                            nc.gpsimd.tensor_tensor(cosq[:, c, :], cosq[:, c, :], rot[:, c, :], ALU.add) \
                                .then_inc(roped[kind], 1)
                        if kind in ("qf", "kf"):
                            c = 0 if kind == "qf" else 1
                            split_lo(kind[0], b, n, stage[:, n, 2 * c + LO, :], cosq[:, c, :], stage[:, n, 2 * c, :])
                        if kind == "x":
                            split_lo("x", b, 0, xf[:, LO, :, :], raw[:, :, :], xf[:, HI, :, :])
                        if kind == "c":
                            split_lo("c", b, 0, cf[:, LO, :, :], raw[:, :, :], cf[:, HI, :, :])
                        if kind in ("w0", "w1"):
                            a, at = int(kind[1]), slice(2 * n, 2 * n + 2)
                            pool.wait_ge(mv_done[a], b * TT + 2 * n + 2)
                            nc.gpsimd.tensor_tensor(rstd[:, at, :], mv[:, at, 1:2], eps[:, at, :], ALU.add) \
                                .then_inc(var_done[a], 1)
                            pool.wait_ge(var_done[a], upto(kind, b, n))
                            nc.gpsimd.tensor_tensor(rstd[:, at, :], rstd[:, at, :], mhalf[:, at, :], ALU.pow) \
                                .then_inc(rstd_done[a], 1)
                        if kind == "x1b":
                            pool.wait_ge(ln_done[SELF], b * TT + TT)
                            wait_done(pool, read["w1"], "w1", b - 1, 1)
                            for t in range(TT):
                                nc.gpsimd.tensor_tensor(x1b[:, t, :], x1[:, t, :], bo[:, :], ALU.add) \
                                    .then_inc(x1b_done, 1)

            every_period(pool, half)

        @block.scalar
        def _(act):
            act.wait_ge(raw_w, 16)
            all_w = prob[:, :, :, :].rearrange("p a h t -> p (a h t)")
            nc.scalar.activation(w[:, HI, :, :].rearrange("p f n -> p (f n)"), all_w, ACT.Copy).then_inc(w_hi, 1)
            act.wait_ge(w_ready, 2)
            act.wait_ge(consts_dma, 48)

            def split_hi(kind, b, n, out, value, bias=None):
                if kind in job_done and kind not in ("q", "k"):
                    act.wait_ge(job_done[kind], upto(kind, b, n))
                if bias is None:
                    ins = nc.scalar.activation(out, value, ACT.Copy)
                else:
                    ins = nc.scalar.activation(out, value, ACT.Identity, bias=bias)
                ins.then_inc(hi_done[kind], 1)

            def mrow_wait(inst, g):
                a, b = inst
                act.wait_ge(mrow_in[a][g % 2], b * 64 + (g // 2) * 32 + 32)

            def head_outputs(inst, before, g):
                a, b = inst
                act.wait_ge(pv_done[a], b * STEPS + TT * g + TT)
                if before:
                    act.wait_ge(job_done[f"ot{before[0]}"], before[1] * TT + TT)
                nc.scalar.activation(ot[:, g, :], ps_out[:, :], ACT.Copy).then_inc(oev_done[a], 1)

            def task(kind, n, b, cur, prv):
                if kind in ("qf", "kf"):
                    act.wait_ge(roped[kind[0]], upto(kind[0], b, n))
                    if kind == "qf" and exists(b - 2):
                        act.wait_ge(cq_out, (b - 2) * 16 + 16)
                    if kind == "kf" and exists(b - 2):
                        act.wait_ge(ck_out, (b - 2) * 16 + 16)
                    c = 0 if kind == "qf" else 1
                    split_hi(kind[0], b, n, stage[:, n, 2 * c, :], cosq[:, c, :])
                if kind in ("v", "cv"):
                    a = SELF if kind == "v" else CROSS
                    if exists(b - 1):
                        act.wait_ge(pv_done[a], (b - 1) * STEPS + STEPS)
                    act.wait_ge(job_done[kind], upto(kind, b, n))
                    nc.scalar.activation(va[:, a, 2 * n:2 * n + 2, :, 0:HD],
                                         bank(kind, n).rearrange("p (t h d) -> p t h d", t=2, h=H),
                                         ACT.Copy).then_inc(read[kind], 1)
                if kind == "x":
                    act.wait_ge(in_sem["x"], b * 16 + 16)
                    wait_done(act, job_done["cq"], "cq", b - 2, 1)
                    split_hi("x", b, 0, xf[:, HI, :, :], raw[:, :, :])
                if kind == "c":
                    act.wait_ge(in_sem["c"], b * 16 + 16)
                    wait_done(act, job_done["w0"], "w0", b, 1)
                    split_hi("c", b, 0, cf[:, HI, :, :], raw[:, :, :])
                if kind == "ck":
                    act.wait_ge(self_out[n], (b + 1 if exists(b + 1) else b) * 16 + 16)
                    split_hi(kind, b, n, stage[:, n, 2, :], bank(kind, n), bcol[:, 1, n:n + 1])
                if kind == "cq":
                    act.wait_ge(self_out[n], (b + 1 if exists(b + 1) else b) * 16 + 16)
                    split_hi(kind, b, n, stage[:, n, 0, :], bank(kind, n), bcol[:, 0, n:n + 1])
                if kind == "nt1":
                    wait_done(act, job_done["cv"], "cv", b + 1, 1)
                    split_hi(kind, b, n, nf[:, HI, n, :], bank(kind, n), bcol[:, 2, n:n + 1])
                if kind == "nt0":
                    wait_done(act, job_done["w1"], "w1", b - 2, 1)
                    split_hi(kind, b, n, nf[:, HI, n, :], bank(kind, n))
                if kind == "xt":
                    wait_done(act, job_done["v"], "v", b + 1, 1)
                    split_hi(kind, b, n, xf[:, HI, n, :], bank(kind, n))
                if kind in ("nm0", "nm1"):
                    a = int(kind[2])
                    if n >= 2:
                        mrow_wait((a, b), n - 2)
                    elif n == 1 and prv:
                        mrow_wait(prv, 3)
                    elif n == 0 and (cur or prv):
                        mrow_wait(cur or prv, 2)
                    split_hi(kind, b, n, mst[:, n % 2, HI, :], bank(kind, n)[0:HG * TT, 0:P])

            def half(h, k):
                cur, nxt, prv = instances(h, k)
                older = instances(prv[0], prv[1] + prv[0])[2] if prv else None
                for s in range(STEPS):
                    for j in range(HG):
                        if j == ACT_AT:
                            for kind, n, b in tasks(h, s - 1, k):
                                task(kind, n, b, cur, prv)
                        if cur:
                            a, b = cur
                            act.wait_ge(st_done[a], b * NMAX + HG * s + j + 1)
                            if j == 0:
                                if s >= 2:
                                    act.wait_ge(pv_done[a], b * STEPS + s - 1)
                                elif prv:
                                    act.wait_ge(pv_done[prv[0]], prv[1] * STEPS + STEPS - 1 + s)
                            nc.scalar.activation(prob[:, s % 2, j, :], ps_sc[:, (HG * s + j) % 3, :],
                                                 ACT.Exp, scale=HD ** -0.5).then_inc(exp_done[a], 1)
                    if s == 0 and unfinished(h, k):
                        head_outputs(prv, older, NG - 1)
                    if cur and s % TT == 0 and s:
                        head_outputs(cur, prv, s // TT - 1)

            every_period(act, half)

        @block.vector
        def _(dve):
            nc.vector.memset(qk[:, 0, :, :].bitcast(F32), 0.0).then_inc(w_ready, 1)
            dve.wait_ge(w_hi, 1)
            all_w = prob[:, :, :, :].rearrange("p a h t -> p (a h t)")
            nc.vector.tensor_tensor(w[:, LO, :, :].rearrange("p f n -> p (f n)"), all_w,
                                    w[:, HI, :, :].rearrange("p f n -> p (f n)").bitcast(F32), ALU.subtract) \
                .then_inc(w_ready, 1)
            dve.wait_ge(consts_dma, 48)

            def split_lo(kind, b, n, out, high, bias=None, value=None):
                value = bank(kind, n) if value is None else value
                dve.wait_ge(hi_done[kind], upto(kind, b, n))
                if bias is None:
                    ins = nc.vector.tensor_tensor(out, value, high.bitcast(F32), ALU.subtract)
                else:
                    ins = nc.vector.scalar_tensor_tensor(out=out, in0=value, scalar=bias, in1=high.bitcast(F32),
                                                         op0=ALU.add, op1=ALU.subtract)
                ins.then_inc(read[kind], 1)

            def maximum(inst, before, n):
                (a, b), g, r = inst, n // (HG * TT), n % (HG * TT)
                dve.wait_ge(smax_done[a], b * NMAX + n + 1)
                if r == 0:
                    if g >= 2:
                        dve.wait_ge(job_done[f"nm{a}"], upto(f"nm{a}", b, g - 2))
                    elif before:
                        dve.wait_ge(job_done[f"nm{before[0]}"], upto(f"nm{before[0]}", before[1], g + 2))
                nc.vector.tensor_reduce(nm[:, g % 2, r:r + 1], ps_max[:, n % 2, :], axis=AX.X, op=ALU.max,
                                        negate=True).then_inc(max_done[a], 1)

            def task(kind, n, b):
                if kind in ("q", "k"):
                    c = 0 if kind == "q" else 1
                    if n:
                        dve.wait_ge(lo_done[kind], upto(kind, b, n - 1))
                    elif exists(b - 1):
                        dve.wait_ge(lo_done[kind], upto(kind, b - 1, 1))
                    if n == 0 and exists(b - 3):
                        dve.wait_ge(x2_out, (b - 3) * 16 + 16)
                    if n == 0 and exists(b - 2):
                        dve.wait_ge(ln_done[SELF], (b - 2) * TT + TT)
                    dve.wait_ge(job_done[kind], upto(kind, b, n))
                    nc.vector.tensor_tensor(cosq[:, c, :], bank(kind, n), trig[:, 0, :], ALU.mult)
                    nc.vector.stream_shuffle(rot[:, c, :], bank(kind, n), [p ^ 1 for p in range(32)]) \
                        .then_inc(read[kind], 1)
                if kind == "ck":
                    split_lo(kind, b, n, stage[:, n, 3, :], stage[:, n, 2, :], bcol[:, 1, n:n + 1])
                if kind == "cq":
                    split_lo(kind, b, n, stage[:, n, 1, :], stage[:, n, 0, :], bcol[:, 0, n:n + 1])
                if kind == "nt0":
                    split_lo(kind, b, n, nf[:, LO, n, :], nf[:, HI, n, :])
                if kind == "nt1":
                    split_lo(kind, b, n, nf[:, LO, n, :], nf[:, HI, n, :], bcol[:, 2, n:n + 1])
                if kind == "xt":
                    split_lo(kind, b, n, xf[:, LO, n, :], xf[:, HI, n, :])
                if kind in ("nm0", "nm1"):
                    split_lo(kind, b, n, mst[:, n % 2, LO, :], mst[:, n % 2, HI, :],
                             value=bank(kind, n)[0:HG * TT, 0:P])
                if kind in ("ot0", "ot1"):
                    a = int(kind[2])
                    heads = bank(kind, n).rearrange("p (h e) -> p h e", h=H)
                    if n == 0:
                        wait_done(dve, job_done["nt1"] if a == SELF else job_done["nt0"],
                                  "nt1" if a == SELF else "nt0", b - 2 if a == SELF else
                                  (b + 1 if exists(b + 1) else b), 1)
                    dve.wait_ge(job_done[kind], upto(kind, b, n))
                    nc.vector.reciprocal(rden[:, n, :], heads[:, :, HD]).then_inc(rden_done[a], 1)
                    dve.wait_ge(rden_done[a], upto(kind, b, n))
                    nc.vector.tensor_tensor(on[:, n, :].rearrange("p (h d) -> p h d", h=H), heads[:, :, 0:HD],
                                            rden[:, n, :].unsqueeze(2).to_broadcast([P, H, HD]), ALU.mult) \
                        .then_inc(read[kind], 1)
                if kind in ("w0", "w1"):
                    a, at = int(kind[1]), slice(2 * n, 2 * n + 2)
                    if a == SELF:
                        dve.wait_ge(in_sem["xin"], b * 16 + 16)
                        wait_done(dve, roped["k"], "k", b + 1, 1)
                        if not exists(b + 1) and n == 0 and exists(b - 2):
                            dve.wait_ge(x2_out, (b - 2) * 16 + 16)
                    else:
                        dve.wait_ge(x1b_done, b * TT + 2 * n + 2)
                        if n == 0:
                            dve.wait_ge(ln_done[SELF], (b + 1 if exists(b + 1) else b) * TT + TT)
                        if n == 0 and not exists(b + 1) and exists(b - 1):
                            dve.wait_ge(x2_out, (b - 1) * 16 + 16)
                    dve.wait_ge(job_done[kind], upto(kind, b, n))
                    nc.vector.tensor_tensor(res[:, at, :], bank(kind, n).rearrange("p (t n) -> p t n", t=2),
                                            (x1b if a else xin)[:, at, :], ALU.add).then_inc(read[kind], 1)
                    dve.wait_ge(read[kind], upto(kind, b, n))
                    for t in (2 * n, 2 * n + 1):
                        nc.vector.bn_stats(st6[:, t, :], res[:, t, :]).then_inc(stat_done[a], 1)
                    for t in (2 * n, 2 * n + 1):
                        wait_alone(dve, stat_done[a], b * TT + t + 1, w_hi, 1)
                        nc.vector.bn_aggr(mv[:, t, :], st6[:, t, :]).then_inc(mv_done[a], 1)
                if kind in ("ln0", "ln1"):
                    a = int(kind[2])
                    if a == SELF:
                        wait_done(dve, job_done["xt"], "xt", b - 1, 1)
                        if exists(b - 1):
                            dve.wait_ge(x1b_done, (b - 1) * TT + TT)
                    for t in range(TT):
                        dve.wait_ge(rstd_done[a], b * 2 + t // 2 + 1)
                        nc.vector.tensor_scalar((res if a else x1)[:, t, :], res[:, t, :], mv[:, t, 0:1],
                                                rstd[:, t, :], ALU.subtract, ALU.mult).then_inc(ln_done[a], 1)

            def half(h, k):
                cur, nxt, prv = instances(h, k)
                for s in range(STEPS):
                    turn = maxima_of(s, cur, nxt)
                    for j in range(HG):
                        if j == DVE_AT:
                            for kind, n, b in tasks(h, s - 1, k):
                                task(kind, n, b)
                        if turn:
                            inst, n = turn[j]
                            maximum(inst, prv if inst is cur else cur or prv, n)

            every_period(dve, half)

        @block.tensor
        def _(pe):
            pe.wait_ge(w_ready, 2)
            pe.wait_ge(consts, 8)

            def products(out, pairs):
                parts = [(a, b) for a, b in ((HI, HI), (HI, LO), (LO, HI))]
                for n, (l, r) in enumerate(pairs):
                    for k, (a, b) in enumerate(parts):
                        ins = nc.tensor.matmul(out, l(a), r(b), start=(n == 0 and k == 0),
                                               stop=(n == len(pairs) - 1 and k == len(parts) - 1))
                return ins

            def free_bank(kind, n, k):
                at = [t[:2] for t in ORDER].index((kind, n)) - 2
                while True:
                    prev, m, off = ORDER[at % len(ORDER)]
                    b = k + off if at >= 0 else k - 1 + off
                    if exists(b):
                        break
                    at -= 2
                    if at < -len(ORDER):
                        return
                pe.wait_ge(read[prev], upto(prev, b, m))

            def by_feature(kind, n, src):
                c = WCOL[kind] + P * n
                return products(bank(kind, n), [(lambda a, f=f: w[:, a, f, c:c + P], lambda b, f=f: src[:, b, f, :])
                                                for f in range(FC)])

            def by_token(kind, n, src):
                c = WCOL[kind]
                for part in range(2):
                    t = P * (2 * n + part)
                    ins = products(bank(kind, n)[:, D * part:D * part + D],
                                   [(lambda a, f=f: src[:, a, f, t:t + P], lambda b, f=f: w[:, b, f, c:c + D])
                                    for f in range(FC)])
                return ins

            def turn(kind, n, src):
                for t in range(TT):
                    ins = nc.tensor.transpose(bank(kind, n)[:, P * t:P * t + P], src[:, t, P * n:P * n + P], ident[:, :])
                return ins

            def job(kind, n, b, k):
                free_bank(kind, n, k)
                if kind in ("q", "k", "v"):
                    pe.wait_ge(lo_done["x"], upto("x", b, 0))
                    ins = (by_token if kind == "v" else by_feature)(kind, n, xf)
                elif kind in ("ck", "cv"):
                    pe.wait_ge(lo_done["c"], upto("c", b, 0))
                    ins = (by_token if kind == "cv" else by_feature)(kind, n, cf)
                elif kind == "cq":
                    pe.wait_ge(lo_done["xt"], upto("xt", b, 1))
                    ins = by_feature(kind, n, xf)
                elif kind in ("ot0", "ot1"):
                    pe.wait_ge(oev_done[int(kind[2])], b * NG + NG)
                    for g in range(NG):
                        ins = nc.tensor.transpose(bank(kind, n)[:, P * g:P * g + P], ot[:, g, P * n:P * n + P], ident[:, :])
                elif kind in ("nt0", "nt1"):
                    a = kind[2]
                    pe.wait_ge(read[f"ot{a}"], upto(f"ot{a}", b, TT - 1))
                    ins = turn(kind, n, on)
                elif kind in ("w0", "w1"):
                    a = kind[1]
                    pe.wait_ge(lo_done[f"nt{a}"], upto(f"nt{a}", b, 1))
                    ins = by_token(kind, n, nf)
                elif kind == "xt":
                    pe.wait_ge(ln_done[SELF], b * TT + TT)
                    ins = turn(kind, n, x1)
                else:
                    a = int(kind[2])
                    pe.wait_ge(max_done[a], b * NMAX + (n + 1) * HG * TT)
                    ins = nc.tensor.transpose(bank(kind, n)[0:HG * TT, 0:P], nm[:, n % 2, :], ident[:, :])
                ins.then_inc(job_done[kind], 1)

            def scores_max(inst, before, n):
                (a, b), h, c = inst, n // TT, n % TT
                if n % (HG * TT) == 0:
                    pe.wait_ge(stack_in[a][h // HG], b * 96 + 96)
                if n >= 2:
                    pe.wait_ge(max_done[a], b * NMAX + n - 1)
                elif before:
                    pe.wait_ge(max_done[before[0]], before[1] * NMAX + NMAX - 1 + n)
                nc.tensor.matmul(ps_max[:, n % 2, :], qk[0:96, 0, h, P * c:P * c + P], qk[0:96, 1, h, :],
                                 start=True, stop=True).then_inc(smax_done[a], 1)

            def scores(inst, before, s, j):
                (a, b), g, c = inst, s // TT, s % TT
                h, n = HG * g + j, HG * s + j
                if n >= 3:
                    pe.wait_ge(exp_done[a], b * NMAX + n - 2)
                elif before:
                    pe.wait_ge(exp_done[before[0]], before[1] * NMAX + NMAX)
                if c == 0 and j == 0:
                    pe.wait_ge(mrow_in[a][g % 2], b * 64 + (g // 2) * 32 + 32)
                nc.tensor.matmul(ps_sc[:, n % 3, :], qk[:, 1, h, P * c:P * c + P], qk[:, 0, h, :],
                                 start=True, stop=True).then_inc(st_done[a], 1)

            def head_outputs(inst, before, s):
                (a, b), g, c = inst, s // TT, s % TT
                pe.wait_ge(exp_done[a], b * NMAX + HG * s + HG)
                if s == 0:
                    v = "cv" if a else "v"
                    pe.wait_ge(read[v], upto(v, b, 1))
                if c == 0:
                    if g:
                        pe.wait_ge(oev_done[a], b * NG + g)
                    elif before:
                        pe.wait_ge(oev_done[before[0]], before[1] * NG + NG)
                for j in range(HG):
                    ins = nc.tensor.matmul(ps_out[32 * j:32 * j + 32, :], va[:, a, c, HG * g + j, :],
                                           prob[:, s % 2, j, :], start=(c == 0), stop=(c == TT - 1),
                                           tile_position=(0, 32 * j))
                ins.then_inc(pv_done[a], 1)

            def half(h, k):
                cur, nxt, prv = instances(h, k)
                for s in range(STEPS):
                    ahead = [(inst, prv if inst is cur else cur or prv, n) for inst, n in maxima_of(s, cur, nxt)]
                    for j in range(HG):
                        if j == PV_AT:
                            if s == 0 and unfinished(h, k):
                                head_outputs(prv, None, STEPS - 1)
                            if s and cur:
                                head_outputs(cur, prv, s - 1)
                        if cur:
                            scores(cur, prv, s, j)
                        if ahead:
                            scores_max(*ahead[j])
                        if j == JOB_AT:
                            for kind, n, b in tasks(h, s, k):
                                if kind in job_done:
                                    job(kind, n, b, k)

            every_period(pe, half)



NE = 8
NSHARED = 2
EXPERTS = list(range(NE, NE + NSHARED)) + list(range(NE))
NX = len(EXPERTS)
I = 256
IC = I // P
CAP = -(-5 * B * T * 2 // (4 * NE))
PLACES = NE * CAP
CH = 256
CT = CH // P
NCH = CAP // CH
CHUNKS = NE * NCH
CLEAR = PLACES // (B * P)
assert CAP % CH == 0 and NE % 2 == 0 and NCH >= 4
BF16 = mybir.dt.bfloat16
U32 = mybir.dt.uint32
ROUTE_STEPS = 29
SELECTED = 16
META_W, META_P = TT * D, TT * D + 2 * TT
META = META_P + 2 * TT
AHEAD = 3


def moe_phase(nc, x2, slots_x, slots_y, meta, w_moe, w_gate, index, out):
    with ExitStack() as ctx:
        def sb(name, shape, dt=F32):
            return ctx.enter_context(nc.sbuf_tensor(name, shape, dt))

        def sem(name):
            return ctx.enter_context(nc.semaphore(name))

        w = sb("we", [P, 4, 2, 3, FC, I], F32R)
        wraw = sb("weraw", [P, 2, 3, FC, I])
        wg = sb("wg", [P, 2, FC, NE], F32R)
        wgraw = sb("wgraw", [P, FC, NE])
        ident = sb("ident2", [P, P])
        before = sb("before", [P, P], BF16)
        ones = sb("ones", [P, P], BF16)
        idx = sb("idx", [P, 2, TT, NE])
        mhalf = sb("mhalf2", [P, TT, 1])
        eps = sb("eps2", [P, TT, 1])
        xin = sb("x2in", [P, 2, TT, D])
        xf = sb("x2f", [P, 2, 2, FC, T], F32R)
        sg = sb("sg", [P, 2, T])
        h = sb("h", [P, 2, T])
        hf = sb("hf", [P, 2, 2, IC, T], F32R)
        ym = sb("ym", [P, 2, META])
        st6 = sb("st62", [P, TT, 6])
        mv = sb("mv2", [P, TT, 2])
        rstd = sb("rstd2", [P, TT, 1])
        r4 = sb("r4", [P, 8, TT, 1])
        r32 = sb("r32", [P, 9, TT, NE])
        choice = sb("choice", [P, 2, TT, NE])
        full = sb("full", [P, 3, TT, NE])
        prod = sb("prod", [P, 2, 3, TT, NE])
        res6 = sb("res6", [P, 2, 3, TT])
        scat = sb("scat", [P, 2, 2, TT], U32)
        sel = sb("sel", [P, TT + 1, NE], BF16)
        carry = sb("carry", [P, 1, NE])
        xs = sb("xs", [P, 2, CT, D])
        ys = sb("ys", [P, 2, CT, D])
        places = sb("places", [P, 2, 2 * TT], U32)
        gath = sb("gath", [P, 2, 2 * TT, D])
        yo = sb("yo", [P, 2, TT, D])

        ps_gu = ctx.enter_context(nc.psum_tensor("ps_gu", [P, 4, T], F32))
        ps_dn = ctx.enter_context(nc.psum_tensor("ps_dn", [P, 2, T], F32))
        ps_t = ctx.enter_context(nc.psum_tensor("ps_t", [P, 2, T], F32))
        logits = ps_t[:, 1, 0:TT * NE].rearrange("p (t e) -> p t e", t=TT)
        counts = ps_t[:, 1, P:P + (TT + 1) * NE].rearrange("p (t e) -> p t e", e=NE)

        w_in = [sem("w_in0"), sem("w_in1")]
        wg_in, idx_in = sem("wg_in"), sem("idx_in")
        w_hi, w_lo, consts, ready = sem("we_hi"), sem("we_lo"), sem("consts2"), sem("ready")
        x_in = [sem("x2_in0"), sem("x2_in1")]
        xt_done, xhi_done, xlo_done = sem("xt2_done"), sem("xhi_done"), sem("xlo_done")
        logits_done, shift_done, exp_done, step_done, cnt_done = (
            sem("logits_done"), sem("shift_done"), sem("rexp_done"), sem("step_done"), sem("cnt_done"))
        gu_done, silu_done, h_done, hhi_done, hlo_done = (
            sem("gu_done"), sem("silu_done"), sem("h_done"), sem("hhi_done"), sem("hlo_done"))
        dn_done, acc_done = sem("dn_done"), sem("acc_done")
        meta_out = [sem("meta_out0"), sem("meta_out1")]
        scattered = [sem("scattered0"), sem("scattered1")]
        xs_in = [sem("xs_in0"), sem("xs_in1")]
        ct_done, chi_done, clo_done = sem("ct_done"), sem("chi_done"), sem("clo_done")
        cgu_done, csilu_done, ch_done, chhi_done, chlo_done = (
            sem("cgu_done"), sem("csilu_done"), sem("ch_done"), sem("chhi_done"), sem("chlo_done"))
        cdn_done, cy_done = sem("cdn_done"), sem("cy_done")
        ys_out = [sem("ys_out0"), sem("ys_out1")]
        ym_in = [sem("ym_in0"), sem("ym_in1")]
        places_in = [sem("places_in0"), sem("places_in1")]
        gathered = [sem("gathered0"), sem("gathered1")]
        sum_done, stat_done, mv_done, var_done, rstd_done, norm_done = (
            sem("sum_done"), sem("stat2"), sem("mv_done2"), sem("var2"), sem("rstd2d"), sem("norm_done"))
        out_done = [sem("out_done0"), sem("out_done1")]
        GU, HN, DN, ACC = 4 * NSHARED, IC * NSHARED, 2 * NSHARED, TT * NSHARED

        block = ctx.enter_context(nc.Block())

        def after(eng, s, value):
            if not (isinstance(value, int) and value <= 0):
                eng.wait_ge(s, value)

        def by_pairs(eng, count, body, unit=1):
            def pair(k):
                for j in range(2 * unit):
                    body(k, j)

            pair(0)
            with eng.Fori(1, count // (2 * unit) - 1) as k:
                pair(k)
            pair(count // (2 * unit) - 1)

        def chunk_of(kk, j):
            return 2 * NCH * kk + j

        def is_chunk(g):
            return not isinstance(g, int) or 0 <= g < CHUNKS

        def is_block(i):
            return not isinstance(i, int) or 0 <= i < B

        def split_next(kk, j):
            e, c = 2 * kk + j // NCH, j % NCH
            if c != 2 or (isinstance(e, int) and not 1 <= e < NE - 1):
                return None
            n = e + 1 + NSHARED
            par = (j // NCH + 1) % 2
            return n, par, (kk + 1 if par else kk + 2) + 1

        @block.sync
        def _(sp):
            def load_block(i, q):
                sp.dma_start(xin[:, q, :, :], x2[i, :, :, :]).then_inc(x_in[q], 16)

            def load_weights(n, expert):
                sp.dma_start(wraw[:, n % 2, :, :, :], w_moe[expert]).then_inc(w_in[n % 2], 16)

            sp.dma_start(wgraw[:, :, :], w_gate).then_inc(wg_in, 16)
            load_block(0, 0)
            load_weights(0, EXPERTS[0])
            sp.dma_start(idx[:, :, :, :], index).then_inc(idx_in, 16)
            load_block(1, 1)
            load_weights(1, EXPERTS[1])
            for n in range(2, 4):
                sp.wait_ge(w_lo, n - 1)
                load_weights(n, EXPERTS[n])

            def tokens(k, q):
                i = 2 * k + q
                wait_alone(sp, acc_done, i * ACC + ACC, idx_in, 16)
                sp.dma_start(meta[i, :, :], ym[:, q, :]).then_inc(meta_out[q], 16)
                if is_block(i + 2):
                    wait_alone(sp, scattered[q], 16 * 2 * TT * (k + 1), idx_in, 16)
                    load_block(i + 2, q)
                if isinstance(k, int) and k == 0:
                    sp.wait_ge(w_lo, 3 + q)
                    load_weights(4 + q, EXPERTS[4 + q])

            by_pairs(sp, B, tokens)

            def load_kept(i, q):
                sp.dma_start(ym[:, q, 0:META_P], meta[i, :, 0:META_P]).then_inc(ym_in[q], 16)

            def load_places(i, q):
                sp.dma_start(places[:, q, :].bitcast(F32), meta[i, :, META_P:META]).then_inc(places_in[q], 16)

            def load_chunk(g, p):
                sp.dma_start(xs[:, p, :, :], slots_x[g]).then_inc(xs_in[p], 16)

            for q in range(2):
                sp.wait_ge(meta_out[q], 16 * (B // 2))
                sp.wait_ge(scattered[q], 16 * 2 * TT * (B // 2))
            load_chunk(0, 0)
            load_chunk(1, 1)
            for q in range(2):
                load_places(q, q)
                load_kept(q, q)

            def chunk(kk, j):
                g = chunk_of(kk, j)
                if is_chunk(g + 2):
                    wait_alone(sp, ct_done, g + 1, idx_in, 16)
                    load_chunk(g + 2, j % 2)
                e = 2 * kk + j // NCH
                if j % NCH == 3 and (not isinstance(e, int) or 1 <= e < NE - 3):
                    wait_alone(sp, w_lo, e + 2 + NSHARED, idx_in, 16)
                    load_weights((j // NCH + 3) % 2, e + 3)

            by_pairs(sp, CHUNKS, chunk, NCH)

            def results(k, q):
                i = 2 * k + q
                if is_block(i + 2):
                    wait_alone(sp, gathered[q], 16 * 2 * TT * (k + 1), idx_in, 16)
                    load_places(i + 2, q)
                wait_alone(sp, norm_done, i * TT + TT, idx_in, 16)
                sp.dma_start(out[i, :, :, :], yo[:, q, :, :]).then_inc(out_done[q], 16)
                if is_block(i + 2):
                    load_kept(i + 2, q)

            by_pairs(sp, B, results)
            for q in range(2):
                sp.wait_ge(out_done[q], 16 * (B // 2))

        @block.gpsimd
        def _(pool):
            nc.gpsimd.memset(ident[:, :], 0.0).then_inc(consts, 1)
            nc.gpsimd.memset(before[:, :], 1.0).then_inc(consts, 1)
            nc.gpsimd.memset(ones[:, :], 1.0).then_inc(consts, 1)
            nc.gpsimd.memset(mhalf[:, :, :], -0.5).then_inc(consts, 1)
            nc.gpsimd.memset(eps[:, :, :], EPS).then_inc(consts, 1)
            pool.wait_ge(consts, 5)
            nc.gpsimd.affine_select(out=ident[:, :], in_=ident[:, :], compare_op=ALU.not_equal, fill=1.0,
                                    base=0, pattern=[[-1, P]], channel_multiplier=1).then_inc(consts, 1)
            nc.gpsimd.affine_select(out=before[:, :], in_=before[:, :], compare_op=ALU.is_gt, fill=0.0,
                                    base=0, pattern=[[1, P]], channel_multiplier=-1).then_inc(consts, 1)
            pool.wait_ge(consts, 7)

            rows_x = slots_x.rearrange("g p t d -> (g p t) d")
            rows_y = slots_y.rearrange("g p t d -> (g p t) d")

            def scatter(k, q):
                i = 2 * k + q
                wait_alone(pool, step_done, i * ROUTE_STEPS + ROUTE_STEPS, consts, 7)
                for t in range(TT):
                    for c in range(2):
                        nc.gpsimd.indirect_dma_start(
                            rows_x, bass.IndirectOffsetOnAxis(ap=scat[:, q, c, t:t + 1], axis=0), xin[:, q, t, :],
                            None, bounds_check=PLACES - 1, oob_is_err=False).then_inc(scattered[q], 16)

            by_pairs(pool, B, scatter)

            def gather(k, q, tiles):
                i = 2 * k + q
                if tiles[0] == 0:
                    wait_alone(pool, places_in[q], 16 * (k + 1), consts, 7)
                    if is_block(i - 2):
                        wait_alone(pool, sum_done, (i - 1) * 2 * TT, consts, 7)
                for t in tiles:
                    for c in range(2):
                        at = TT * c + t
                        nc.gpsimd.indirect_dma_start(
                            gath[:, q, 2 * t + c, :], None, rows_y,
                            bass.IndirectOffsetOnAxis(ap=places[:, q, at:at + 1], axis=0),
                            bounds_check=PLACES - 1, oob_is_err=False).then_inc(gathered[q], 16)

            for q in range(2):
                pool.wait_ge(ys_out[q], 16 * (CHUNKS // 2))

            def norm(k, q):
                i = 2 * k + q
                if is_block(i + 1):
                    gather(k + q, 1 - q, range(AHEAD))
                pool.wait_ge(mv_done, i * TT + TT)
                nc.gpsimd.tensor_tensor(rstd[:, :, :], mv[:, :, 1:2], eps[:, :, :], ALU.add).then_inc(var_done, 1)
                pool.wait_ge(var_done, i + 1)
                nc.gpsimd.tensor_tensor(rstd[:, :, :], rstd[:, :, :], mhalf[:, :, :], ALU.pow).then_inc(rstd_done, 1)
                if is_block(i + 1):
                    gather(k + q, 1 - q, range(AHEAD, TT))

            gather(0, 0, range(TT))
            by_pairs(pool, B, norm)

        @block.scalar
        def _(act):
            act.wait_ge(wg_in, 16)
            nc.scalar.activation(wg[:, HI, :, :], wgraw[:, :, :], ACT.Copy).then_inc(w_hi, 1)

            def split_hi(at, par, loaded):
                act.wait_ge(w_in[par], 16 * loaded)
                nc.scalar.activation(w[:, at, HI, :, :, :].rearrange("p a f i -> p (a f i)"),
                                     wraw[:, par, :, :, :].rearrange("p a f i -> p (a f i)"),
                                     ACT.Copy).then_inc(w_hi, 1)

            def x_hi(i, q, f):
                act.wait_ge(xt_done, i * FC + f + 1)
                if f == 0 and is_block(i - 2):
                    act.wait_ge(gu_done, (i - 1) * GU)
                nc.scalar.activation(xf[:, q, HI, f, :], ps_t[:, 0, :], ACT.Copy).then_inc(xhi_done, 1)

            for f in range(FC):
                x_hi(0, 0, f)
            for n in range(NSHARED):
                split_hi(n, n, 1)

            def tokens(k, q):
                i = 2 * k + q
                act.wait_ge(shift_done, i + 1)
                nc.scalar.activation(r32[:, 1, :, :], r32[:, 0, :, :], ACT.Exp).then_inc(exp_done, 1)
                for n in range(NSHARED):
                    for c in range(IC):
                        act.wait_ge(gu_done, i * GU + 4 * n + 2 * c + 1)
                        after(act, h_done, i * HN + IC * (n - 1) + c + 1)
                        nc.scalar.activation(sg[:, c, :], ps_gu[:, 2 * c, :], ACT.Silu).then_inc(silu_done, 1)
                    for c in range(IC):
                        act.wait_ge(h_done, i * HN + IC * n + c + 1)
                        if c == 0:
                            after(act, dn_done, i * DN + 2 * (n - 1))
                        nc.scalar.activation(hf[:, n % 2, HI, c, :], h[:, c, :], ACT.Copy).then_inc(hhi_done, 1)
                if is_block(i + 1):
                    for f in range(FC):
                        x_hi(i + 1, 1 - q, f)
                if isinstance(k, int) and k == 0:
                    split_hi(2 + q, q, 2)

            by_pairs(act, B, tokens)

            def chunk_hi(g, p):
                act.wait_ge(ct_done, g + 1)
                if is_chunk(g - 2):
                    act.wait_ge(cgu_done, 2 * (g - 1))
                else:
                    act.wait_ge(gu_done, B * GU)
                nc.scalar.activation(xf[:, p, HI, :, 0:CH], ps_t[:, p, :].rearrange("p (f t) -> p f t", f=FC),
                                     ACT.Copy).then_inc(chi_done, 1)

            def store(g, p):
                wait_alone(act, cy_done, g + 1, wg_in, 16)
                act.dma_start(slots_y[g], ys[:, p, :, :]).then_inc(ys_out[p], 16)

            def chunk(kk, j):
                g, p = chunk_of(kk, j), j % 2
                if is_chunk(g - 2):
                    act.wait_ge(cdn_done, g - 1)
                    if is_chunk(g - 4):
                        act.wait_ge(ys_out[p], 16 * (NCH * kk + j // 2 - 1))
                    nc.scalar.activation(ys[:, p, :, :], ps_dn[:, p, :].rearrange("p (t d) -> p t d", t=CT),
                                         ACT.Copy).then_inc(cy_done, 1)
                if is_chunk(g + 1):
                    chunk_hi(g + 1, 1 - p)
                if is_chunk(g - 2):
                    store(g - 2, p)
                act.wait_ge(cgu_done, 2 * g + 1)
                if is_chunk(g - 2):
                    act.wait_ge(ch_done, g - 1)
                else:
                    act.wait_ge(h_done, B * HN)
                nc.scalar.activation(sg[:, p, :], ps_gu[:, 2 * p, :], ACT.Silu).then_inc(csilu_done, 1)
                act.wait_ge(ch_done, g + 1)
                if is_chunk(g - 2):
                    act.wait_ge(cdn_done, g - 1)
                else:
                    act.wait_ge(dn_done, B * DN)
                nc.scalar.activation(hf[:, p, HI, :, 0:CH], h[:, p, :].rearrange("p (c t) -> p c t", c=IC),
                                     ACT.Copy).then_inc(chhi_done, 1)
                nxt = split_next(kk, j)
                if nxt:
                    n, par, loaded = nxt
                    act.wait_ge(cdn_done, g - 2)
                    split_hi(2 + par, par, loaded)

            chunk_hi(0, 0)
            by_pairs(act, CHUNKS, chunk, NCH)
            for g in (CHUNKS - 2, CHUNKS - 1):
                act.wait_ge(cdn_done, g + 1)
                act.wait_ge(ys_out[g % 2], 16 * (g // 2))
                nc.scalar.activation(ys[:, g % 2, :, :], ps_dn[:, g % 2, :].rearrange("p (t d) -> p t d", t=CT),
                                     ACT.Copy).then_inc(cy_done, 1)
                store(g, g % 2)

        @block.vector
        def _(dve):
            nc.vector.memset(sel[:, TT, :], 0.0)
            nc.vector.memset(carry[:, :, :], 0.0).then_inc(ready, 1)
            dve.wait_ge(w_hi, 1)
            nc.vector.tensor_tensor(wg[:, LO, :, :], wgraw[:, :, :], wg[:, HI, :, :].bitcast(F32), ALU.subtract) \
                .then_inc(ready, 1)

            def split_lo(at, par, n):
                dve.wait_ge(w_hi, n + 2)
                nc.vector.tensor_tensor(w[:, at, LO, :, :, :].rearrange("p a f i -> p (a f i)"),
                                        wraw[:, par, :, :, :].rearrange("p a f i -> p (a f i)"),
                                        w[:, at, HI, :, :, :].rearrange("p a f i -> p (a f i)").bitcast(F32),
                                        ALU.subtract).then_inc(w_lo, 1)

            def x_lo(i, q, f):
                dve.wait_ge(xhi_done, i * FC + f + 1)
                nc.vector.tensor_tensor(xf[:, q, LO, f, :], ps_t[:, 0, :], xf[:, q, HI, f, :].bitcast(F32),
                                        ALU.subtract).then_inc(xlo_done, 1)

            for f in range(FC):
                x_lo(0, 0, f)
            for n in range(NSHARED):
                split_lo(n, n, n)
            dve.wait_ge(ready, 2)
            dve.wait_ge(idx_in, 16)

            v = nc.vector
            mx, total, inv, top1, j1, top2, j2, den = (r4[:, k, :, :] for k in range(8))
            shifted, e, s, eq, cand, rest, pos, keep, weight = (r32[:, k, :, :] for k in range(9))
            one, two = (choice[:, c, :, :] for c in range(2))
            number, first_place = (idx[:, c, :, :] for c in range(2))

            def wide(a):
                return a.to_broadcast([P, TT, NE])

            def make_step(i, done):
                def step(ins):
                    done[0] += 1
                    ins.then_inc(step_done, 1)
                    dve.wait_ge(step_done, i * ROUTE_STEPS + done[0])
                return step

            def choose(i):
                done = [0]
                step = make_step(i, done)
                dve.wait_ge(logits_done, i + 1)
                step(v.tensor_reduce(mx, logits, axis=AX.X, op=ALU.max))
                v.tensor_tensor(shifted, logits, wide(mx), ALU.subtract).then_inc(shift_done, 1)
                dve.wait_ge(exp_done, i + 1)
                step(v.tensor_reduce(total, e, axis=AX.X, op=ALU.add))
                step(v.reciprocal(inv, total))
                step(v.tensor_tensor(s, e, wide(inv), ALU.mult))
                step(v.tensor_reduce(top1, s, axis=AX.X, op=ALU.max))
                step(v.tensor_tensor(eq, s, wide(top1), ALU.is_equal))
                step(v.tensor_tensor(cand, eq, number, ALU.mult))
                step(v.tensor_reduce(j1, cand, axis=AX.X, op=ALU.min))
                step(v.tensor_tensor(one, number, wide(j1), ALU.is_equal))
                step(v.scalar_tensor_tensor(out=rest, in0=one, scalar=-2.0, in1=s, op0=ALU.mult, op1=ALU.add))
                step(v.tensor_reduce(top2, rest, axis=AX.X, op=ALU.max))
                step(v.tensor_tensor(eq, rest, wide(top2), ALU.is_equal))
                step(v.tensor_tensor(cand, eq, number, ALU.mult))
                step(v.tensor_reduce(j2, cand, axis=AX.X, op=ALU.min))
                step(v.tensor_tensor(two, number, wide(j2), ALU.is_equal))
                step(v.tensor_tensor(sel[:, 0:TT, :], one, two, ALU.add))
                assert done[0] == SELECTED, done
                step(v.scalar_tensor_tensor(out=den, in0=top1, scalar=1e-20, in1=top2, op0=ALU.add, op1=ALU.add))
                step(v.reciprocal(inv, den))
                step(v.tensor_tensor(weight, s, wide(inv), ALU.mult))
                return done

            def place(i, k, q, done):
                step = make_step(i, done)
                dve.wait_ge(cnt_done, i + 1)
                step(v.tensor_tensor(pos, counts[:, 0:TT, :], carry[:, :, :].to_broadcast([P, TT, NE]), ALU.add))
                v.tensor_tensor(carry[:, :, :], carry[:, :, :], counts[:, TT:TT + 1, :], ALU.add).then_inc(ready, 1)
                step(v.scalar_tensor_tensor(out=full[:, 0, :, :], in0=pos, scalar=float(CAP), in1=weight,
                                            op0=ALU.is_lt, op1=ALU.mult))
                step(v.scalar_tensor_tensor(out=full[:, 1, :, :], in0=pos, scalar=float(CAP - 1), in1=first_place,
                                            op0=ALU.min, op1=ALU.add))
                step(v.tensor_scalar(keep, pos, float(CAP), float(PLACES), ALU.is_ge, ALU.mult))
                step(v.tensor_tensor(full[:, 2, :, :], full[:, 1, :, :], keep, ALU.add))
                step(v.tensor_tensor(prod[:, :, :, :, :].rearrange("p c k t e -> p c k (t e)"),
                                     choice[:, :, :, :].rearrange("p c t e -> p c (t e)").unsqueeze(2)
                                     .to_broadcast([P, 2, 3, TT * NE]),
                                     full[:, :, :, :].rearrange("p k t e -> p k (t e)").unsqueeze(1)
                                     .to_broadcast([P, 2, 3, TT * NE]), ALU.mult))
                step(v.tensor_reduce(res6[:, :, :, :].rearrange("p c k t -> p (c k t)"),
                                     prod[:, :, :, :, :].rearrange("p c k t e -> p (c k t) e"), axis=AX.X, op=ALU.add))
                if is_block(i - 2):
                    dve.wait_ge(meta_out[q], 16 * k)
                    dve.wait_ge(scattered[q], 16 * 2 * TT * k)
                step(v.tensor_copy(ym[:, q, META_W:META_P].rearrange("p (c t) -> p c t", c=2), res6[:, :, 0, :]))
                step(v.tensor_copy(ym[:, q, META_P:META].rearrange("p (c t) -> p c t", c=2).bitcast(U32),
                                   res6[:, :, 1, :]))
                step(v.tensor_copy(scat[:, q, :, :], res6[:, :, 2, :]))
                assert done[0] == ROUTE_STEPS, done

            def product(i, n):
                for c in range(IC):
                    dve.wait_ge(silu_done, i * HN + IC * n + c + 1)
                    dve.wait_ge(gu_done, i * GU + 4 * n + 2 * c + 2)
                    after(dve, hlo_done, i * HN + IC * (n - 1) + c + 1)
                    nc.vector.tensor_tensor(h[:, c, :], ps_gu[:, 2 * c + 1, :], sg[:, c, :], ALU.mult) \
                        .then_inc(h_done, 1)
                for c in range(IC):
                    dve.wait_ge(hhi_done, i * HN + IC * n + c + 1)
                    nc.vector.tensor_tensor(hf[:, n % 2, LO, c, :], h[:, c, :],
                                            hf[:, n % 2, HI, c, :].bitcast(F32), ALU.subtract).then_inc(hlo_done, 1)

            def accumulate(i, q, n):
                for t in range(TT):
                    dve.wait_ge(dn_done, i * DN + 2 * n + t // 2 + 1)
                    if n:
                        dve.wait_ge(acc_done, i * ACC + TT * (n - 1) + t + 1)
                    y = ym[:, q, D * t:D * t + D]
                    nc.vector.tensor_tensor(y, ps_dn[:, t // 2, D * (t % 2):D * (t % 2) + D],
                                            y if n else xin[:, q, t, :], ALU.add).then_inc(acc_done, 1)

            def tokens(k, q):
                i = 2 * k + q
                done = choose(i)
                product(i, 0)
                place(i, k, q, done)
                product(i, 1)
                if is_block(i + 1):
                    x_lo(i + 1, 1 - q, 0)
                accumulate(i, q, 0)
                if is_block(i + 1):
                    x_lo(i + 1, 1 - q, 1)
                accumulate(i, q, 1)
                if isinstance(k, int) and k == 0:
                    split_lo(2 + q, q, 2 + q)

            by_pairs(dve, B, tokens)

            def chunk_lo(g, p):
                dve.wait_ge(chi_done, g + 1)
                nc.vector.tensor_tensor(xf[:, p, LO, :, 0:CH], ps_t[:, p, :].rearrange("p (f t) -> p f t", f=FC),
                                        xf[:, p, HI, :, 0:CH].bitcast(F32), ALU.subtract).then_inc(clo_done, 1)

            def chunk(kk, j):
                g, p = chunk_of(kk, j), j % 2
                if is_chunk(g + 1):
                    chunk_lo(g + 1, 1 - p)
                dve.wait_ge(csilu_done, g + 1)
                dve.wait_ge(cgu_done, 2 * g + 2)
                if is_chunk(g - 2):
                    dve.wait_ge(chlo_done, g - 1)
                else:
                    dve.wait_ge(hlo_done, B * HN)
                nc.vector.tensor_tensor(h[:, p, :], ps_gu[:, 2 * p + 1, :], sg[:, p, :], ALU.mult).then_inc(ch_done, 1)
                dve.wait_ge(chhi_done, g + 1)
                nc.vector.tensor_tensor(hf[:, p, LO, :, 0:CH], h[:, p, :].rearrange("p (c t) -> p c t", c=IC),
                                        hf[:, p, HI, :, 0:CH].bitcast(F32), ALU.subtract).then_inc(chlo_done, 1)
                nxt = split_next(kk, j)
                if nxt:
                    n, par, loaded = nxt
                    split_lo(2 + par, par, n)

            chunk_lo(0, 0)
            by_pairs(dve, CHUNKS, chunk, NCH)

            def norm(k, q):
                i = 2 * k + q
                dve.wait_ge(ym_in[q], 16 * (k + 1))
                dve.wait_ge(gathered[q], 16 * 2 * TT * (k + 1))
                for c in range(2):
                    for t in range(TT):
                        if c:
                            dve.wait_ge(sum_done, i * 2 * TT + t + 1)
                        y = ym[:, q, D * t:D * t + D]
                        at = META_W + TT * c + t
                        nc.vector.scalar_tensor_tensor(out=y, in0=gath[:, q, 2 * t + c, :], scalar=ym[:, q, at:at + 1],
                                                       in1=y, op0=ALU.mult, op1=ALU.add).then_inc(sum_done, 1)
                for t in range(TT):
                    dve.wait_ge(sum_done, i * 2 * TT + TT + t + 1)
                    nc.vector.bn_stats(st6[:, t, :], ym[:, q, D * t:D * t + D]).then_inc(stat_done, 1)
                if is_block(i - 1):
                    dve.wait_ge(norm_done, i * TT)
                for t in range(TT):
                    wait_alone(dve, stat_done, i * TT + t + 1, idx_in, 16)
                    nc.vector.bn_aggr(mv[:, t, :], st6[:, t, :]).then_inc(mv_done, 1)
                dve.wait_ge(rstd_done, i + 1)
                if is_block(i - 2):
                    dve.wait_ge(out_done[q], 16 * k)
                for t in range(TT):
                    nc.vector.tensor_scalar(yo[:, q, t, :], ym[:, q, D * t:D * t + D], mv[:, t, 0:1], rstd[:, t, :],
                                            ALU.subtract, ALU.mult).then_inc(norm_done, 1)

            by_pairs(dve, B, norm)

        @block.tensor
        def _(pe):
            pe.wait_ge(consts, 7)

            def products(o, pairs):
                parts = ((HI, HI), (HI, LO), (LO, HI))
                for n, (l, r) in enumerate(pairs):
                    for k, (a, b) in enumerate(parts):
                        ins = nc.tensor.matmul(o, l(a), r(b), start=(n == 0 and k == 0),
                                               stop=(n == len(pairs) - 1 and k == len(parts) - 1))
                return ins

            def turn(i, k, q, f):
                if f == 0:
                    pe.wait_ge(x_in[q], 16 * (k + 1))
                after(pe, xlo_done, i * FC + f)
                for t in range(TT):
                    ins = nc.tensor.transpose(ps_t[:, 0, P * t:P * t + P], xin[:, q, t, P * f:P * f + P], ident[:, :])
                ins.then_inc(xt_done, 1)

            def gate_up(i, q, n):
                for c in range(IC):
                    for kind in range(2):
                        after(pe, h_done if kind else silu_done, i * HN + IC * (n - 1) + c + 1)
                        products(ps_gu[:, 2 * c + kind, :],
                                 [(lambda a, f=f: w[:, n, a, kind, f, P * c:P * c + P], lambda b, f=f: xf[:, q, b, f, :])
                                  for f in range(FC)]).then_inc(gu_done, 1)

            def down(i, n):
                pe.wait_ge(hlo_done, i * HN + IC * n + IC)
                for pair in range(2):
                    after(pe, acc_done, i * ACC + TT * (n - 1) + 2 * pair + 2)
                    for half in range(2):
                        t = P * (2 * pair + half)
                        ins = products(ps_dn[:, pair, D * half:D * half + D],
                                       [(lambda a, c=c: hf[:, n % 2, a, c, t:t + P], lambda b, c=c: w[:, n, b, 2, c, :])
                                        for c in range(IC)])
                    ins.then_inc(dn_done, 1)

            def count(i):
                pe.wait_ge(step_done, i * ROUTE_STEPS + SELECTED)
                nc.tensor.matmul(counts[:, :, :], before[:, :], sel[:, :, :], start=True, stop=False)
                for d in range(1, TT + 1):
                    ins = nc.tensor.matmul(counts[:, d:, :], ones[:, :], sel[:, 0:TT + 1 - d, :], start=False,
                                           stop=(d == TT))
                ins.then_inc(cnt_done, 1)

            for f in range(FC):
                turn(0, 0, 0, f)
            pe.wait_ge(ready, 2)

            def tokens(k, q):
                i = 2 * k + q
                pe.wait_ge(xlo_done, i * FC + FC)
                after(pe, ready, i + 2)
                for t in range(TT):
                    ins = products(logits[:, t, :],
                                   [(lambda a, f=f, t=t: xf[:, q, a, f, P * t:P * t + P], lambda b, f=f: wg[:, b, f, :])
                                    for f in range(FC)])
                ins.then_inc(logits_done, 1)
                if isinstance(k, int) and i == 0:
                    pe.wait_ge(w_lo, 1)
                gate_up(i, q, 0)
                count(i)
                if isinstance(k, int) and i == 0:
                    pe.wait_ge(w_lo, 2)
                gate_up(i, q, 1)
                if is_block(i + 1):
                    turn(i + 1, k + q, 1 - q, 0)
                down(i, 0)
                if is_block(i + 1):
                    turn(i + 1, k + q, 1 - q, 1)
                down(i, 1)

            by_pairs(pe, B, tokens)

            def chunk_turn(g, p, rounds):
                pe.wait_ge(xs_in[p], 16 * rounds)
                if is_chunk(g - 2):
                    pe.wait_ge(clo_done, g - 1)
                else:
                    pe.wait_ge(xlo_done, B * FC)
                    pe.wait_ge(ready, B + 2)
                for f in range(FC):
                    for t in range(CT):
                        at = CH * f + P * t
                        ins = nc.tensor.transpose(ps_t[:, p, at:at + P], xs[:, p, t, P * f:P * f + P], ident[:, :])
                ins.then_inc(ct_done, 1)

            def chunk_down(g, p, at):
                pe.wait_ge(chlo_done, g + 1)
                if is_chunk(g - 2):
                    pe.wait_ge(cy_done, g - 1)
                else:
                    pe.wait_ge(acc_done, B * ACC)
                for t in range(CT):
                    ins = products(ps_dn[:, p, D * t:D * t + D],
                                   [(lambda a, c=c: hf[:, p, a, c, P * t:P * t + P], lambda b, c=c: w[:, at, b, 2, c, :])
                                    for c in range(IC)])
                ins.then_inc(cdn_done, 1)

            def chunk(kk, j):
                g, p, at = chunk_of(kk, j), j % 2, 2 + j // NCH
                if is_chunk(g + 1):
                    chunk_turn(g + 1, 1 - p, NCH * kk + (j + 1) // 2 + 1)
                pe.wait_ge(clo_done, g + 1)
                if j % NCH == 0:
                    pe.wait_ge(w_lo, 2 * kk + j // NCH + NSHARED + 1)
                for kind in range(2):
                    if is_chunk(g - 2):
                        pe.wait_ge(ch_done if kind else csilu_done, g - 1)
                    else:
                        pe.wait_ge(h_done, B * HN)
                    for c in range(IC):
                        ins = products(ps_gu[:, 2 * p + kind, CH * c:CH * c + CH],
                                       [(lambda a, f=f: w[:, at, a, kind, f, P * c:P * c + P],
                                         lambda b, f=f: xf[:, p, b, f, 0:CH]) for f in range(FC)])
                    ins.then_inc(cgu_done, 1)
                if is_chunk(g - 1):
                    chunk_down(g - 1, 1 - p, 2 + (j - 1) % (2 * NCH) // NCH)

            chunk_turn(0, 0, 1)
            by_pairs(pe, CHUNKS, chunk, NCH)
            chunk_down(CHUNKS - 1, (CHUNKS - 1) % 2, 3)


SCRATCH = {"x2": [B, P, TT, D], "hbm_self": [FC, P, SLOTS, T], "hbm_ck": [P, FC, 2, T], "hbm_cq": [P, FC, 2, T],
           "slots_x": [CHUNKS, P, CT, D], "slots_y": [CHUNKS, P, CT, D], "meta": [B, P, META]}


def program(nc, ap, scratch, out):
    attention_phase(nc, ap["x"], ap["xT"], ap["cT"], ap["w_att"], ap["tables"], ap["b_cols"], ap["bo_rows"],
                    scratch["x2"], scratch["hbm_self"], scratch["hbm_ck"], scratch["hbm_cq"], scratch["slots_x"])
    moe_phase(nc, scratch["x2"], scratch["slots_x"], scratch["slots_y"], scratch["meta"], ap["w_moe"], ap["w_gate"],
              ap["index"], out)


def layout(inp):
    f = {k: np.asarray(v) for k, v in inp.items()}

    def by_token(a):
        return np.ascontiguousarray(a.reshape(a.shape[0], TT, P, D).transpose(0, 2, 1, 3))

    def by_feature(a):
        return np.ascontiguousarray(a.transpose(0, 2, 1).reshape(a.shape[0], FC, P, T).transpose(0, 2, 1, 3))

    def col(b):
        return b.reshape(FC, P).transpose(1, 0)

    w_all = np.concatenate([f["L0_attn_Wqkv"], f["L0_attn_Wout"]]
                           + [f[f"L0_xattn_w_{n}"].T for n in ("q", "k", "v", "o")], axis=1)
    inv_freq = (1.0 / np.float32(10000.0) ** (np.arange(0, HD, 2, dtype=np.float32) / np.float32(HD))).astype(np.float32)
    angle = np.arange(T, dtype=np.float32)[None, :] * inv_freq[np.arange(P) % (HD // 2)][:, None]
    sign = np.where(np.arange(P) % 2 == 0, -1.0, 1.0).astype(np.float32)[:, None]
    def shared(a):
        return a.reshape(NSHARED, I, D)

    gate = np.concatenate([f["L0_ffn_we_gate"], shared(f["L0_ffn_ws_gate"])]).transpose(0, 2, 1)
    up = np.concatenate([f["L0_ffn_we_up"], shared(f["L0_ffn_ws_up"])]).transpose(0, 2, 1)
    down = np.concatenate([f["L0_ffn_we_down"].transpose(0, 2, 1), shared(f["L0_ffn_ws_down"].T)])
    w_moe = np.ascontiguousarray(np.stack([gate, up, down], axis=1).reshape(NX, 3, FC, P, I).transpose(0, 3, 1, 2, 4))
    return {
        "x": by_token(f["x"]), "xT": by_feature(f["x"]), "cT": by_feature(f["ctx_1024"]),
        "w_att": np.ascontiguousarray(w_all.reshape(FC, P, NW).transpose(1, 0, 2)),
        "tables": np.stack([np.cos(angle), np.sin(angle) * sign], axis=1).astype(np.float32),
        "b_cols": np.ascontiguousarray(np.stack([col(f[f"L0_xattn_b_{n}"]) for n in ("q", "k", "v")], axis=1)),
        "w_moe": w_moe, "w_gate": np.ascontiguousarray(f["L0_ffn_gate_w"].T.reshape(FC, P, NE).transpose(1, 0, 2)),
        "index": np.ascontiguousarray(np.broadcast_to(
            np.stack([np.arange(NE, dtype=np.float32) - NE, np.arange(NE, dtype=np.float32) * CAP])[:, None, :],
            (P, 2, TT, NE))),
        "bo_rows": np.ascontiguousarray(np.broadcast_to(f["L0_xattn_b_o"], (P, D))),
    }

def kernel(**inputs):
    import concourse.bacc as bacc
    from concourse.bass_utils import run_bass_kernel_spmd as run

    nc = bacc.Bacc("TRN2", target_bir_lowering=False, num_devices=1)
    arrays = layout(inputs)
    ap = {n: nc.dram_tensor(n, a.shape, F32, kind="ExternalInput").ap() for n, a in arrays.items()}
    out = nc.dram_tensor("out", [B, P, TT, D], F32, kind="ExternalOutput").ap()
    scratch = {n: nc.dram_tensor(n, s, F32, kind="Internal").ap() for n, s in SCRATCH.items()}
    program(nc, ap, scratch, out)
    r = run(nc, [arrays], core_ids=[0])
    got = np.asarray(r.results[0]["out"])
    return np.ascontiguousarray(got.transpose(0, 2, 1, 3).reshape(B, T, D))
```

```python
import concourse.bass as bass
from concourse import mybir
from contextlib import ExitStack

import numpy as np

F32 = mybir.dt.float32
F32R = mybir.dt.float32r
ALU = mybir.AluOpType
ACT = mybir.ActivationFunctionType
AX = mybir.AxisListType

P = 128
B, T, D = 8, 512, 256
H, HD = 16, 16
TT = T // P
FC = D // P
HG = 4
NG = H // HG
HM = H // FC
NSC, NMX = 2, 3
LEAD = 6
PV_AT = 2
JOB_AT = 3
STEPS = NG * TT
NMAX = H * TT
EPS = 1e-5
HI, LO = 0, 1
SLOTS = 4

WCOL = {n: i * D for i, n in enumerate(("q", "k", "v", "w0", "cq", "ck", "cv", "w1"))}
NW = len(WCOL) * D

FIRST, SECOND = 0, 1
SELF, CROSS = 0, 1
TASKS = {
    FIRST: {
        0: [("cq", 0, -1), ("ck", 0, -1)], 1: [("ot1", 0, -2), ("cq", 1, -1)], 2: [("nm0", 1, 0), ("ot1", 1, -2)],
        3: [("ot1", 2, -2), ("ck", 1, -1)], 4: [("ot1", 3, -2), ("cv", 0, -1)], 5: [("cv", 1, -1)],
        6: [("nm0", 2, 0)], 7: [("nt1", 0, -2)], 8: [("nt1", 1, -2)], 9: [("w1", 0, -2)],
        10: [("nm0", 3, 0), ("w1", 1, -2)], 11: [("x", 0, 1)], 12: [("ln1", 0, -2)], 13: [("x1b", 0, -1)],
        14: [("nm1", 0, -1)],
    },
    SECOND: {
        0: [("q", 0, 1)], 1: [("ot0", 0, 0), ("k", 0, 1), ("qf", 0, 1)], 2: [("nm1", 1, -1), ("ot0", 1, 0)],
        3: [("kf", 0, 1), ("ot0", 2, 0), ("q", 1, 1)], 4: [("k", 1, 1), ("qf", 1, 1), ("ot0", 3, 0)],
        5: [("kf", 1, 1), ("v", 0, 1)], 6: [("nm1", 2, -1), ("nt0", 0, 0)], 7: [("nt0", 1, 0), ("v", 1, 1)],
        8: [("w0", 0, 0)], 9: [("w0", 1, 0)], 10: [("nm1", 3, -1)], 11: [("ln0", 0, 0)], 12: [("c", 0, 0)],
        13: [("xt", 0, 0)], 14: [("nm0", 0, 1), ("xt", 1, 0)],
    },
}
PER = {"q": 2, "k": 2, "v": 2, "ck": 2, "cv": 2, "xt": 2, "cq": 2, "nt0": 2, "nt1": 2, "w0": 2, "w1": 2,
       "ot0": TT, "ot1": TT, "nm0": NG, "nm1": NG, "x": 1, "c": 1}
ORDER = [task for half in (FIRST, SECOND) for s in sorted(TASKS[half]) for task in TASKS[half][s]
         if task[0] in PER and task[0] not in ("x", "c")]
assert len(ORDER) % 2 == 0
SPLIT = ("q", "k", "ck", "cq", "xt", "nt0", "nt1", "nm0", "nm1", "x", "c")


def exists(b):
    return not isinstance(b, int) or 0 <= b < B


def upto(kind, b, n):
    return b * PER[kind] + n + 1


def wait_alone(eng, s, value, met, least):
    value = value if isinstance(value, int) else eng.snap(eng.to_reg(value))
    eng.wait_ge(met, least)
    eng.wait_ge(s, value)


def attention_phase(nc, x, xT, cT, w_att, tables, b_cols, bo_rows, x2, hbm_self, hbm_ck, hbm_cq, slots_x):
    with ExitStack() as ctx:
        def sb(name, shape, dt=F32):
            return ctx.enter_context(nc.sbuf_tensor(name, shape, dt))

        def sem(name):
            return ctx.enter_context(nc.semaphore(name))

        w = sb("w", [P, 2, FC, NW], F32R)
        ident = sb("ident", [P, P])
        trig = sb("trig", [P, 2, T])
        bcol = sb("bcol", [P, 3, FC])
        bo = sb("bo", [P, D])
        xin = sb("xin", [P, TT, D])
        raw = sb("raw", [P, FC, T])
        xf = sb("xf", [P, 2, FC, T], F32R)
        cf = sb("cf", [P, 2, FC, T], F32R)
        nf = cf
        ot = sb("ot", [P, NG, T])
        on = sb("on", [P, TT, D])
        res = sb("res", [P, TT, D])
        rot = res[:, :, :].rearrange("p (a u) d -> p a (u d)", a=2)
        cosq = sb("cosq", [P, 2, T])
        stage = sb("stage", [P, FC, SLOTS, T], F32R)
        qk = sb("qk", [P, 2, H, T], F32R)
        va = sb("va", [P, 2, TT, H, 2 * HD])
        prob = sb("prob", [P, 2, HG, T])
        nm = sb("nm", [P, 2, HG * TT])
        mst = sb("mst", [HG * TT, 2, 2, P], F32R)
        rden = sb("rden", [P, TT, H])
        x1 = sb("x1", [P, TT, D])
        x1b = sb("x1b", [P, TT, D])
        st6 = sb("st6", [P, TT, 6])
        mv = sb("mv", [P, TT, 2])
        rstd = sb("rstd", [P, TT, 1])
        mhalf = sb("mhalf", [P, TT, 1])
        eps = sb("eps", [P, TT, 1])
        zeros = sb("zeros", [P, ROW])
        one = sb("one", [P, 1])

        ps_sc = ctx.enter_context(nc.psum_tensor("ps_sc", [P, NSC, T], F32))
        ps_max = ctx.enter_context(nc.psum_tensor("ps_max", [P, NMX, T], F32))
        ps_out = ctx.enter_context(nc.psum_tensor("ps_out", [P, T], F32))
        ps_job = ctx.enter_context(nc.psum_tensor("ps_job", [P, 2, T], F32))

        raw_w = [sem("raw_w0"), sem("raw_w1")]
        w_hi, w_ready, consts = sem("w_hi"), sem("w_ready"), sem("consts")
        consts_dma = sem("consts_dma")
        in_sem = {n: sem(f"{n}_in") for n in ("x", "c", "xin")}
        job_done = {k: sem(f"{k}_done") for k in PER if k not in ("x", "c")}
        read = {k: sem(f"{k}_read") for k in job_done}
        hi_done = {k: sem(f"{k}_hi") for k in SPLIT}
        lo_done = {k: sem(f"{k}_lo") if k in ("q", "k", "x", "c") else read[k] for k in SPLIT}
        sin_done = {k: sem(f"{k}_sin") for k in ("q", "k")}
        roped = {k: sem(f"{k}_roped") for k in ("q", "k")}
        self_out = [sem(f"self_out{m}") for m in range(FC)]
        ck_out, cq_out = sem("ck_out"), sem("cq_out")
        stack_in = [[sem(f"stack_in{a}{g}") for g in range(NG)] for a in range(2)]
        smax_done, max_done, st_done, exp_done, pv_done, oev_done = (
            [sem(f"{n}{a}") for a in range(2)] for n in ("smax", "max", "st", "exp", "pv", "oev"))
        mrow_in = [[sem(f"mrow_in{a}{g}") for g in range(2)] for a in range(2)]
        rden_done, stat_done, mv_done, var_done, rstd_done, ln_done = (
            [sem(f"{n}{a}") for a in range(2)] for n in ("rden", "stat", "mv", "var", "rstd", "ln"))
        x1b_done, x2_out, cleared = sem("x1b_done"), sem("x2_out"), sem("cleared")

        block = ctx.enter_context(nc.Block())

        def tasks(half, s, k):
            return [(kind, n, k + off) for kind, n, off in TASKS[half].get(s, []) if exists(k + off)]

        def instances(half, k):
            def one(half, k):
                a = (SELF, k) if half == FIRST else (CROSS, k - 1)
                return a if exists(a[1]) else None

            cur = one(half, k)
            nxt = one(SECOND, k) if half == FIRST else one(FIRST, k + 1)
            h, p, prv = half, k, None
            while prv is None and not (isinstance(p, int) and p < -1):
                h, p = (SECOND, p - 1) if h == FIRST else (FIRST, p)
                prv = one(h, p)
            return cur, nxt, prv

        def unfinished(h, k):
            return exists(k if h == SECOND else k - 2)

        def every_period(eng, half):
            for k in (-1, 0, 1):
                half(FIRST, k)
                half(SECOND, k)
            with eng.Fori(2, B - 1) as k:
                half(FIRST, k)
                half(SECOND, k)
            for k in (B - 1, B, B + 1):
                half(FIRST, k)
                half(SECOND, k)

        def bank(kind, n):
            return ps_job[:, [t[:2] for t in ORDER].index((kind, n)) % 2, :]

        def maxima_of(s, cur, nxt):
            inst, first = (cur, TT * (s + LEAD)) if s + LEAD < STEPS else (nxt, TT * (s + LEAD - STEPS))
            return [(inst, n) for n in range(first, first + TT)] if inst else []

        def wait_done(eng, s, kind, b, n):
            if exists(b):
                eng.wait_ge(s, upto(kind, b, n))

        def columns(a):
            return slice(a * (NW // 2), (a + 1) * (NW // 2))

        def staged_w(a):
            return prob[:, :, :, :].rearrange("p a h t -> p (a h t)").rearrange("p (f n) -> p f n", f=FC)[:, :, columns(a)]

        @block.sync
        def _(sp):
            for a in (SELF, CROSS):
                sp.dma_start(staged_w(a), w_att[:, :, columns(a)]).then_inc(raw_w[a], 16)
            sp.dma_start(trig[:, :, :], tables).then_inc(consts_dma, 16)
            sp.dma_start(bcol[:, :, :], b_cols).then_inc(consts_dma, 16)
            sp.dma_start(bo[:, :], bo_rows).then_inc(consts_dma, 16)

            def mrows(a, b, g):
                sp.wait_ge(read[f"nm{a}"], upto(f"nm{a}", b, g))
                for part in (HI, LO):
                    row = 96 + part
                    sp.dma_start(
                        qk[row:row + 1, 0, HG * g:HG * g + HG, :].rearrange("o h (c q) -> o (h c) q", q=P).bitcast(F32),
                        mst[:, g % 2, part, :].bitcast(F32)).then_inc(mrow_in[a][g % 2], 16)

            def stack(inst, before, g):
                a, b = inst
                m, rows = g // 2, slice(64 * (g % 2), 64 * (g % 2) + 64)
                if before:
                    free = before[1] * NMAX + 4 * TT * (g + 1)
                    free = free if isinstance(free, int) else sp.snap(sp.to_reg(free))
                if a == SELF:
                    sp.wait_ge(self_out[m], b * 16 + 16)
                else:
                    out_c = b * 16 + 16
                    out_c = out_c if isinstance(out_c, int) else sp.snap(sp.to_reg(out_c))
                    sp.wait_ge(ck_out, out_c)
                    sp.wait_ge(cq_out, out_c)
                if before:
                    sp.wait_ge(st_done[before[0]], free)
                for r, (qp, kp) in enumerate(((HI, HI), (HI, LO), (LO, HI))):
                    for s, part in ((0, qp), (1, kp)):
                        if a == SELF:
                            src = hbm_self[m, rows, 2 * s + part, :]
                        else:
                            src = (hbm_ck if s else hbm_cq)[rows, m, part, :]
                        sp.dma_start(qk[HD * r:HD * r + HD, s, HG * g:HG * g + HG, :].bitcast(F32),
                                     src.rearrange("(h d) t -> d h t", d=HD)).then_inc(stack_in[a][g], 16)

            shares = slots_x.rearrange("g p t d -> (g p t) d").rearrange("(k p a) d -> k p a d", k=B, p=P)

            def load(name, dst, src, b, ready):
                if ready is not None:
                    wait_alone(sp, *ready, consts_dma, 48)
                sp.dma_start(dst, src[b, :, :, :]).then_inc(in_sem[name], 16)

            def half(h, k):
                cur, nxt, prv = instances(h, k)
                last = cur or prv
                if h == SECOND and isinstance(k, int) and k == -1:
                    sp.wait_ge(consts, 7)
                    sp.wait_ge(w_hi, 1)
                    sp.wait_ge(w_ready, 1)
                if cur:
                    stack(cur, prv, NG - 1)
                if h == FIRST:
                    if exists(k + 1):
                        load("x", raw[:, :, :], xT, k + 1, (lo_done["c"], upto("c", k - 1, 0)) if exists(k - 1) else None)
                    if exists(k):
                        load("xin", xin[:, :, :], x, k, (read["w0"], upto("w0", k - 1, 1)) if exists(k - 1) else None)
                elif exists(k):
                    load("c", raw[:, :, :], cT, k, (lo_done["x"], upto("x", k + 1 if exists(k + 1) else k, 0)))
                for s in range(STEPS):
                    for kind, n, b in tasks(h, s, k):
                        if kind in ("nm0", "nm1"):
                            mrows(int(kind[2]), b, n)
                    if h == FIRST and s == 3 and exists(k - 1):
                        sp.wait_ge(lo_done["ck"], upto("ck", k - 1, 1))
                        sp.dma_start(hbm_ck, stage[:, :, 2:4, :].bitcast(F32)).then_inc(ck_out, 16)
                        sp.wait_ge(lo_done["cq"], upto("cq", k - 1, 1))
                        sp.dma_start(hbm_cq, stage[:, :, 0:2, :].bitcast(F32)).then_inc(cq_out, 16)
                    if h == SECOND and s in (3, 5) and exists(k + 1):
                        m = (s - 3) // 2
                        sp.wait_ge(lo_done["k"], upto("k", k + 1, m))
                        sp.dma_start(hbm_self[m], stage[:, m, :, :].bitcast(F32)).then_inc(self_out[m], 16)
                    if h == FIRST and s == 10 and exists(k):
                        sp.dma_start(shares[k, :, :, :], zeros[:, :].unsqueeze(1).to_broadcast([P, CLEAR, ROW])) \
                            .then_inc(cleared, 16)
                    if h == FIRST and s == 13 and exists(k - 2):
                        wait_alone(sp, ln_done[CROSS], (k - 2) * TT + TT, consts_dma, 48)
                        sp.dma_start(x2[k - 2, :, :, :], res[:, :, :]).then_inc(x2_out, 16)
                    if nxt and s % TT == 0 and s:
                        stack(nxt, last, s // TT - 1)

            every_period(sp, half)
            sp.wait_ge(x2_out, B * 16)
            sp.wait_ge(cleared, B * 16)

        @block.gpsimd
        def _(pool):
            nc.gpsimd.memset(ident[:, :], 0.0).then_inc(consts, 1)
            pool.wait_ge(consts, 1)
            nc.gpsimd.affine_select(out=ident[:, :], in_=ident[:, :], compare_op=ALU.not_equal, fill=1.0,
                                    base=0, pattern=[[-1, P]], channel_multiplier=1).then_inc(consts, 1)
            nc.gpsimd.memset(mhalf[:, :, :], -0.5).then_inc(consts, 1)
            nc.gpsimd.memset(eps[:, :, :], EPS).then_inc(consts, 1)
            nc.gpsimd.memset(one[:, :], 1.0).then_inc(consts, 1)
            nc.gpsimd.memset(zeros[:, :], 0.0).then_inc(consts, 1)
            nc.gpsimd.memset(qk[0:96, 1, :, :].bitcast(F32), 0.0).then_inc(consts, 1)
            pool.wait_ge(consts, 7)
            pool.wait_ge(consts_dma, 48)

            def split_lo(kind, b, n, out, value, high):
                pool.wait_ge(hi_done[kind], upto(kind, b, n))
                nc.gpsimd.tensor_tensor(out, value, high.bitcast(F32), ALU.subtract).then_inc(lo_done[kind], 1)

            def half(h, k):
                for s in range(STEPS):
                    for kind, n, b in tasks(h, s, k):
                        if kind in ("q", "k"):
                            c = 0 if kind == "q" else 1
                            pool.wait_ge(read[kind], upto(kind, b, n))
                            nc.gpsimd.tensor_tensor(rot[:, c, :], rot[:, c, :], trig[:, 1, :], ALU.mult) \
                                .then_inc(sin_done[kind], 1)
                            pool.wait_ge(sin_done[kind], upto(kind, b, n))
                            nc.gpsimd.tensor_tensor(cosq[:, c, :], cosq[:, c, :], rot[:, c, :], ALU.add) \
                                .then_inc(roped[kind], 1)
                        if kind in ("qf", "kf"):
                            c = 0 if kind == "qf" else 1
                            split_lo(kind[0], b, n, stage[:, n, 2 * c + LO, :], cosq[:, c, :], stage[:, n, 2 * c, :])
                        if kind == "x":
                            split_lo("x", b, 0, xf[:, LO, :, :], raw[:, :, :], xf[:, HI, :, :])
                        if kind == "c":
                            split_lo("c", b, 0, cf[:, LO, :, :], raw[:, :, :], cf[:, HI, :, :])
                        if kind in ("w0", "w1"):
                            a, at = int(kind[1]), slice(2 * n, 2 * n + 2)
                            pool.wait_ge(mv_done[a], b * TT + 2 * n + 2)
                            nc.gpsimd.tensor_tensor(rstd[:, at, :], mv[:, at, 1:2], eps[:, at, :], ALU.add) \
                                .then_inc(var_done[a], 1)
                            pool.wait_ge(var_done[a], upto(kind, b, n))
                            nc.gpsimd.tensor_tensor(rstd[:, at, :], rstd[:, at, :], mhalf[:, at, :], ALU.pow) \
                                .then_inc(rstd_done[a], 1)
                        if kind == "x1b":
                            pool.wait_ge(ln_done[SELF], b * TT + TT)
                            wait_done(pool, read["w1"], "w1", b - 1, 1)
                            for t in range(TT):
                                nc.gpsimd.tensor_tensor(x1b[:, t, :], x1[:, t, :], bo[:, :], ALU.add) \
                                    .then_inc(x1b_done, 1)

            every_period(pool, half)

        @block.scalar
        def _(act):
            act.wait_ge(consts, 5)
            nc.scalar.activation(qk[96:P, 1, :, :].rearrange("p h t -> p (h t)"), one[96:P, :].to_broadcast([P - 96, H * T]),
                                 ACT.Copy).then_inc(w_hi, 1)
            for a in (SELF, CROSS):
                act.wait_ge(raw_w[a], 16)
                nc.scalar.activation(w[:, HI, :, columns(a)], staged_w(a), ACT.Copy).then_inc(w_hi, 1)
            act.wait_ge(consts_dma, 48)

            def split_hi(kind, b, n, out, value, bias=None):
                if kind in job_done and kind not in ("q", "k"):
                    act.wait_ge(job_done[kind], upto(kind, b, n))
                if bias is None:
                    ins = nc.scalar.activation(out, value, ACT.Copy)
                else:
                    ins = nc.scalar.activation(out, value, ACT.Identity, bias=bias)
                ins.then_inc(hi_done[kind], 1)

            def mrow_wait(inst, g):
                a, b = inst
                act.wait_ge(mrow_in[a][g % 2], b * 64 + (g // 2) * 32 + 32)

            def head_outputs(inst, before, g):
                a, b = inst
                act.wait_ge(pv_done[a], b * STEPS + TT * g + TT)
                if before:
                    act.wait_ge(job_done[f"ot{before[0]}"], before[1] * TT + TT)
                nc.scalar.activation(ot[:, g, :], ps_out[:, :], ACT.Copy).then_inc(oev_done[a], 1)

            def task(kind, n, b, cur, prv):
                if kind in ("qf", "kf"):
                    act.wait_ge(roped[kind[0]], upto(kind[0], b, n))
                    if kind == "qf" and exists(b - 2):
                        act.wait_ge(cq_out, (b - 2) * 16 + 16)
                    if kind == "kf" and exists(b - 2):
                        act.wait_ge(ck_out, (b - 2) * 16 + 16)
                    c = 0 if kind == "qf" else 1
                    split_hi(kind[0], b, n, stage[:, n, 2 * c, :], cosq[:, c, :])
                if kind in ("v", "cv"):
                    a = SELF if kind == "v" else CROSS
                    if exists(b - 1):
                        act.wait_ge(pv_done[a], (b - 1) * STEPS + STEPS)
                    act.wait_ge(job_done[kind], upto(kind, b, n))
                    nc.scalar.activation(va[:, a, 2 * n:2 * n + 2, :, 0:HD],
                                         bank(kind, n).rearrange("p (t h d) -> p t h d", t=2, h=H),
                                         ACT.Copy).then_inc(read[kind], 1)
                if kind == "x":
                    act.wait_ge(in_sem["x"], b * 16 + 16)
                    wait_done(act, job_done["cq"], "cq", b - 2, 1)
                    split_hi("x", b, 0, xf[:, HI, :, :], raw[:, :, :])
                if kind == "c":
                    act.wait_ge(in_sem["c"], b * 16 + 16)
                    wait_done(act, job_done["w0"], "w0", b, 1)
                    split_hi("c", b, 0, cf[:, HI, :, :], raw[:, :, :])
                if kind == "ck":
                    act.wait_ge(self_out[n], (b + 1 if exists(b + 1) else b) * 16 + 16)
                    split_hi(kind, b, n, stage[:, n, 2, :], bank(kind, n), bcol[:, 1, n:n + 1])
                if kind == "cq":
                    act.wait_ge(self_out[n], (b + 1 if exists(b + 1) else b) * 16 + 16)
                    split_hi(kind, b, n, stage[:, n, 0, :], bank(kind, n), bcol[:, 0, n:n + 1])
                if kind == "nt1":
                    wait_done(act, job_done["cv"], "cv", b + 1, 1)
                    split_hi(kind, b, n, nf[:, HI, n, :], bank(kind, n), bcol[:, 2, n:n + 1])
                if kind == "nt0":
                    wait_done(act, job_done["w1"], "w1", b - 2, 1)
                    split_hi(kind, b, n, nf[:, HI, n, :], bank(kind, n))
                if kind == "xt":
                    wait_done(act, job_done["v"], "v", b + 1, 1)
                    split_hi(kind, b, n, xf[:, HI, n, :], bank(kind, n))
                if kind in ("nm0", "nm1"):
                    a = int(kind[2])
                    if n >= 2:
                        mrow_wait((a, b), n - 2)
                    elif n == 1 and prv:
                        mrow_wait(prv, 3)
                    elif n == 0 and (cur or prv):
                        mrow_wait(cur or prv, 2)
                    split_hi(kind, b, n, mst[:, n % 2, HI, :], bank(kind, n)[0:HG * TT, 0:P])

            def half(h, k):
                cur, nxt, prv = instances(h, k)
                if h == FIRST and isinstance(k, int) and k == 0:
                    act.wait_ge(w_ready, 5)
                older = instances(prv[0], prv[1] + prv[0])[2] if prv else None
                for s in range(STEPS):
                    for kind, n, b in tasks(h, s - 1, k):
                        task(kind, n, b, cur, prv)
                    for j in range(HG):
                        if cur:
                            a, b = cur
                            act.wait_ge(st_done[a], b * NMAX + HG * s + j + 1)
                            if j == 0:
                                if s >= 2:
                                    act.wait_ge(pv_done[a], b * STEPS + s - 1)
                                elif prv:
                                    act.wait_ge(pv_done[prv[0]], prv[1] * STEPS + STEPS - 1 + s)
                            nc.scalar.activation(prob[:, s % 2, j, :], ps_sc[:, (HG * s + j) % NSC, :],
                                                 ACT.Exp, scale=HD ** -0.5).then_inc(exp_done[a], 1)
                    if s == 0 and unfinished(h, k):
                        head_outputs(prv, older, NG - 1)
                    if cur and s % TT == 0 and s:
                        head_outputs(cur, prv, s // TT - 1)

            every_period(act, half)

        @block.vector
        def _(dve):
            nc.vector.memset(qk[:, 0, :, :].bitcast(F32), 0.0).then_inc(w_ready, 1)
            for a in (SELF, CROSS):
                dve.wait_ge(w_hi, 2 + a)
                nc.vector.tensor_tensor(w[:, LO, :, columns(a)], staged_w(a), w[:, HI, :, columns(a)].bitcast(F32),
                                        ALU.subtract).then_inc(w_ready, 1)
                nc.vector.memset(va[:, a, :, :, HD:2 * HD], 1.0).then_inc(w_ready, 1)
            dve.wait_ge(consts_dma, 48)

            def split_lo(kind, b, n, out, high, bias=None, value=None):
                value = bank(kind, n) if value is None else value
                dve.wait_ge(hi_done[kind], upto(kind, b, n))
                if bias is None:
                    ins = nc.vector.tensor_tensor(out, value, high.bitcast(F32), ALU.subtract)
                else:
                    ins = nc.vector.scalar_tensor_tensor(out=out, in0=value, scalar=bias, in1=high.bitcast(F32),
                                                         op0=ALU.add, op1=ALU.subtract)
                ins.then_inc(read[kind], 1)

            def maximum(inst, before, n):
                (a, b), g, r = inst, n // (HG * TT), n % (HG * TT)
                dve.wait_ge(smax_done[a], b * NMAX + n + 1)
                if r == 0:
                    if g >= 2:
                        dve.wait_ge(job_done[f"nm{a}"], upto(f"nm{a}", b, g - 2))
                    elif before:
                        dve.wait_ge(job_done[f"nm{before[0]}"], upto(f"nm{before[0]}", before[1], g + 2))
                nc.vector.tensor_reduce(nm[:, g % 2, r:r + 1], ps_max[:, n % NMX, :], axis=AX.X, op=ALU.max,
                                        negate=True).then_inc(max_done[a], 1)

            def task(kind, n, b):
                if kind in ("q", "k"):
                    c = 0 if kind == "q" else 1
                    if n:
                        dve.wait_ge(lo_done[kind], upto(kind, b, n - 1))
                    elif exists(b - 1):
                        dve.wait_ge(lo_done[kind], upto(kind, b - 1, 1))
                    if n == 0 and exists(b - 3):
                        dve.wait_ge(x2_out, (b - 3) * 16 + 16)
                    if n == 0 and exists(b - 2):
                        dve.wait_ge(ln_done[SELF], (b - 2) * TT + TT)
                    dve.wait_ge(job_done[kind], upto(kind, b, n))
                    nc.vector.tensor_tensor(cosq[:, c, :], bank(kind, n), trig[:, 0, :], ALU.mult)
                    nc.vector.stream_shuffle(rot[:, c, :], bank(kind, n), [p ^ 1 for p in range(32)]) \
                        .then_inc(read[kind], 1)
                if kind == "ck":
                    split_lo(kind, b, n, stage[:, n, 3, :], stage[:, n, 2, :], bcol[:, 1, n:n + 1])
                if kind == "cq":
                    split_lo(kind, b, n, stage[:, n, 1, :], stage[:, n, 0, :], bcol[:, 0, n:n + 1])
                if kind == "nt0":
                    split_lo(kind, b, n, nf[:, LO, n, :], nf[:, HI, n, :])
                if kind == "nt1":
                    split_lo(kind, b, n, nf[:, LO, n, :], nf[:, HI, n, :], bcol[:, 2, n:n + 1])
                if kind == "xt":
                    split_lo(kind, b, n, xf[:, LO, n, :], xf[:, HI, n, :])
                if kind in ("nm0", "nm1"):
                    split_lo(kind, b, n, mst[:, n % 2, LO, :], mst[:, n % 2, HI, :],
                             value=bank(kind, n)[0:HG * TT, 0:P])
                if kind in ("ot0", "ot1"):
                    a = int(kind[2])
                    heads = bank(kind, n).rearrange("p (h e) -> p h e", h=H)
                    if n == 0:
                        wait_done(dve, job_done["nt1"] if a == SELF else job_done["nt0"],
                                  "nt1" if a == SELF else "nt0", b - 2 if a == SELF else
                                  (b + 1 if exists(b + 1) else b), 1)
                    dve.wait_ge(job_done[kind], upto(kind, b, n))
                    nc.vector.reciprocal(rden[:, n, :], heads[:, :, HD]).then_inc(rden_done[a], 1)
                    dve.wait_ge(rden_done[a], upto(kind, b, n))
                    nc.vector.tensor_tensor(on[:, n, :].rearrange("p (h d) -> p h d", h=H), heads[:, :, 0:HD],
                                            rden[:, n, :].unsqueeze(2).to_broadcast([P, H, HD]), ALU.mult) \
                        .then_inc(read[kind], 1)
                if kind in ("w0", "w1"):
                    a, at = int(kind[1]), slice(2 * n, 2 * n + 2)
                    if a == SELF:
                        dve.wait_ge(in_sem["xin"], b * 16 + 16)
                        wait_done(dve, roped["k"], "k", b + 1, 1)
                        if not exists(b + 1) and n == 0 and exists(b - 2):
                            dve.wait_ge(x2_out, (b - 2) * 16 + 16)
                    else:
                        dve.wait_ge(x1b_done, b * TT + 2 * n + 2)
                        if n == 0:
                            dve.wait_ge(ln_done[SELF], (b + 1 if exists(b + 1) else b) * TT + TT)
                        if n == 0 and not exists(b + 1) and exists(b - 1):
                            dve.wait_ge(x2_out, (b - 1) * 16 + 16)
                    dve.wait_ge(job_done[kind], upto(kind, b, n))
                    nc.vector.tensor_tensor(res[:, at, :], bank(kind, n).rearrange("p (t n) -> p t n", t=2),
                                            (x1b if a else xin)[:, at, :], ALU.add).then_inc(read[kind], 1)
                    dve.wait_ge(read[kind], upto(kind, b, n))
                    for t in (2 * n, 2 * n + 1):
                        nc.vector.bn_stats(st6[:, t, :], res[:, t, :]).then_inc(stat_done[a], 1)
                    for t in (2 * n, 2 * n + 1):
                        wait_alone(dve, stat_done[a], b * TT + t + 1, w_hi, 1)
                        nc.vector.bn_aggr(mv[:, t, :], st6[:, t, :]).then_inc(mv_done[a], 1)
                if kind in ("ln0", "ln1"):
                    a = int(kind[2])
                    if a == SELF:
                        wait_done(dve, job_done["xt"], "xt", b - 1, 1)
                        if exists(b - 1):
                            dve.wait_ge(x1b_done, (b - 1) * TT + TT)
                    for t in range(TT):
                        dve.wait_ge(rstd_done[a], b * 2 + t // 2 + 1)
                        nc.vector.tensor_scalar((res if a else x1)[:, t, :], res[:, t, :], mv[:, t, 0:1],
                                                rstd[:, t, :], ALU.subtract, ALU.mult).then_inc(ln_done[a], 1)

            def half(h, k):
                cur, nxt, prv = instances(h, k)
                for s in range(STEPS):
                    turn = maxima_of(s, cur, nxt)
                    for kind, n, b in tasks(h, s - 1, k):
                        task(kind, n, b)
                    for j in range(HG):
                        if turn:
                            inst, n = turn[j]
                            maximum(inst, prv if inst is cur else cur or prv, n)

            every_period(dve, half)

        @block.tensor
        def _(pe):
            pe.wait_ge(w_ready, 2)
            pe.wait_ge(consts, 7)
            pe.wait_ge(w_hi, 1)

            def products(out, pairs):
                parts = [(a, b) for a, b in ((HI, HI), (HI, LO), (LO, HI))]
                for n, (l, r) in enumerate(pairs):
                    for k, (a, b) in enumerate(parts):
                        ins = nc.tensor.matmul(out, l(a), r(b), start=(n == 0 and k == 0),
                                               stop=(n == len(pairs) - 1 and k == len(parts) - 1))
                return ins

            def free_bank(kind, n, k):
                at = [t[:2] for t in ORDER].index((kind, n)) - 2
                while True:
                    prev, m, off = ORDER[at % len(ORDER)]
                    b = k + off if at >= 0 else k - 1 + off
                    if exists(b):
                        break
                    at -= 2
                    if at < -len(ORDER):
                        return
                pe.wait_ge(read[prev], upto(prev, b, m))

            def by_feature(kind, n, src):
                c = WCOL[kind] + P * n
                return products(bank(kind, n), [(lambda a, f=f: w[:, a, f, c:c + P], lambda b, f=f: src[:, b, f, :])
                                                for f in range(FC)])

            def by_token(kind, n, src):
                c = WCOL[kind]
                for part in range(2):
                    t = P * (2 * n + part)
                    ins = products(bank(kind, n)[:, D * part:D * part + D],
                                   [(lambda a, f=f: src[:, a, f, t:t + P], lambda b, f=f: w[:, b, f, c:c + D])
                                    for f in range(FC)])
                return ins

            def turn(kind, n, src):
                for t in range(TT):
                    ins = nc.tensor.transpose(bank(kind, n)[:, P * t:P * t + P], src[:, t, P * n:P * n + P], ident[:, :])
                return ins

            def job(kind, n, b, k):
                free_bank(kind, n, k)
                if kind in ("q", "k", "v"):
                    pe.wait_ge(lo_done["x"], upto("x", b, 0))
                    ins = (by_token if kind == "v" else by_feature)(kind, n, xf)
                elif kind in ("ck", "cv"):
                    pe.wait_ge(lo_done["c"], upto("c", b, 0))
                    ins = (by_token if kind == "cv" else by_feature)(kind, n, cf)
                elif kind == "cq":
                    pe.wait_ge(lo_done["xt"], upto("xt", b, 1))
                    ins = by_feature(kind, n, xf)
                elif kind in ("ot0", "ot1"):
                    pe.wait_ge(oev_done[int(kind[2])], b * NG + NG)
                    for g in range(NG):
                        ins = nc.tensor.transpose(bank(kind, n)[:, P * g:P * g + P], ot[:, g, P * n:P * n + P], ident[:, :])
                elif kind in ("nt0", "nt1"):
                    a = kind[2]
                    pe.wait_ge(read[f"ot{a}"], upto(f"ot{a}", b, TT - 1))
                    ins = turn(kind, n, on)
                elif kind in ("w0", "w1"):
                    a = kind[1]
                    pe.wait_ge(lo_done[f"nt{a}"], upto(f"nt{a}", b, 1))
                    ins = by_token(kind, n, nf)
                elif kind == "xt":
                    pe.wait_ge(ln_done[SELF], b * TT + TT)
                    ins = turn(kind, n, x1)
                else:
                    a = int(kind[2])
                    pe.wait_ge(max_done[a], b * NMAX + (n + 1) * HG * TT)
                    ins = nc.tensor.transpose(bank(kind, n)[0:HG * TT, 0:P], nm[:, n % 2, :], ident[:, :])
                ins.then_inc(job_done[kind], 1)

            def scores_max(inst, before, n):
                (a, b), h, c = inst, n // TT, n % TT
                if n % (HG * TT) == 0:
                    pe.wait_ge(stack_in[a][h // HG], b * 96 + 96)
                if n >= NMX:
                    pe.wait_ge(max_done[a], b * NMAX + n - NMX + 1)
                elif before:
                    pe.wait_ge(max_done[before[0]], before[1] * NMAX + NMAX)
                nc.tensor.matmul(ps_max[:, n % NMX, :], qk[0:96, 0, h, P * c:P * c + P], qk[0:96, 1, h, :],
                                 start=True, stop=True).then_inc(smax_done[a], 1)

            def scores(inst, before, s, j):
                (a, b), g, c = inst, s // TT, s % TT
                h, n = HG * g + j, HG * s + j
                if n >= NSC:
                    pe.wait_ge(exp_done[a], b * NMAX + n - NSC + 1)
                elif before:
                    pe.wait_ge(exp_done[before[0]], before[1] * NMAX + NMAX)
                if c == 0 and j == 0:
                    pe.wait_ge(mrow_in[a][g % 2], b * 64 + (g // 2) * 32 + 32)
                nc.tensor.matmul(ps_sc[:, n % NSC, :], qk[:, 1, h, P * c:P * c + P], qk[:, 0, h, :],
                                 start=True, stop=True).then_inc(st_done[a], 1)

            def head_outputs(inst, before, s):
                (a, b), g, c = inst, s // TT, s % TT
                pe.wait_ge(exp_done[a], b * NMAX + HG * s + HG)
                if s == 0:
                    v = "cv" if a else "v"
                    pe.wait_ge(read[v], upto(v, b, 1))
                if c == 0:
                    if g:
                        pe.wait_ge(oev_done[a], b * NG + g)
                    elif before:
                        pe.wait_ge(oev_done[before[0]], before[1] * NG + NG)
                for j in range(HG):
                    ins = nc.tensor.matmul(ps_out[32 * j:32 * j + 32, :], va[:, a, c, HG * g + j, :],
                                           prob[:, s % 2, j, :], start=(c == 0), stop=(c == TT - 1),
                                           tile_position=(0, 32 * j))
                ins.then_inc(pv_done[a], 1)

            def half(h, k):
                cur, nxt, prv = instances(h, k)
                if h == FIRST and isinstance(k, int) and k == 0:
                    pe.wait_ge(w_ready, 5)
                for s in range(STEPS):
                    ahead = [(inst, prv if inst is cur else cur or prv, n) for inst, n in maxima_of(s, cur, nxt)]
                    for j in range(HG):
                        if j == PV_AT:
                            if s == 0 and unfinished(h, k):
                                head_outputs(prv, None, STEPS - 1)
                            if s and cur:
                                head_outputs(cur, prv, s - 1)
                        if cur:
                            scores(cur, prv, s, j)
                        if ahead:
                            scores_max(*ahead[j])
                        if j == JOB_AT:
                            for kind, n, b in tasks(h, s, k):
                                if kind in job_done:
                                    job(kind, n, b, k)

            every_period(pe, half)



NE = 8
NSHARED = 2
EXPERTS = list(range(NE, NE + NSHARED)) + list(range(NE))
NX = len(EXPERTS)
I = 256
IC = I // P
CAP = -(-5 * B * T * 2 // (4 * NE))
PLACES = NE * CAP
CH = 256
CT = CH // P
NCH = CAP // CH
CHUNKS = NE * NCH
CLEAR = PLACES // (B * P)
assert CAP % CH == 0 and NE % 2 == 0 and NCH >= 4
BF16 = mybir.dt.bfloat16
U32 = mybir.dt.uint32
ROUTE_STEPS = 29
SELECTED = 16
TOKENS = B * T
ROW_W, ROW_N = D, D + NE
ROW = D + 2 * NE
PICKS = 3
KEPT = NCH
RING = 4


def moe_phase(nc, x2, slots_x, sums, w_moe, w_gate, index, numbers, out):
    with ExitStack() as ctx:
        def sb(name, shape, dt=F32):
            return ctx.enter_context(nc.sbuf_tensor(name, shape, dt))

        def sem(name):
            return ctx.enter_context(nc.semaphore(name))

        w = sb("we", [P, 4, 2, 3, FC, I], F32R)
        wraw = sb("weraw", [P, 2, 3, FC, I])
        wg = sb("wg", [P, 2, FC, NE], F32R)
        wgraw = sb("wgraw", [P, FC, NE])
        ident = sb("ident2", [P, P])
        before = sb("before", [P, P], BF16)
        ones = sb("ones", [P, P], BF16)
        idx = sb("idx", [P, 2, TT, NE])
        mhalf = sb("mhalf2", [P, TT, 1])
        eps = sb("eps2", [P, TT, 1])
        xin = sb("x2in", [P, 2, TT, ROW])
        tok = sb("tok", [P, TT, 1])
        spare = sb("spare", [P, NCH, CT, 1])
        zrow = sb("zrow", [P, D])
        xf = sb("x2f", [P, 2, 2, FC, T], F32R)
        sg = sb("sg", [P, 2, T])
        h = sb("h", [P, 2, T])
        hf = sb("hf", [P, 2, 2, IC, T], F32R)
        ym = sb("ym", [P, 2, TT, D])
        st6 = sb("st62", [P, 2, TT, 6])
        mv = sb("mv2", [P, 2, TT, 2])
        rstd = sb("rstd2", [P, 2, TT, 1])
        r4 = sb("r4", [P, 8, TT, 1])
        r32 = sb("r32", [P, 9, TT, NE])
        choice = sb("choice", [P, 2, TT, NE])
        prod = sb("prod", [P, 2, TT, NE])
        place2 = sb("place2", [P, 2, TT])
        scat = sb("scat", [P, 2, 2, TT], U32)
        sel = sb("sel", [P, TT + 1, NE], BF16)
        carry = sb("carry", [P, 1, NE])
        xs = sb("xs", [P, 2, CT, ROW])
        cw = sb("cw", [P, KEPT, CT, 1])
        extra = sb("extra", [P, CT, 1])
        dest = sb("dest", [P, KEPT, CT], U32)
        ys = sb("ys", [P, 2, CT, D])
        complete = sb("complete", [P, RING, TT, D])
        yo = sb("yo", [P, 2, TT, D])

        ps_gu = ctx.enter_context(nc.psum_tensor("ps_gu", [P, 4, T], F32))
        ps_dn = ctx.enter_context(nc.psum_tensor("ps_dn", [P, 2, T], F32))
        ps_t = ctx.enter_context(nc.psum_tensor("ps_t", [P, 2, T], F32))
        logits = ps_t[:, 1, 0:TT * NE].rearrange("p (t e) -> p t e", t=TT)
        counts = ps_t[:, 1, P:P + (TT + 1) * NE].rearrange("p (t e) -> p t e", e=NE)

        w_in = [sem("w_in0"), sem("w_in1")]
        wg_in, idx_in = sem("wg_in"), sem("idx_in")
        w_hi, w_lo, consts, ready = sem("we_hi"), sem("we_lo"), sem("consts2"), sem("ready")
        x_in = [sem("x2_in0"), sem("x2_in1")]
        xt_done, xhi_done, xlo_done = sem("xt2_done"), sem("xhi_done"), sem("xlo_done")
        logits_done, shift_done, exp_done, step_done, cnt_done = (
            sem("logits_done"), sem("shift_done"), sem("rexp_done"), sem("step_done"), sem("cnt_done"))
        gu_done, silu_done, h_done, hhi_done, hlo_done = (
            sem("gu_done"), sem("silu_done"), sem("h_done"), sem("hhi_done"), sem("hlo_done"))
        dn_done, acc_done = sem("dn_done"), sem("acc_done")
        sums_out = [sem("sums_out0"), sem("sums_out1")]
        scattered = [sem("scattered0"), sem("scattered1")]
        xs_in = [sem("xs_in0"), sem("xs_in1")]
        ct_done, chi_done, clo_done = sem("ct_done"), sem("chi_done"), sem("clo_done")
        cgu_done, csilu_done, ch_done, chhi_done, chlo_done = (
            sem("cgu_done"), sem("csilu_done"), sem("ch_done"), sem("chhi_done"), sem("chlo_done"))
        cdn_done, cy_done, picked = sem("cdn_done"), sem("cy_done"), sem("picked")
        added = [sem("added0"), sem("added1")]
        complete_in = [sem(f"complete_in{n}") for n in range(RING)]
        stat_done, mv_done, var_done, rstd_done, norm_done = (
            sem("stat2"), sem("mv_done2"), sem("var2"), sem("rstd2d"), sem("norm_done"))
        out_done = [sem("out_done0"), sem("out_done1")]
        GU, HN, DN, ACC = 4 * NSHARED, IC * NSHARED, 2 * NSHARED, TT * NSHARED

        block = ctx.enter_context(nc.Block())

        def after(eng, s, value):
            if not (isinstance(value, int) and value <= 0):
                eng.wait_ge(s, value)

        def by_pairs(eng, count, body, unit=1):
            def pair(k):
                for j in range(2 * unit):
                    body(k, j)

            pair(0)
            if count > 4 * unit:
                with eng.Fori(1, count // (2 * unit) - 1) as k:
                    pair(k)
            pair(count // (2 * unit) - 1)

        def chunk_of(kk, j):
            return 2 * NCH * kk + j

        def is_chunk(g):
            return not isinstance(g, int) or 0 <= g < CHUNKS

        def is_block(i):
            return not isinstance(i, int) or 0 <= i < B

        def split_next(kk, j):
            e, c = 2 * kk + j // NCH, j % NCH
            if c != 2 or (isinstance(e, int) and not 1 <= e < NE - 1):
                return None
            n = e + 1 + NSHARED
            par = (j // NCH + 1) % 2
            return n, par, (kk + 1 if par else kk + 2) + 1

        @block.sync
        def _(sp):
            def load_block(i, q):
                sp.dma_start(xin[:, q, :, 0:D], x2[i, :, :, :]).then_inc(x_in[q], 16)

            def load_weights(n, expert):
                sp.dma_start(wraw[:, n % 2, :, :, :], w_moe[expert]).then_inc(w_in[n % 2], 16)

            sp.dma_start(wgraw[:, :, :], w_gate).then_inc(wg_in, 16)
            load_block(0, 0)
            load_weights(0, EXPERTS[0])
            sp.dma_start(idx[:, :, :, :], index).then_inc(idx_in, 16)
            sp.dma_start(tok[:, :, :], numbers[:, 0:TT, :]).then_inc(idx_in, 16)
            sp.dma_start(spare[:, :, :, :].rearrange("p c t o -> p (c t) o"), numbers[:, TT:, :]).then_inc(idx_in, 16)
            load_block(1, 1)
            load_weights(1, EXPERTS[1])
            for n in range(2, 4):
                sp.wait_ge(w_lo, n - 1)
                load_weights(n, EXPERTS[n])

            token_rows = sums[0:TOKENS, :].rearrange("(i t p) d -> i p t d", t=TT, p=P)

            def tokens(k, q):
                i = 2 * k + q
                wait_alone(sp, acc_done, i * ACC + ACC, idx_in, 48)
                sp.dma_start(token_rows[i], ym[:, q, :, :]).then_inc(sums_out[q], 16)
                if is_block(i + 2):
                    wait_alone(sp, scattered[q], 16 * 2 * TT * (k + 1), idx_in, 48)
                    load_block(i + 2, q)
                if isinstance(k, int) and k == 0:
                    sp.wait_ge(w_lo, 3 + q)
                    load_weights(4 + q, EXPERTS[4 + q])

            by_pairs(sp, B, tokens)

            sp.wait_ge(consts, 9)
            sp.dma_start(sums[TOKENS:, :].rearrange("(p a) d -> p a d", p=P),
                         zrow[:, :].unsqueeze(1).to_broadcast([P, CAP // P, D])).then_inc(idx_in, 16)

            def load_sums(i, n):
                sp.dma_start(complete[:, n, :, :], token_rows[i]).then_inc(complete_in[n], 16)

            def load_chunk(g, p):
                sp.dma_start(xs[:, p, :, :], slots_x[g]).then_inc(xs_in[p], 16)

            for q in range(2):
                sp.wait_ge(sums_out[q], 16 * (B // 2))
                sp.wait_ge(scattered[q], 16 * 2 * TT * (B // 2))
            load_chunk(0, 0)
            load_chunk(1, 1)

            def chunk(kk, j):
                g = chunk_of(kk, j)
                if is_chunk(g + 2):
                    wait_alone(sp, picked, PICKS * (g + 1), idx_in, 48)
                    wait_alone(sp, ct_done, g + 1, idx_in, 48)
                    load_chunk(g + 2, j % 2)
                e = 2 * kk + j // NCH
                if j % NCH == 3 and (not isinstance(e, int) or 1 <= e < NE - 3):
                    wait_alone(sp, w_lo, e + 2 + NSHARED, idx_in, 48)
                    load_weights((j // NCH + 3) % 2, e + 3)

            by_pairs(sp, CHUNKS, chunk, NCH)

            for p in range(2):
                sp.wait_ge(added[p], 16 * CT * (CHUNKS // 2))
            for n in range(RING):
                load_sums(n, n)

            def results(k, n):
                i, q = RING * k + n, n % 2
                wait_alone(sp, norm_done, i * TT + TT, idx_in, 48)
                if is_block(i + RING):
                    load_sums(i + RING, n)
                sp.dma_start(out[i, :, :, :], yo[:, q, :, :]).then_inc(out_done[q], 16)

            by_pairs(sp, B, results, RING // 2)
            for q in range(2):
                sp.wait_ge(out_done[q], 16 * (B // 2))

        @block.gpsimd
        def _(pool):
            nc.gpsimd.memset(ident[:, :], 0.0).then_inc(consts, 1)
            nc.gpsimd.memset(before[:, :], 1.0).then_inc(consts, 1)
            nc.gpsimd.memset(ones[:, :], 1.0).then_inc(consts, 1)
            nc.gpsimd.memset(mhalf[:, :, :], -0.5).then_inc(consts, 1)
            nc.gpsimd.memset(eps[:, :, :], EPS).then_inc(consts, 1)
            nc.gpsimd.memset(zrow[:, :], 0.0).then_inc(consts, 1)
            nc.gpsimd.memset(xin[:, :, :, D:ROW], 0.0).then_inc(consts, 1)
            pool.wait_ge(consts, 7)
            nc.gpsimd.affine_select(out=ident[:, :], in_=ident[:, :], compare_op=ALU.not_equal, fill=1.0,
                                    base=0, pattern=[[-1, P]], channel_multiplier=1).then_inc(consts, 1)
            nc.gpsimd.affine_select(out=before[:, :], in_=before[:, :], compare_op=ALU.is_gt, fill=0.0,
                                    base=0, pattern=[[1, P]], channel_multiplier=-1).then_inc(consts, 1)
            pool.wait_ge(consts, 9)

            rows_x = slots_x.rearrange("g p t d -> (g p t) d")

            def scatter(k, q):
                i = 2 * k + q
                wait_alone(pool, step_done, i * ROUTE_STEPS + ROUTE_STEPS, consts, 9)
                for t in range(TT):
                    for c in range(2):
                        nc.gpsimd.indirect_dma_start(
                            rows_x, bass.IndirectOffsetOnAxis(ap=scat[:, q, c, t:t + 1], axis=0), xin[:, q, t, :],
                            None, bounds_check=PLACES - 1, oob_is_err=False).then_inc(scattered[q], 16)

            by_pairs(pool, B, scatter)

            def add(kk, j):
                g, p, c = chunk_of(kk, j), j % 2, j % NCH
                if c == 0 and is_chunk(g - 1):
                    for par in range(2):
                        wait_alone(pool, added[par], 16 * CT * (NCH * kk + (j + 1 - par) // 2), consts, 9)
                wait_alone(pool, picked, PICKS * (g + 1), consts, 9)
                wait_alone(pool, cy_done, CT * (g + 1), consts, 9)
                for t in range(CT):
                    nc.gpsimd.indirect_dma_start(
                        sums, bass.IndirectOffsetOnAxis(ap=dest[:, c, t:t + 1], axis=0), ys[:, p, t, :],
                        None, bounds_check=TOKENS + CAP - 1, oob_is_err=True, compute_op=ALU.add) \
                        .then_inc(added[p], 16)

            for q in range(2):
                pool.wait_ge(sums_out[q], 16 * (B // 2))
            pool.wait_ge(idx_in, 64)
            by_pairs(pool, CHUNKS, add, NCH)

            def norm(k, n):
                i, q = RING * k + n, n % 2
                pool.wait_ge(mv_done, i * TT + TT)
                nc.gpsimd.tensor_tensor(rstd[:, q, :, :], mv[:, q, :, 1:2], eps[:, :, :], ALU.add).then_inc(var_done, 1)
                pool.wait_ge(var_done, i + 1)
                nc.gpsimd.tensor_tensor(rstd[:, q, :, :], rstd[:, q, :, :], mhalf[:, :, :], ALU.pow) \
                    .then_inc(rstd_done, 1)

            by_pairs(pool, B, norm, RING // 2)

        @block.scalar
        def _(act):
            act.wait_ge(wg_in, 16)
            nc.scalar.activation(wg[:, HI, :, :], wgraw[:, :, :], ACT.Copy).then_inc(w_hi, 1)

            def split_hi(at, par, loaded):
                act.wait_ge(w_in[par], 16 * loaded)
                nc.scalar.activation(w[:, at, HI, :, :, :].rearrange("p a f i -> p (a f i)"),
                                     wraw[:, par, :, :, :].rearrange("p a f i -> p (a f i)"),
                                     ACT.Copy).then_inc(w_hi, 1)

            def x_hi(i, q, f):
                act.wait_ge(xt_done, i * FC + f + 1)
                if f == 0 and is_block(i - 2):
                    act.wait_ge(gu_done, (i - 1) * GU)
                nc.scalar.activation(xf[:, q, HI, f, :], ps_t[:, 0, :], ACT.Copy).then_inc(xhi_done, 1)

            for f in range(FC):
                x_hi(0, 0, f)
            for n in range(NSHARED):
                split_hi(n, n, 1)

            def tokens(k, q):
                i = 2 * k + q
                act.wait_ge(shift_done, i + 1)
                nc.scalar.activation(r32[:, 1, :, :], r32[:, 0, :, :], ACT.Exp).then_inc(exp_done, 1)
                for n in range(NSHARED):
                    for c in range(IC):
                        act.wait_ge(gu_done, i * GU + 4 * n + 2 * c + 1)
                        after(act, h_done, i * HN + IC * (n - 1) + c + 1)
                        nc.scalar.activation(sg[:, c, :], ps_gu[:, 2 * c, :], ACT.Silu).then_inc(silu_done, 1)
                    for c in range(IC):
                        act.wait_ge(h_done, i * HN + IC * n + c + 1)
                        if c == 0:
                            after(act, dn_done, i * DN + 2 * (n - 1))
                        nc.scalar.activation(hf[:, n % 2, HI, c, :], h[:, c, :], ACT.Copy).then_inc(hhi_done, 1)
                if is_block(i + 1):
                    for f in range(FC):
                        x_hi(i + 1, 1 - q, f)
                if isinstance(k, int) and k == 0:
                    split_hi(2 + q, q, 2)

            by_pairs(act, B, tokens)

            def chunk_hi(g, p):
                act.wait_ge(ct_done, g + 1)
                if is_chunk(g - 2):
                    act.wait_ge(cgu_done, 2 * (g - 1))
                else:
                    act.wait_ge(gu_done, B * GU)
                nc.scalar.activation(xf[:, p, HI, :, 0:CH], ps_t[:, p, :].rearrange("p (f t) -> p f t", f=FC),
                                     ACT.Copy).then_inc(chi_done, 1)

            def weigh(g, p, c, before):
                act.wait_ge(cdn_done, g + 1)
                act.wait_ge(picked, PICKS * (g + 1))
                if before is not None:
                    act.wait_ge(added[p], 16 * CT * before)
                for t in range(CT):
                    nc.scalar.activation(ys[:, p, t, :], ps_dn[:, p, D * t:D * t + D], ACT.Copy,
                                         scale=cw[:, c, t, :]).then_inc(cy_done, 1)

            def chunk(kk, j):
                g, p = chunk_of(kk, j), j % 2
                if is_chunk(g - 2):
                    weigh(g - 2, p, (j - 2) % NCH, NCH * kk + j // 2 - 1 if is_chunk(g - 4) else None)
                if is_chunk(g + 1):
                    chunk_hi(g + 1, 1 - p)
                act.wait_ge(cgu_done, 2 * g + 1)
                if is_chunk(g - 2):
                    act.wait_ge(ch_done, g - 1)
                else:
                    act.wait_ge(h_done, B * HN)
                nc.scalar.activation(sg[:, p, :], ps_gu[:, 2 * p, :], ACT.Silu).then_inc(csilu_done, 1)
                act.wait_ge(ch_done, g + 1)
                if is_chunk(g - 2):
                    act.wait_ge(cdn_done, g - 1)
                else:
                    act.wait_ge(dn_done, B * DN)
                nc.scalar.activation(hf[:, p, HI, :, 0:CH], h[:, p, :].rearrange("p (c t) -> p c t", c=IC),
                                     ACT.Copy).then_inc(chhi_done, 1)
                nxt = split_next(kk, j)
                if nxt:
                    n, par, loaded = nxt
                    act.wait_ge(cdn_done, g - 2)
                    split_hi(2 + par, par, loaded)

            chunk_hi(0, 0)
            by_pairs(act, CHUNKS, chunk, NCH)
            for g in (CHUNKS - 2, CHUNKS - 1):
                weigh(g, g % 2, g % NCH, g // 2)

        @block.vector
        def _(dve):
            nc.vector.memset(sel[:, TT, :], 0.0)
            nc.vector.memset(carry[:, :, :], 0.0).then_inc(ready, 1)
            dve.wait_ge(w_hi, 1)
            nc.vector.tensor_tensor(wg[:, LO, :, :], wgraw[:, :, :], wg[:, HI, :, :].bitcast(F32), ALU.subtract) \
                .then_inc(ready, 1)

            def split_lo(at, par, n):
                dve.wait_ge(w_hi, n + 2)
                nc.vector.tensor_tensor(w[:, at, LO, :, :, :].rearrange("p a f i -> p (a f i)"),
                                        wraw[:, par, :, :, :].rearrange("p a f i -> p (a f i)"),
                                        w[:, at, HI, :, :, :].rearrange("p a f i -> p (a f i)").bitcast(F32),
                                        ALU.subtract).then_inc(w_lo, 1)

            def x_lo(i, q, f):
                dve.wait_ge(xhi_done, i * FC + f + 1)
                nc.vector.tensor_tensor(xf[:, q, LO, f, :], ps_t[:, 0, :], xf[:, q, HI, f, :].bitcast(F32),
                                        ALU.subtract).then_inc(xlo_done, 1)

            for f in range(FC):
                x_lo(0, 0, f)
            for n in range(NSHARED):
                split_lo(n, n, n)
            dve.wait_ge(ready, 2)
            dve.wait_ge(idx_in, 48)

            v = nc.vector
            mx, total, inv, top1, j1, top2, j2, den = (r4[:, k, :, :] for k in range(8))
            shifted, e, s, eq, cand, rest, pos, past, weight = (r32[:, k, :, :] for k in range(9))
            one, two = (choice[:, c, :, :] for c in range(2))
            number, first_place = (idx[:, c, :, :] for c in range(2))

            def wide(a):
                return a.to_broadcast([P, TT, NE])

            def make_step(i, done):
                def step(ins):
                    done[0] += 1
                    ins.then_inc(step_done, 1)
                    dve.wait_ge(step_done, i * ROUTE_STEPS + done[0])
                return step

            def choose(i):
                done = [0]
                step = make_step(i, done)
                dve.wait_ge(logits_done, i + 1)
                step(v.tensor_reduce(mx, logits, axis=AX.X, op=ALU.max))
                v.tensor_tensor(shifted, logits, wide(mx), ALU.subtract).then_inc(shift_done, 1)
                dve.wait_ge(exp_done, i + 1)
                step(v.tensor_reduce(total, e, axis=AX.X, op=ALU.add))
                step(v.reciprocal(inv, total))
                step(v.tensor_tensor(s, e, wide(inv), ALU.mult))
                step(v.tensor_reduce(top1, s, axis=AX.X, op=ALU.max))
                step(v.tensor_tensor(eq, s, wide(top1), ALU.is_equal))
                step(v.tensor_tensor(cand, eq, number, ALU.mult))
                step(v.tensor_reduce(j1, cand, axis=AX.X, op=ALU.min))
                step(v.tensor_tensor(one, number, wide(j1), ALU.is_equal))
                step(v.scalar_tensor_tensor(out=rest, in0=one, scalar=-2.0, in1=s, op0=ALU.mult, op1=ALU.add))
                step(v.tensor_reduce(top2, rest, axis=AX.X, op=ALU.max))
                step(v.tensor_tensor(eq, rest, wide(top2), ALU.is_equal))
                step(v.tensor_tensor(cand, eq, number, ALU.mult))
                step(v.tensor_reduce(j2, cand, axis=AX.X, op=ALU.min))
                step(v.tensor_tensor(two, number, wide(j2), ALU.is_equal))
                step(v.tensor_tensor(sel[:, 0:TT, :], one, two, ALU.add))
                assert done[0] == SELECTED, done
                step(v.scalar_tensor_tensor(out=den, in0=top1, scalar=1e-20, in1=top2, op0=ALU.add, op1=ALU.add))
                step(v.reciprocal(inv, den))
                step(v.tensor_tensor(weight, s, wide(inv), ALU.mult))
                return done

            def place(i, k, q, done):
                step = make_step(i, done)
                dve.wait_ge(cnt_done, i + 1)
                step(v.tensor_tensor(pos, counts[:, 0:TT, :], carry[:, :, :].to_broadcast([P, TT, NE]), ALU.add))
                v.tensor_tensor(carry[:, :, :], carry[:, :, :], counts[:, TT:TT + 1, :], ALU.add).then_inc(ready, 1)
                step(v.tensor_scalar(past, pos, float(CAP), float(PLACES), ALU.is_ge, ALU.mult))
                step(v.tensor_tensor(pos, pos, first_place, ALU.add))
                step(v.tensor_tensor(pos, pos, past, ALU.add))
                step(v.tensor_tensor(prod[:, :, :, :].rearrange("p c t e -> p c (t e)"),
                                     choice[:, :, :, :].rearrange("p c t e -> p c (t e)"),
                                     pos.rearrange("p t e -> p (t e)").unsqueeze(1).to_broadcast([P, 2, TT * NE]),
                                     ALU.mult))
                step(v.tensor_reduce(place2[:, :, :].rearrange("p c t -> p (c t)"),
                                     prod[:, :, :, :].rearrange("p c t e -> p (c t) e"), axis=AX.X, op=ALU.add))
                if is_block(i - 2):
                    dve.wait_ge(scattered[q], 16 * 2 * TT * k)
                step(v.tensor_copy(scat[:, q, :, :], place2[:, :, :]))
                step(v.tensor_copy(xin[:, q, :, ROW_W:ROW_W + NE], weight))
                step(v.tensor_copy(xin[:, q, :, ROW_N:ROW_N + 1], tok[:, :, :]))
                step(v.tensor_scalar(tok[:, :, :], tok[:, :, :], float(T), 0.0, ALU.add, ALU.add))
                assert done[0] == ROUTE_STEPS, done

            def product(i, n):
                for c in range(IC):
                    dve.wait_ge(silu_done, i * HN + IC * n + c + 1)
                    dve.wait_ge(gu_done, i * GU + 4 * n + 2 * c + 2)
                    after(dve, hlo_done, i * HN + IC * (n - 1) + c + 1)
                    nc.vector.tensor_tensor(h[:, c, :], ps_gu[:, 2 * c + 1, :], sg[:, c, :], ALU.mult) \
                        .then_inc(h_done, 1)
                for c in range(IC):
                    dve.wait_ge(hhi_done, i * HN + IC * n + c + 1)
                    nc.vector.tensor_tensor(hf[:, n % 2, LO, c, :], h[:, c, :],
                                            hf[:, n % 2, HI, c, :].bitcast(F32), ALU.subtract).then_inc(hlo_done, 1)

            def accumulate(i, q, n):
                for t in range(TT):
                    dve.wait_ge(dn_done, i * DN + 2 * n + t // 2 + 1)
                    if n:
                        dve.wait_ge(acc_done, i * ACC + TT * (n - 1) + t + 1)
                    y = ym[:, q, t, :]
                    nc.vector.tensor_tensor(y, ps_dn[:, t // 2, D * (t % 2):D * (t % 2) + D],
                                            y if n else xin[:, q, t, 0:D], ALU.add).then_inc(acc_done, 1)

            def tokens(k, q):
                i = 2 * k + q
                done = choose(i)
                product(i, 0)
                place(i, k, q, done)
                product(i, 1)
                if is_block(i + 1):
                    x_lo(i + 1, 1 - q, 0)
                if is_block(i - 2):
                    dve.wait_ge(sums_out[q], 16 * k)
                accumulate(i, q, 0)
                if is_block(i + 1):
                    x_lo(i + 1, 1 - q, 1)
                accumulate(i, q, 1)
                if isinstance(k, int) and k == 0:
                    split_lo(2 + q, q, 2 + q)

            by_pairs(dve, B, tokens)

            def pick(g, p, c, e, rounds, before):
                if before is not None:
                    dve.wait_ge(added[1 - p], 16 * CT * before)
                dve.wait_ge(xs_in[p], 16 * rounds)
                if is_chunk(g - 1):
                    dve.wait_ge(picked, PICKS * g)
                number_of = xs[:, p, :, ROW_N:ROW_N + 1]
                nc.vector.scalar_tensor_tensor(out=extra[:, :, :], in0=number_of, scalar=0.0, in1=spare[:, c, :, :],
                                               op0=ALU.is_equal, op1=ALU.mult).then_inc(picked, 1)
                nc.vector.tensor_copy(cw[:, c, :, :], xs[:, p, :, bass.ds(ROW_W + e, 1)]).then_inc(picked, 1)
                dve.wait_ge(picked, PICKS * g + 1)
                nc.vector.scalar_tensor_tensor(out=dest[:, c, :].unsqueeze(2), in0=number_of, scalar=float(TOKENS),
                                               in1=extra[:, :, :], op0=ALU.add, op1=ALU.add).then_inc(picked, 1)

            def chunk_lo(g, p):
                dve.wait_ge(chi_done, g + 1)
                nc.vector.tensor_tensor(xf[:, p, LO, :, 0:CH], ps_t[:, p, :].rearrange("p (f t) -> p f t", f=FC),
                                        xf[:, p, HI, :, 0:CH].bitcast(F32), ALU.subtract).then_inc(clo_done, 1)

            def chunk(kk, j):
                g, p = chunk_of(kk, j), j % 2
                if is_chunk(g + 1):
                    before = NCH * kk + (j + 1 - NCH) // 2 + 1 if is_chunk(g + 1 - NCH) else None
                    pick(g + 1, 1 - p, (j + 1) % NCH, 2 * kk + (j + 1) // NCH, NCH * kk + (j + 1) // 2 + 1, before)
                    chunk_lo(g + 1, 1 - p)
                dve.wait_ge(csilu_done, g + 1)
                dve.wait_ge(cgu_done, 2 * g + 2)
                if is_chunk(g - 2):
                    dve.wait_ge(chlo_done, g - 1)
                else:
                    dve.wait_ge(hlo_done, B * HN)
                nc.vector.tensor_tensor(h[:, p, :], ps_gu[:, 2 * p + 1, :], sg[:, p, :], ALU.mult).then_inc(ch_done, 1)
                dve.wait_ge(chhi_done, g + 1)
                nc.vector.tensor_tensor(hf[:, p, LO, :, 0:CH], h[:, p, :].rearrange("p (c t) -> p c t", c=IC),
                                        hf[:, p, HI, :, 0:CH].bitcast(F32), ALU.subtract).then_inc(chlo_done, 1)
                nxt = split_next(kk, j)
                if nxt:
                    n, par, loaded = nxt
                    split_lo(2 + par, par, n)

            pick(0, 0, 0, 0, 1, None)
            chunk_lo(0, 0)
            by_pairs(dve, CHUNKS, chunk, NCH)

            def moments(i, k, n):
                q = n % 2
                dve.wait_ge(complete_in[n], 16 * (k + 1))
                for t in range(TT):
                    nc.vector.bn_stats(st6[:, q, t, :], complete[:, n, t, :]).then_inc(stat_done, 1)
                for t in range(TT):
                    wait_alone(dve, stat_done, i * TT + t + 1, idx_in, 48)
                    nc.vector.bn_aggr(mv[:, q, t, :], st6[:, q, t, :]).then_inc(mv_done, 1)

            def norm(k, n):
                i, q = RING * k + n, n % 2
                if is_block(i - 1):
                    dve.wait_ge(norm_done, i * TT)
                if is_block(i + 1):
                    moments(i + 1, k + (n + 1) // RING, (n + 1) % RING)
                dve.wait_ge(rstd_done, i + 1)
                if is_block(i - 2):
                    dve.wait_ge(out_done[q], 16 * (RING // 2 * k + n // 2))
                for t in range(TT):
                    nc.vector.tensor_scalar(yo[:, q, t, :], complete[:, n, t, :], mv[:, q, t, 0:1], rstd[:, q, t, :],
                                            ALU.subtract, ALU.mult).then_inc(norm_done, 1)

            moments(0, 0, 0)
            by_pairs(dve, B, norm, RING // 2)

        @block.tensor
        def _(pe):
            pe.wait_ge(consts, 9)

            def products(o, pairs):
                parts = ((HI, HI), (HI, LO), (LO, HI))
                for n, (l, r) in enumerate(pairs):
                    for k, (a, b) in enumerate(parts):
                        ins = nc.tensor.matmul(o, l(a), r(b), start=(n == 0 and k == 0),
                                               stop=(n == len(pairs) - 1 and k == len(parts) - 1))
                return ins

            def turn(i, k, q, f):
                if f == 0:
                    pe.wait_ge(x_in[q], 16 * (k + 1))
                after(pe, xlo_done, i * FC + f)
                for t in range(TT):
                    ins = nc.tensor.transpose(ps_t[:, 0, P * t:P * t + P], xin[:, q, t, P * f:P * f + P], ident[:, :])
                ins.then_inc(xt_done, 1)

            def gate_up(i, q, n):
                for c in range(IC):
                    for kind in range(2):
                        after(pe, h_done if kind else silu_done, i * HN + IC * (n - 1) + c + 1)
                        products(ps_gu[:, 2 * c + kind, :],
                                 [(lambda a, f=f: w[:, n, a, kind, f, P * c:P * c + P], lambda b, f=f: xf[:, q, b, f, :])
                                  for f in range(FC)]).then_inc(gu_done, 1)

            def down(i, n):
                pe.wait_ge(hlo_done, i * HN + IC * n + IC)
                for pair in range(2):
                    after(pe, acc_done, i * ACC + TT * (n - 1) + 2 * pair + 2)
                    for half in range(2):
                        t = P * (2 * pair + half)
                        ins = products(ps_dn[:, pair, D * half:D * half + D],
                                       [(lambda a, c=c: hf[:, n % 2, a, c, t:t + P], lambda b, c=c: w[:, n, b, 2, c, :])
                                        for c in range(IC)])
                    ins.then_inc(dn_done, 1)

            def count(i):
                pe.wait_ge(step_done, i * ROUTE_STEPS + SELECTED)
                nc.tensor.matmul(counts[:, :, :], before[:, :], sel[:, :, :], start=True, stop=False)
                for d in range(1, TT + 1):
                    ins = nc.tensor.matmul(counts[:, d:, :], ones[:, :], sel[:, 0:TT + 1 - d, :], start=False,
                                           stop=(d == TT))
                ins.then_inc(cnt_done, 1)

            for f in range(FC):
                turn(0, 0, 0, f)
            pe.wait_ge(ready, 2)

            def tokens(k, q):
                i = 2 * k + q
                pe.wait_ge(xlo_done, i * FC + FC)
                after(pe, ready, i + 2)
                for t in range(TT):
                    ins = products(logits[:, t, :],
                                   [(lambda a, f=f, t=t: xf[:, q, a, f, P * t:P * t + P], lambda b, f=f: wg[:, b, f, :])
                                    for f in range(FC)])
                ins.then_inc(logits_done, 1)
                if isinstance(k, int) and i == 0:
                    pe.wait_ge(w_lo, 1)
                gate_up(i, q, 0)
                count(i)
                if isinstance(k, int) and i == 0:
                    pe.wait_ge(w_lo, 2)
                gate_up(i, q, 1)
                if is_block(i + 1):
                    turn(i + 1, k + q, 1 - q, 0)
                down(i, 0)
                if is_block(i + 1):
                    turn(i + 1, k + q, 1 - q, 1)
                down(i, 1)

            by_pairs(pe, B, tokens)

            def chunk_turn(g, p, rounds):
                pe.wait_ge(xs_in[p], 16 * rounds)
                if is_chunk(g - 2):
                    pe.wait_ge(clo_done, g - 1)
                else:
                    pe.wait_ge(xlo_done, B * FC)
                    pe.wait_ge(ready, B + 2)
                for f in range(FC):
                    for t in range(CT):
                        at = CH * f + P * t
                        ins = nc.tensor.transpose(ps_t[:, p, at:at + P], xs[:, p, t, P * f:P * f + P], ident[:, :])
                ins.then_inc(ct_done, 1)

            def chunk_down(g, p, at):
                pe.wait_ge(chlo_done, g + 1)
                if is_chunk(g - 2):
                    pe.wait_ge(cy_done, CT * (g - 1))
                else:
                    pe.wait_ge(acc_done, B * ACC)
                for t in range(CT):
                    ins = products(ps_dn[:, p, D * t:D * t + D],
                                   [(lambda a, c=c: hf[:, p, a, c, P * t:P * t + P], lambda b, c=c: w[:, at, b, 2, c, :])
                                    for c in range(IC)])
                ins.then_inc(cdn_done, 1)

            def chunk(kk, j):
                g, p, at = chunk_of(kk, j), j % 2, 2 + j // NCH
                if is_chunk(g + 1):
                    chunk_turn(g + 1, 1 - p, NCH * kk + (j + 1) // 2 + 1)
                pe.wait_ge(clo_done, g + 1)
                if j % NCH == 0:
                    pe.wait_ge(w_lo, 2 * kk + j // NCH + NSHARED + 1)
                for kind in range(2):
                    if is_chunk(g - 2):
                        pe.wait_ge(ch_done if kind else csilu_done, g - 1)
                    else:
                        pe.wait_ge(h_done, B * HN)
                    for c in range(IC):
                        ins = products(ps_gu[:, 2 * p + kind, CH * c:CH * c + CH],
                                       [(lambda a, f=f: w[:, at, a, kind, f, P * c:P * c + P],
                                         lambda b, f=f: xf[:, p, b, f, 0:CH]) for f in range(FC)])
                    ins.then_inc(cgu_done, 1)
                if is_chunk(g - 1):
                    chunk_down(g - 1, 1 - p, 2 + (j - 1) % (2 * NCH) // NCH)

            chunk_turn(0, 0, 1)
            by_pairs(pe, CHUNKS, chunk, NCH)
            chunk_down(CHUNKS - 1, (CHUNKS - 1) % 2, 3)


SCRATCH = {"x2": [B, P, TT, D], "hbm_self": [FC, P, SLOTS, T], "hbm_ck": [P, FC, 2, T], "hbm_cq": [P, FC, 2, T],
           "slots_x": [CHUNKS, P, CT, ROW], "sums": [TOKENS + CAP, D]}


def program(nc, ap, scratch, out):
    attention_phase(nc, ap["x"], ap["xT"], ap["cT"], ap["w_att"], ap["tables"], ap["b_cols"], ap["bo_rows"],
                    scratch["x2"], scratch["hbm_self"], scratch["hbm_ck"], scratch["hbm_cq"], scratch["slots_x"])
    moe_phase(nc, scratch["x2"], scratch["slots_x"], scratch["sums"], ap["w_moe"], ap["w_gate"], ap["index"],
              ap["numbers"], out)


def layout(inp):
    f = {k: np.asarray(v) for k, v in inp.items()}

    def by_token(a):
        return np.ascontiguousarray(a.reshape(a.shape[0], TT, P, D).transpose(0, 2, 1, 3))

    def by_feature(a):
        return np.ascontiguousarray(a.transpose(0, 2, 1).reshape(a.shape[0], FC, P, T).transpose(0, 2, 1, 3))

    def col(b):
        return b.reshape(FC, P).transpose(1, 0)

    w_all = np.concatenate([f["L0_attn_Wqkv"], f["L0_attn_Wout"]]
                           + [f[f"L0_xattn_w_{n}"].T for n in ("q", "k", "v", "o")], axis=1)
    inv_freq = (1.0 / np.float32(10000.0) ** (np.arange(0, HD, 2, dtype=np.float32) / np.float32(HD))).astype(np.float32)
    angle = np.arange(T, dtype=np.float32)[None, :] * inv_freq[np.arange(P) % (HD // 2)][:, None]
    sign = np.where(np.arange(P) % 2 == 0, -1.0, 1.0).astype(np.float32)[:, None]
    def shared(a):
        return a.reshape(NSHARED, I, D)

    gate = np.concatenate([f["L0_ffn_we_gate"], shared(f["L0_ffn_ws_gate"])]).transpose(0, 2, 1)
    up = np.concatenate([f["L0_ffn_we_up"], shared(f["L0_ffn_ws_up"])]).transpose(0, 2, 1)
    down = np.concatenate([f["L0_ffn_we_down"].transpose(0, 2, 1), shared(f["L0_ffn_ws_down"].T)])
    w_moe = np.ascontiguousarray(np.stack([gate, up, down], axis=1).reshape(NX, 3, FC, P, I).transpose(0, 3, 1, 2, 4))
    return {
        "x": by_token(f["x"]), "xT": by_feature(f["x"]), "cT": by_feature(f["ctx_1024"]),
        "w_att": np.ascontiguousarray(w_all.reshape(FC, P, NW).transpose(1, 0, 2)),
        "tables": np.stack([np.cos(angle), np.sin(angle) * sign], axis=1).astype(np.float32),
        "b_cols": np.ascontiguousarray(np.stack([col(f[f"L0_xattn_b_{n}"]) for n in ("q", "k", "v")], axis=1)),
        "w_moe": w_moe, "w_gate": np.ascontiguousarray(f["L0_ffn_gate_w"].T.reshape(FC, P, NE).transpose(1, 0, 2)),
        "index": np.ascontiguousarray(np.broadcast_to(
            np.stack([np.arange(NE, dtype=np.float32) - NE, np.arange(NE, dtype=np.float32) * CAP])[:, None, :],
            (P, 2, TT, NE))),
        "numbers": np.concatenate([np.arange(TT) * P - TOKENS, np.arange(CAP // P) * P])
        .astype(np.float32)[None, :, None] + np.arange(P, dtype=np.float32)[:, None, None],
        "bo_rows": np.ascontiguousarray(np.broadcast_to(f["L0_xattn_b_o"], (P, D))),
    }

def kernel(**inputs):
    import concourse.bacc as bacc
    from concourse.bass_utils import run_bass_kernel_spmd as run

    nc = bacc.Bacc("TRN2", target_bir_lowering=False, num_devices=1)
    arrays = layout(inputs)
    ap = {n: nc.dram_tensor(n, a.shape, F32, kind="ExternalInput").ap() for n, a in arrays.items()}
    out = nc.dram_tensor("out", [B, P, TT, D], F32, kind="ExternalOutput").ap()
    scratch = {n: nc.dram_tensor(n, s, F32, kind="Internal").ap() for n, s in SCRATCH.items()}
    program(nc, ap, scratch, out)
    r = run(nc, [arrays], core_ids=[0])
    got = np.asarray(r.results[0]["out"])
    return np.ascontiguousarray(got.transpose(0, 2, 1, 3).reshape(B, T, D))
```
